# Optimizing a Trainium2 kernel written in Bass

```python
import numpy as np
import jax
import jax.numpy as jnp

def _softmax(x, axis=-1):
    return jax.nn.softmax(x, axis=axis)

def _gelu(x):
    return jax.nn.gelu(x, approximate=True)

def _silu(x):
    return jax.nn.silu(x)

def _sigmoid(x):
    return jax.nn.sigmoid(x)

def _layernorm(x, axis=-1, eps=1e-05):
    m = jnp.mean(x, axis=axis, keepdims=True)
    v = jnp.var(x, axis=axis, keepdims=True)
    return (x - m) / jnp.sqrt(v + eps)

def _scatter_add(tgt, idx, src, axis=0):
    return tgt.at[idx].add(src)

def _segment_sum(src, seg, n):
    return jax.ops.segment_sum(src, seg, n)
kernel_name = 'mk_flamingo_gated_d4_seqx_r8_73512c'

def setup_inputs(seed: int=0):
    np.random.seed(seed)
    _w = jnp.asarray

    def _rec_inputs():
        import jax
        import jax.numpy as jnp
        _rk = jax.random.key(seed)
        x = -0.0002928 + 1 * jax.random.normal(jax.random.fold_in(_rk, 1), (64, 64, 128), jnp.float32)
        _lenS = 64 - jax.random.randint(jax.random.fold_in(_rk, 7), (64,), 0, max(1, 64 // 4) + 1, jnp.int32)
        _lenS2 = 64 - jax.random.randint(jax.random.fold_in(_rk, 8), (64,), 0, max(1, 64 // 4) + 1, jnp.int32)
        _ctx_1024P = jax.random.normal(jax.random.fold_in(_rk, 11), (64, 16, 128), jnp.float32)
        _ctx_1024c = jax.random.dirichlet(jax.random.fold_in(_rk, 511), 0.3 * jnp.ones((16,), jnp.float32), (64, 64))
        _ctx_1024t = jnp.einsum('bsk,bkd->bsd', _ctx_1024c, _ctx_1024P)
        _ctx_1024t = _ctx_1024t * jax.lax.rsqrt(jnp.mean(jnp.square(_ctx_1024t)) + 1e-12) * 0.953939
        ctx_1024 = -1.39393e-06 + 0.999914 * (_ctx_1024t + 0.3 * jax.random.normal(jax.random.fold_in(_rk, 611), (64, 64, 128), jnp.float32))
        _validS = jnp.arange(64)[None, :] < _lenS[:, None]
        _validS2 = jnp.arange(64)[None, :] < _lenS2[:, None]
        _causal = jnp.tril(jnp.ones((64, 64), dtype=bool))
        mask_Bx1xSxS2_ik1 = jnp.where(jnp.broadcast_to(_validS2[:, None, None, :], (64, 1, 64, 64)), 1, 0).astype(jnp.int32)
        _g = jax.random.normal(jax.random.fold_in(_rk, 9001), (2, 4), jnp.float32)
        _g = jnp.sign(_g) * jnp.maximum(jnp.abs(_g), 1.0) + (_g == 0) * 1.0
        g_xattn = _g[0]
        g_ffn = _g[1]
        return (x, ctx_1024, _lenS2, mask_Bx1xSxS2_ik1, g_xattn, g_ffn)
    x, ctx_1024, _lenS2, mask_Bx1xSxS2_ik1, g_xattn, g_ffn = _rec_inputs()

    def _L0_xattn_setup():
        import jax, jax.numpy as jnp
        import numpy as np
        B, S, H, NH = (2, 256, 128, 4)
        DH = H // NH
        EPS_BACKEND = 1e-06
        EPS_LN = 1e-06

        def _mlstm_parallel_stabilized(q, k, v, igate_preact, fgate_preact):
            b, nh, s, dh = q.shape
            log_fg = jax.nn.log_sigmoid(fgate_preact)
            cs = jnp.concatenate([jnp.zeros((b, nh, 1), q.dtype), jnp.cumsum(log_fg[..., 0], axis=2)], axis=2)
            fg_matrix = cs[:, :, :, None] - cs[:, :, None, :]
            fg_matrix = fg_matrix[:, :, 1:, 1:]
            causal = jnp.tril(jnp.ones((s, s), dtype=bool))
            log_fg_matrix = jnp.where(causal, fg_matrix, -jnp.inf)
            log_D = log_fg_matrix + jnp.swapaxes(igate_preact, -2, -1)
            max_log_D = jnp.max(log_D, axis=-1, keepdims=True)
            D = jnp.exp(log_D - max_log_D)
            qk = jnp.einsum('bhsd,bhtd->bhst', q, k) / jnp.sqrt(jnp.asarray(dh, q.dtype))
            C = qk * D
            normalizer = jnp.maximum(jnp.abs(jnp.sum(C, axis=-1, keepdims=True)), jnp.exp(-max_log_D))
            C_norm = C / (normalizer + EPS_BACKEND)
            return jnp.einsum('bhst,bhtd->bhsd', C_norm, v)

        def _multihead_layernorm(x, scale):
            mean = jnp.mean(x, axis=-1, keepdims=True)
            var = jnp.var(x, axis=-1, keepdims=True)
            xn = (x - mean) * jax.lax.rsqrt(var + EPS_LN)
            return xn * scale.reshape(NH, 1, DH)
        key = jax.random.key(seed)
        kq, kk, kv, kib = jax.random.split(key, 4)
        q = jax.random.normal(kq, (B, S, H), dtype=jnp.float32)
        k = jax.random.normal(kk, (B, S, H), dtype=jnp.float32)
        v = jax.random.normal(kv, (B, S, H), dtype=jnp.float32)
        igate_kernel = jnp.zeros((3 * H, NH), dtype=jnp.float32)
        igate_bias = 0.1 * jax.random.normal(kib, (NH,), dtype=jnp.float32)
        fgate_kernel = jnp.zeros((3 * H, NH), dtype=jnp.float32)
        fgate_bias = jnp.linspace(3.0, 6.0, NH, dtype=jnp.float32)
        outnorm_scale = jnp.ones((H,), dtype=jnp.float32)
        return {'q': q, 'k': k, 'v': v, 'igate_kernel': igate_kernel, 'igate_bias': igate_bias, 'fgate_kernel': fgate_kernel, 'fgate_bias': fgate_bias, 'outnorm_scale': outnorm_scale}
    _L0_xattn_all = _L0_xattn_setup()
    _L0_xattn_in = {k: v for k, v in _L0_xattn_all.items() if k in ('igate_kernel', 'igate_bias', 'fgate_kernel', 'fgate_bias', 'outnorm_scale')}
    del _L0_xattn_all

    def _L0_ffn_setup():
        import jax, jax.numpy as jnp
        import numpy as np
        B, N, DIM = (2, 256, 128)
        HEADS, DIM_HEAD, EXPERTS = (8, 64, 8)
        SCALE = DIM_HEAD ** (-0.5)
        key = jax.random.key(seed)
        ks = jax.random.split(key, 6)
        dim_inner = HEADS * DIM_HEAD
        return {'x': jax.random.normal(ks[0], (B, N, DIM), jnp.float32), 'w_q': jax.random.normal(ks[1], (DIM, dim_inner), jnp.float32) * 0.02, 'w_k': jax.random.normal(ks[2], (DIM, dim_inner), jnp.float32) * 0.02, 'w_gate': jax.random.normal(ks[3], (DIM, HEADS * EXPERTS), jnp.float32) * 0.02, 'value_experts': jax.random.normal(ks[4], (EXPERTS, HEADS, DIM, DIM_HEAD), jnp.float32) * 0.02, 'output_experts': jax.random.normal(ks[5], (EXPERTS, HEADS, DIM_HEAD, DIM), jnp.float32) * 0.02}
    _L0_ffn_all = _L0_ffn_setup()
    _L0_ffn_in = {k: v for k, v in _L0_ffn_all.items() if k in ('w_q', 'w_k', 'w_gate', 'value_experts', 'output_experts')}
    del _L0_ffn_all

    def _L1_xattn_setup():
        import jax, jax.numpy as jnp
        import numpy as np
        DIM, HEADS, HEAD_DIM = (128, 16, 64)
        B, L, S = (4, 256, 256)
        EPS = 1e-05
        NEG_INF = -1000000000.0

        def rms_norm(x, w):
            var = jnp.mean(jnp.square(x), axis=-1, keepdims=True)
            return x * jax.lax.rsqrt(var + EPS) * w
        key = jax.random.key(seed)
        ks = jax.random.split(key, 9)
        hd = HEADS * HEAD_DIM
        scale = 1.0 / np.sqrt(DIM)
        return {'q': jax.random.normal(ks[0], (B, L, DIM), dtype=jnp.float32), 'kv': jax.random.normal(ks[1], (B, S, DIM), dtype=jnp.float32), 'x_seqlens': jax.random.randint(ks[2], (B,), 1, S + 1, dtype=jnp.int32), 'Wq': jax.random.normal(ks[3], (DIM, hd), dtype=jnp.float32) * scale, 'Wk': jax.random.normal(ks[4], (DIM, hd), dtype=jnp.float32) * scale, 'Wv': jax.random.normal(ks[5], (DIM, hd), dtype=jnp.float32) * scale, 'Wo': jax.random.normal(ks[6], (hd, DIM), dtype=jnp.float32) * (1.0 / np.sqrt(hd)), 'q_norm_w': jnp.ones((HEAD_DIM,), dtype=jnp.float32), 'k_norm_w': jnp.ones((HEAD_DIM,), dtype=jnp.float32)}
    _L1_xattn_all = _L1_xattn_setup()
    _L1_xattn_in = {k: v for k, v in _L1_xattn_all.items() if k in ('Wq', 'Wk', 'Wv', 'Wo', 'q_norm_w', 'k_norm_w')}
    del _L1_xattn_all

    def _L1_ffn_setup():
        import jax, jax.numpy as jnp
        import numpy as np
        E = 8
        D = 128
        DO = 128
        R = 64
        H = 32
        B, T = (8, 256)
        key = jax.random.key(seed)
        ks = jax.random.split(key, 12)
        s = lambda k, shape, fan: jax.random.normal(k, shape, jnp.float32) / np.sqrt(fan)
        return {'x': jax.random.normal(ks[0], (B, T, D), jnp.float32), 'W_base': s(ks[1], (D, DO), D), 'b_base': jnp.zeros((DO,), jnp.float32), 'Wd1': s(ks[2], (E, D, H), D), 'bd1': jnp.zeros((E, H), jnp.float32), 'Wd2': s(ks[3], (E, H, D), H), 'bd2': jnp.zeros((E, D), jnp.float32), 'Wa_down': s(ks[4], (E, D, R), D), 'ba_down': jnp.zeros((E, R), jnp.float32), 'Wa_up': s(ks[5], (E, R, DO), R), 'ba_up': jnp.zeros((E, DO), jnp.float32)}
    _L1_ffn_all = _L1_ffn_setup()
    _L1_ffn_in = {k: v for k, v in _L1_ffn_all.items() if k in ('W_base', 'b_base', 'Wd1', 'bd1', 'Wd2', 'bd2', 'Wa_down', 'ba_down', 'Wa_up', 'ba_up')}
    del _L1_ffn_all

    def _L2_xattn_setup():
        import jax, jax.numpy as jnp
        import numpy as np
        B, SQ, SKV, D, H = (2, 256, 256, 128, 16)
        HD = D // H
        ROPE_BASE = 10000.0

        def _rope_interleaved(x):
            s, hd = (x.shape[1], x.shape[-1])
            dim = hd // 2
            freqs = jnp.exp(-jnp.arange(dim, dtype=x.dtype) * jnp.log(jnp.asarray(ROPE_BASE, x.dtype)) / dim)
            ang = jnp.arange(s, dtype=x.dtype)[:, None] * freqs[None, :]
            cos = jnp.cos(ang)[None, :, None, :]
            sin = jnp.sin(ang)[None, :, None, :]
            xe, xo = (x[..., ::2], x[..., 1::2])
            re = xe * cos - xo * sin
            ro = xe * sin + xo * cos
            return jnp.stack([re, ro], axis=-1).reshape(x.shape)
        key = jax.random.key(seed)
        ks = jax.random.split(key, 6)
        s = 1.0 / np.sqrt(D)
        return {'x_q': jax.random.normal(ks[0], (B, SQ, D), jnp.float32), 'x_kv': jax.random.normal(ks[1], (B, SKV, D), jnp.float32), 'wq': jax.random.normal(ks[2], (D, D), jnp.float32) * s, 'bq': jnp.zeros((D,), jnp.float32), 'wk': jax.random.normal(ks[3], (D, D), jnp.float32) * s, 'bk': jnp.zeros((D,), jnp.float32), 'wv': jax.random.normal(ks[4], (D, D), jnp.float32) * s, 'bv': jnp.zeros((D,), jnp.float32), 'wo': jax.random.normal(ks[5], (D, D), jnp.float32) * s, 'bo': jnp.zeros((D,), jnp.float32)}
    _L2_xattn_all = _L2_xattn_setup()
    _L2_xattn_in = {k: v for k, v in _L2_xattn_all.items() if k in ('wq', 'bq', 'wk', 'bk', 'wv', 'bv', 'wo', 'bo')}
    del _L2_xattn_all

    def _L2_ffn_setup():
        import jax, jax.numpy as jnp
        import numpy as np
        B, S, H = (2, 512, 128)
        E, K, I = (8, 2, 176)
        key = jax.random.key(seed)
        ks = jax.random.split(key, 9)
        sc = 0.02
        return {'hidden_states': jax.random.normal(ks[0], (B, S, H), jnp.float32), 'gate_w': jax.random.normal(ks[1], (E, H), jnp.float32) * sc, 'w_gate': jax.random.normal(ks[2], (E, H, I), jnp.float32) * sc, 'w_up': jax.random.normal(ks[3], (E, H, I), jnp.float32) * sc, 'w_down': jax.random.normal(ks[4], (E, I, H), jnp.float32) * sc, 'sw_gate': jax.random.normal(ks[5], (H, I), jnp.float32) * sc, 'sw_up': jax.random.normal(ks[6], (H, I), jnp.float32) * sc, 'sw_down': jax.random.normal(ks[7], (I, H), jnp.float32) * sc, 'shared_gate_w': jax.random.normal(ks[8], (1, H), jnp.float32) * sc}
    _L2_ffn_all = _L2_ffn_setup()
    _L2_ffn_in = {k: v for k, v in _L2_ffn_all.items() if k in ('gate_w', 'w_gate', 'w_up', 'w_down', 'sw_gate', 'sw_up', 'sw_down', 'shared_gate_w')}
    del _L2_ffn_all

    def _L3_xattn_setup():
        import jax, jax.numpy as jnp
        import numpy as np
        EMBED_SIZE = 128
        HEADS = 16
        HEAD_DIM = EMBED_SIZE // HEADS
        N, L = (2, 256)
        key = jax.random.key(seed)
        ks = jax.random.split(key, 6)
        values = jax.random.normal(ks[0], (N, L, EMBED_SIZE), dtype=jnp.float32)
        keys_t = jax.random.normal(ks[1], (N, L, EMBED_SIZE), dtype=jnp.float32)
        query = jax.random.normal(ks[2], (N, L, EMBED_SIZE), dtype=jnp.float32)
        mask = jax.random.randint(ks[3], (N, 1, L, L), 0, 2, dtype=jnp.int32)
        Wo = jax.random.normal(ks[4], (EMBED_SIZE, EMBED_SIZE), dtype=jnp.float32) * EMBED_SIZE ** (-0.5)
        bo = jax.random.normal(ks[5], (EMBED_SIZE,), dtype=jnp.float32) * 0.01
        return {'values': values, 'keys': keys_t, 'query': query, 'mask': mask, 'Wo': Wo, 'bo': bo}
    _L3_xattn_all = _L3_xattn_setup()
    _L3_xattn_in = {k: v for k, v in _L3_xattn_all.items() if k in ('Wo', 'bo')}
    del _L3_xattn_all

    def _L3_ffn_setup():
        import jax, jax.numpy as jnp
        import numpy as np
        QMAX = 127.0

        def _ste_round(v):
            return v + jax.lax.stop_gradient(jnp.round(v) - v)

        def _act_fake_quant(x, clip_factor):
            scale = jax.nn.sigmoid(clip_factor) * jnp.max(jnp.abs(x)) / QMAX
            return jnp.clip(_ste_round(x / scale), -QMAX - 1.0, QMAX) * scale

        def _weight_fake_quant(w):
            scale = jnp.max(jnp.abs(w), axis=1, keepdims=True) / QMAX
            return jnp.clip(_ste_round(w / scale), -QMAX - 1.0, QMAX) * scale
        key = jax.random.key(seed)
        k1, k2, k3, k4 = jax.random.split(key, 4)
        B, S, H, I = (8, 1024, 128, 352)
        return {'x': jax.random.normal(k1, (B, S, H), dtype=jnp.float32), 'clip_x': jnp.full((1,), 4.0, dtype=jnp.float32), 'clip_down': jnp.full((1,), 4.0, dtype=jnp.float32), 'w_gate': jax.random.normal(k2, (I, H), dtype=jnp.float32) * 0.02, 'w_up': jax.random.normal(k3, (I, H), dtype=jnp.float32) * 0.02, 'w_down': jax.random.normal(k4, (H, I), dtype=jnp.float32) * 0.02}
    _L3_ffn_all = _L3_ffn_setup()
    _L3_ffn_in = {k: v for k, v in _L3_ffn_all.items() if k in ('clip_x', 'clip_down', 'w_gate', 'w_up', 'w_down')}
    del _L3_ffn_all
    return {'x': x, 'ctx_1024': ctx_1024, '_lenS2': _lenS2, 'mask_Bx1xSxS2_ik1': mask_Bx1xSxS2_ik1, 'g_xattn': g_xattn, 'g_ffn': g_ffn, 'L0_xattn_igate_kernel': _L0_xattn_in['igate_kernel'], 'L0_xattn_igate_bias': _L0_xattn_in['igate_bias'], 'L0_xattn_fgate_kernel': _L0_xattn_in['fgate_kernel'], 'L0_xattn_fgate_bias': _L0_xattn_in['fgate_bias'], 'L0_xattn_outnorm_scale': _L0_xattn_in['outnorm_scale'], 'L0_ffn_w_q': _L0_ffn_in['w_q'], 'L0_ffn_w_k': _L0_ffn_in['w_k'], 'L0_ffn_w_gate': _L0_ffn_in['w_gate'], 'L0_ffn_value_experts': _L0_ffn_in['value_experts'], 'L0_ffn_output_experts': _L0_ffn_in['output_experts'], 'L1_xattn_Wq': _L1_xattn_in['Wq'], 'L1_xattn_Wk': _L1_xattn_in['Wk'], 'L1_xattn_Wv': _L1_xattn_in['Wv'], 'L1_xattn_Wo': _L1_xattn_in['Wo'], 'L1_xattn_q_norm_w': _L1_xattn_in['q_norm_w'], 'L1_xattn_k_norm_w': _L1_xattn_in['k_norm_w'], 'L1_ffn_W_base': _L1_ffn_in['W_base'], 'L1_ffn_b_base': _L1_ffn_in['b_base'], 'L1_ffn_Wd1': _L1_ffn_in['Wd1'], 'L1_ffn_bd1': _L1_ffn_in['bd1'], 'L1_ffn_Wd2': _L1_ffn_in['Wd2'], 'L1_ffn_bd2': _L1_ffn_in['bd2'], 'L1_ffn_Wa_down': _L1_ffn_in['Wa_down'], 'L1_ffn_ba_down': _L1_ffn_in['ba_down'], 'L1_ffn_Wa_up': _L1_ffn_in['Wa_up'], 'L1_ffn_ba_up': _L1_ffn_in['ba_up'], 'L2_xattn_wq': _L2_xattn_in['wq'], 'L2_xattn_bq': _L2_xattn_in['bq'], 'L2_xattn_wk': _L2_xattn_in['wk'], 'L2_xattn_bk': _L2_xattn_in['bk'], 'L2_xattn_wv': _L2_xattn_in['wv'], 'L2_xattn_bv': _L2_xattn_in['bv'], 'L2_xattn_wo': _L2_xattn_in['wo'], 'L2_xattn_bo': _L2_xattn_in['bo'], 'L2_ffn_gate_w': _L2_ffn_in['gate_w'], 'L2_ffn_w_gate': _L2_ffn_in['w_gate'], 'L2_ffn_w_up': _L2_ffn_in['w_up'], 'L2_ffn_w_down': _L2_ffn_in['w_down'], 'L2_ffn_sw_gate': _L2_ffn_in['sw_gate'], 'L2_ffn_sw_up': _L2_ffn_in['sw_up'], 'L2_ffn_sw_down': _L2_ffn_in['sw_down'], 'L2_ffn_shared_gate_w': _L2_ffn_in['shared_gate_w'], 'L3_xattn_Wo': _L3_xattn_in['Wo'], 'L3_xattn_bo': _L3_xattn_in['bo'], 'L3_ffn_clip_x': _L3_ffn_in['clip_x'], 'L3_ffn_clip_down': _L3_ffn_in['clip_down'], 'L3_ffn_w_gate': _L3_ffn_in['w_gate'], 'L3_ffn_w_up': _L3_ffn_in['w_up'], 'L3_ffn_w_down': _L3_ffn_in['w_down']}

def reference(x, ctx_1024, _lenS2, mask_Bx1xSxS2_ik1, g_xattn, g_ffn, L0_xattn_igate_kernel, L0_xattn_igate_bias, L0_xattn_fgate_kernel, L0_xattn_fgate_bias, L0_xattn_outnorm_scale, L0_ffn_w_q, L0_ffn_w_k, L0_ffn_w_gate, L0_ffn_value_experts, L0_ffn_output_experts, L1_xattn_Wq, L1_xattn_Wk, L1_xattn_Wv, L1_xattn_Wo, L1_xattn_q_norm_w, L1_xattn_k_norm_w, L1_ffn_W_base, L1_ffn_b_base, L1_ffn_Wd1, L1_ffn_bd1, L1_ffn_Wd2, L1_ffn_bd2, L1_ffn_Wa_down, L1_ffn_ba_down, L1_ffn_Wa_up, L1_ffn_ba_up, L2_xattn_wq, L2_xattn_bq, L2_xattn_wk, L2_xattn_bk, L2_xattn_wv, L2_xattn_bv, L2_xattn_wo, L2_xattn_bo, L2_ffn_gate_w, L2_ffn_w_gate, L2_ffn_w_up, L2_ffn_w_down, L2_ffn_sw_gate, L2_ffn_sw_up, L2_ffn_sw_down, L2_ffn_shared_gate_w, L3_xattn_Wo, L3_xattn_bo, L3_ffn_clip_x, L3_ffn_clip_down, L3_ffn_w_gate, L3_ffn_w_up, L3_ffn_w_down):
    import jax
    import jax.numpy as jnp

    def _L0_xattn_ref(q, k, v, igate_kernel, igate_bias, fgate_kernel, fgate_bias, outnorm_scale):
        import jax, jax.numpy as jnp
        import numpy as np
        B, S, H, NH = (2, 256, 128, 4)
        DH = H // NH
        EPS_BACKEND = 1e-06
        EPS_LN = 1e-06

        def _mlstm_parallel_stabilized(q, k, v, igate_preact, fgate_preact):
            b, nh, s, dh = q.shape
            log_fg = jax.nn.log_sigmoid(fgate_preact)
            cs = jnp.concatenate([jnp.zeros((b, nh, 1), q.dtype), jnp.cumsum(log_fg[..., 0], axis=2)], axis=2)
            fg_matrix = cs[:, :, :, None] - cs[:, :, None, :]
            fg_matrix = fg_matrix[:, :, 1:, 1:]
            causal = jnp.tril(jnp.ones((s, s), dtype=bool))
            log_fg_matrix = jnp.where(causal, fg_matrix, -jnp.inf)
            log_D = log_fg_matrix + jnp.swapaxes(igate_preact, -2, -1)
            max_log_D = jnp.max(log_D, axis=-1, keepdims=True)
            D = jnp.exp(log_D - max_log_D)
            qk = jnp.einsum('bhsd,bhtd->bhst', q, k) / jnp.sqrt(jnp.asarray(dh, q.dtype))
            C = qk * D
            normalizer = jnp.maximum(jnp.abs(jnp.sum(C, axis=-1, keepdims=True)), jnp.exp(-max_log_D))
            C_norm = C / (normalizer + EPS_BACKEND)
            return jnp.einsum('bhst,bhtd->bhsd', C_norm, v)

        def _multihead_layernorm(x, scale):
            mean = jnp.mean(x, axis=-1, keepdims=True)
            var = jnp.var(x, axis=-1, keepdims=True)
            xn = (x - mean) * jax.lax.rsqrt(var + EPS_LN)
            return xn * scale.reshape(NH, 1, DH)
        b, s, h = q.shape
        gate_in = jnp.concatenate([q, k, v], axis=-1)
        ig = gate_in @ igate_kernel + igate_bias
        fg = gate_in @ fgate_kernel + fgate_bias
        ig = jnp.transpose(ig, (0, 2, 1))[..., None]
        fg = jnp.transpose(fg, (0, 2, 1))[..., None]
        qh = jnp.transpose(q.reshape(b, s, NH, DH), (0, 2, 1, 3))
        kh = jnp.transpose(k.reshape(b, s, NH, DH), (0, 2, 1, 3))
        vh = jnp.transpose(v.reshape(b, s, NH, DH), (0, 2, 1, 3))
        hs = _mlstm_parallel_stabilized(qh, kh, vh, ig, fg)
        hn = _multihead_layernorm(hs, outnorm_scale)
        return jnp.transpose(hn, (0, 2, 1, 3)).reshape(b, s, h)

    def _L0_ffn_ref(x, w_q, w_k, w_gate, value_experts, output_experts):
        import jax, jax.numpy as jnp
        import numpy as np
        B, N, DIM = (2, 256, 128)
        HEADS, DIM_HEAD, EXPERTS = (8, 64, 8)
        SCALE = DIM_HEAD ** (-0.5)
        b, n, _ = x.shape
        q = (x @ w_q).reshape(b, n, HEADS, DIM_HEAD).transpose(0, 2, 1, 3)
        k = (x @ w_k).reshape(b, n, HEADS, DIM_HEAD).transpose(0, 2, 1, 3)
        gates = jax.nn.sigmoid((x @ w_gate).reshape(b, n, HEADS, EXPERTS).transpose(0, 2, 1, 3))
        sel = jnp.argmax(gates, axis=-1)
        gm = jax.nn.one_hot(sel, EXPERTS, dtype=x.dtype) * gates
        values = jnp.einsum('bhne,ehdk,bnd->bhnk', gm, value_experts, x)
        sim = jnp.einsum('bhid,bhjd->bhij', q * SCALE, k)
        causal_mask = jnp.triu(jnp.ones((n, n), dtype=bool), 1)
        sim = jnp.where(causal_mask, jnp.finfo(sim.dtype).min, sim)
        attn = jax.nn.softmax(sim, axis=-1)
        out = jnp.einsum('bhij,bhjk->bhik', attn, values)
        out = jnp.einsum('bhne,ehkd,bhnk->bhnd', gm, output_experts, out)
        return out.sum(axis=1)

    def _L1_xattn_ref(q, kv, x_seqlens, Wq, Wk, Wv, Wo, q_norm_w, k_norm_w):
        import jax, jax.numpy as jnp
        import numpy as np
        DIM, HEADS, HEAD_DIM = (128, 16, 64)
        B, L, S = (4, 256, 256)
        EPS = 1e-05
        NEG_INF = -1000000000.0

        def rms_norm(x, w):
            var = jnp.mean(jnp.square(x), axis=-1, keepdims=True)
            return x * jax.lax.rsqrt(var + EPS) * w
        b, l, _ = q.shape
        s = kv.shape[1]
        qh = (q @ Wq).reshape(b, l, HEADS, HEAD_DIM).transpose(0, 2, 1, 3)
        kh = (kv @ Wk).reshape(b, s, HEADS, HEAD_DIM).transpose(0, 2, 1, 3)
        vh = (kv @ Wv).reshape(b, s, HEADS, HEAD_DIM).transpose(0, 2, 1, 3)
        qh = rms_norm(qh, q_norm_w)
        kh = rms_norm(kh, k_norm_w)
        mask = (jnp.arange(s, dtype=jnp.int32)[None, :] < x_seqlens[:, None])[:, None, None, :]
        scores = jnp.einsum('bhld,bhsd->bhls', qh, kh) * (1.0 / np.sqrt(HEAD_DIM))
        scores = jnp.where(mask, scores, NEG_INF)
        attn = jax.nn.softmax(scores, axis=-1)
        o = jnp.einsum('bhls,bhsd->bhld', attn, vh)
        o = o.transpose(0, 2, 1, 3).reshape(b, l, HEADS * HEAD_DIM)
        return o @ Wo

    def _L1_ffn_ref(x, W_base, b_base, Wd1, bd1, Wd2, bd2, Wa_down, ba_down, Wa_up, ba_up):
        import jax, jax.numpy as jnp
        import numpy as np
        E = 8
        D = 128
        DO = 128
        R = 64
        H = 32
        B, T = (8, 256)
        base = jnp.einsum('btd,do->bto', x, W_base) + b_base
        h = jax.nn.relu(jnp.einsum('btd,edh->ebth', x, Wd1) + bd1[:, None, None, :])
        recon = jnp.einsum('ebth,ehd->ebtd', h, Wd2) + bd2[:, None, None, :]
        losses = jnp.mean((recon - x[None]) ** 2, axis=(2, 3))
        idx = jnp.argmin(losses, axis=0)
        a = jax.nn.relu(jnp.einsum('btd,bdr->btr', x, Wa_down[idx]) + ba_down[idx][:, None, :])
        adapter_out = jnp.einsum('btr,bro->bto', a, Wa_up[idx]) + ba_up[idx][:, None, :]
        return base + adapter_out

    def _L2_xattn_ref(x_q, x_kv, wq, bq, wk, bk, wv, bv, wo, bo):
        import jax, jax.numpy as jnp
        import numpy as np
        B, SQ, SKV, D, H = (2, 256, 256, 128, 16)
        HD = D // H
        ROPE_BASE = 10000.0

        def _rope_interleaved(x):
            s, hd = (x.shape[1], x.shape[-1])
            dim = hd // 2
            freqs = jnp.exp(-jnp.arange(dim, dtype=x.dtype) * jnp.log(jnp.asarray(ROPE_BASE, x.dtype)) / dim)
            ang = jnp.arange(s, dtype=x.dtype)[:, None] * freqs[None, :]
            cos = jnp.cos(ang)[None, :, None, :]
            sin = jnp.sin(ang)[None, :, None, :]
            xe, xo = (x[..., ::2], x[..., 1::2])
            re = xe * cos - xo * sin
            ro = xe * sin + xo * cos
            return jnp.stack([re, ro], axis=-1).reshape(x.shape)
        b, sq, _ = x_q.shape
        skv = x_kv.shape[1]
        q = (jnp.einsum('bsd,ed->bse', x_q, wq) + bq).reshape(b, sq, H, HD)
        k = (jnp.einsum('bsd,ed->bse', x_kv, wk) + bk).reshape(b, skv, H, HD)
        v = (jnp.einsum('bsd,ed->bse', x_kv, wv) + bv).reshape(b, skv, H, HD)
        q = _rope_interleaved(q)
        k = _rope_interleaved(k)
        scores = jnp.einsum('bqhd,bkhd->bhqk', q, k) / jnp.sqrt(jnp.asarray(HD, q.dtype))
        attn = jax.nn.softmax(scores, axis=-1)
        ctx = jnp.einsum('bhqk,bkhd->bqhd', attn, v).reshape(b, sq, D)
        return jnp.einsum('bsd,ed->bse', ctx, wo) + bo

    def _L2_ffn_ref(hidden_states, gate_w, w_gate, w_up, w_down, sw_gate, sw_up, sw_down, shared_gate_w):
        import jax, jax.numpy as jnp
        import numpy as np
        B, S, H = (2, 512, 128)
        E, K, I = (8, 2, 176)
        b, s, h = hidden_states.shape
        x = hidden_states.reshape(-1, h)
        logits = jnp.einsum('th,eh->te', x, gate_w)
        probs = jax.nn.softmax(logits.astype(jnp.float32), axis=-1)
        topk_w, topk_i = jax.lax.top_k(probs, K)
        topk_w = topk_w / jnp.sum(topk_w, axis=-1, keepdims=True)
        combine = jnp.sum(jax.nn.one_hot(topk_i, E, dtype=topk_w.dtype) * topk_w[..., None], axis=1)
        combine = combine.astype(x.dtype)
        g = jnp.einsum('th,ehi->eti', x, w_gate)
        u = jnp.einsum('th,ehi->eti', x, w_up)
        eo = jnp.einsum('eti,eih->eth', jax.nn.silu(g) * u, w_down)
        out = jnp.einsum('te,eth->th', combine, eo)
        sg = jax.nn.sigmoid(jnp.einsum('th,oh->to', x, shared_gate_w))
        so = jax.nn.silu(x @ sw_gate) * (x @ sw_up) @ sw_down
        out = out + sg * so
        return out.reshape(b, s, h)

    def _L3_xattn_ref(values, keys, query, mask, Wo, bo):
        import jax, jax.numpy as jnp
        import numpy as np
        EMBED_SIZE = 128
        HEADS = 16
        HEAD_DIM = EMBED_SIZE // HEADS
        N, L = (2, 256)
        n, q_len, _ = query.shape
        v = values.reshape(n, -1, HEADS, HEAD_DIM)
        k = keys.reshape(n, -1, HEADS, HEAD_DIM)
        q = query.reshape(n, q_len, HEADS, HEAD_DIM)
        energy = jnp.einsum('nqhd,nkhd->nhqk', q, k)
        energy = jnp.where(mask == 0, jnp.float32(-1e+20), energy)
        scale = jnp.float32(EMBED_SIZE) ** 0.5
        attn = jax.nn.softmax(energy / scale, axis=3)
        out = jnp.einsum('nhqk,nkhd->nqhd', attn, v).reshape(n, q_len, HEADS * HEAD_DIM)
        return out @ Wo.T + bo

    def _L3_ffn_ref(x, clip_x, clip_down, w_gate, w_up, w_down):
        import jax, jax.numpy as jnp
        import numpy as np
        QMAX = 127.0

        def _ste_round(v):
            return v + jax.lax.stop_gradient(jnp.round(v) - v)

        def _act_fake_quant(x, clip_factor):
            scale = jax.nn.sigmoid(clip_factor) * jnp.max(jnp.abs(x)) / QMAX
            return jnp.clip(_ste_round(x / scale), -QMAX - 1.0, QMAX) * scale

        def _weight_fake_quant(w):
            scale = jnp.max(jnp.abs(w), axis=1, keepdims=True) / QMAX
            return jnp.clip(_ste_round(w / scale), -QMAX - 1.0, QMAX) * scale
        xq = _act_fake_quant(x, clip_x[0])
        gate = jnp.einsum('bsh,ih->bsi', xq, _weight_fake_quant(w_gate))
        up = jnp.einsum('bsh,ih->bsi', xq, _weight_fake_quant(w_up))
        h = _act_fake_quant(jax.nn.silu(gate) * up, clip_down[0])
        return jnp.einsum('bsi,hi->bsh', h, _weight_fake_quant(w_down))
    x = x + jnp.tanh(g_xattn[0]) * _L0_xattn_ref(_layernorm(x, axis=-1), ctx_1024, ctx_1024, L0_xattn_igate_kernel, L0_xattn_igate_bias, L0_xattn_fgate_kernel, L0_xattn_fgate_bias, L0_xattn_outnorm_scale)
    x = x + jnp.tanh(g_ffn[0]) * _L0_ffn_ref(_layernorm(x, axis=-1), L0_ffn_w_q, L0_ffn_w_k, L0_ffn_w_gate, L0_ffn_value_experts, L0_ffn_output_experts)
    x = x + jnp.tanh(g_xattn[1]) * _L1_xattn_ref(_layernorm(x, axis=-1), ctx_1024, _lenS2, L1_xattn_Wq, L1_xattn_Wk, L1_xattn_Wv, L1_xattn_Wo, L1_xattn_q_norm_w, L1_xattn_k_norm_w)
    x = x + jnp.tanh(g_ffn[1]) * _L1_ffn_ref(_layernorm(x, axis=-1), L1_ffn_W_base, L1_ffn_b_base, L1_ffn_Wd1, L1_ffn_bd1, L1_ffn_Wd2, L1_ffn_bd2, L1_ffn_Wa_down, L1_ffn_ba_down, L1_ffn_Wa_up, L1_ffn_ba_up)
    x = x + jnp.tanh(g_xattn[2]) * _L2_xattn_ref(_layernorm(x, axis=-1), ctx_1024, L2_xattn_wq, L2_xattn_bq, L2_xattn_wk, L2_xattn_bk, L2_xattn_wv, L2_xattn_bv, L2_xattn_wo, L2_xattn_bo)
    x = x + jnp.tanh(g_ffn[2]) * _L2_ffn_ref(_layernorm(x, axis=-1), L2_ffn_gate_w, L2_ffn_w_gate, L2_ffn_w_up, L2_ffn_w_down, L2_ffn_sw_gate, L2_ffn_sw_up, L2_ffn_sw_down, L2_ffn_shared_gate_w)
    x = x + jnp.tanh(g_xattn[3]) * _L3_xattn_ref(ctx_1024, ctx_1024, _layernorm(x, axis=-1), mask_Bx1xSxS2_ik1, L3_xattn_Wo, L3_xattn_bo)
    x = x + jnp.tanh(g_ffn[3]) * _L3_ffn_ref(_layernorm(x, axis=-1), L3_ffn_clip_x, L3_ffn_clip_down, L3_ffn_w_gate, L3_ffn_w_up, L3_ffn_w_down)
    return x

_drawn_inputs = setup_inputs


def setup_inputs(seed=0):
    import zlib

    import numpy as np

    out = dict(_drawn_inputs(seed))
    spreads = {'L0_xattn_igate_kernel': (0.0, 0.1),
     'L0_xattn_fgate_kernel': (0.0, 0.1),
     'L0_xattn_outnorm_scale': (1.0, 0.2),
     'L1_xattn_q_norm_w': (1.0, 0.2),
     'L1_xattn_k_norm_w': (1.0, 0.2),
     'L1_ffn_b_base': (0.0, 0.1),
     'L1_ffn_bd1': (0.0, 0.1),
     'L1_ffn_bd2': (0.0, 0.1),
     'L1_ffn_ba_down': (0.0, 0.1),
     'L1_ffn_ba_up': (0.0, 0.1),
     'L2_xattn_bq': (0.0, 0.8),
     'L2_xattn_bk': (0.0, 0.8),
     'L2_xattn_bv': (0.0, 0.1),
     'L2_xattn_bo': (0.0, 0.1)}
    factors = {'L0_xattn_igate_bias': 8.0,
     'L0_ffn_w_q': 8.0,
     'L0_ffn_w_k': 8.0,
     'L0_ffn_w_gate': 8.0,
     'L0_ffn_value_experts': 8.0,
     'L0_ffn_output_experts': 8.0,
     'L2_ffn_gate_w': 8.0,
     'L2_ffn_w_gate': 8.0,
     'L2_ffn_w_up': 8.0,
     'L2_ffn_w_down': 8.0,
     'L2_ffn_sw_gate': 8.0,
     'L2_ffn_sw_up': 8.0,
     'L2_ffn_sw_down': 8.0,
     'L2_ffn_shared_gate_w': 8.0,
     'L3_xattn_bo': 8.0,
     'L3_ffn_w_gate': 8.0,
     'L3_ffn_w_up': 8.0,
     'L3_ffn_w_down': 8.0}
    for name, (base, spread) in spreads.items():
        noise = np.random.default_rng([zlib.crc32(name.encode()), seed]).standard_normal(out[name].shape)
        drawn = base * np.exp(spread * noise) if base else spread * noise
        out[name] = jnp.asarray(drawn.astype(out[name].dtype))
    for name, factor in factors.items():
        out[name] = (out[name] * factor).astype(out[name].dtype)
    return out
```

```python
import concourse.bass as bass
from concourse import mybir
from contextlib import ExitStack
import numpy as np

F32 = mybir.dt.float32
BF16 = mybir.dt.bfloat16
I32 = mybir.dt.int32
ALU = mybir.AluOpType
ACT = mybir.ActivationFunctionType
AX = mybir.AxisListType

P = 128
SEQ = 64
NSEQ = 64
D = 128
TILES = NSEQ * SEQ // P
G = 4
GROUPS = TILES // G
GT = G * P
COUNTERS = 52
NEG = -1e30

CONST = {}
_at = 0
for _name, _w in (("ident", 128), ("tri", 128), ("caus_t", 64), ("caus_n", 64), ("hm", 4), ("rope_c", 128),
                  ("rope_s", 128), ("prio", 8), ("iota", 64)):
    CONST[_name] = (_at, _at + _w)
    _at += _w
CONST_W = _at

WEIGHTS = {}
_at = 0
for _name, _w in (("l0_gate", 24), ("l0_q", 512), ("l0_k", 512), ("l0_g", 64), ("l0_ve", 4096), ("l0_oe", 4096),
                  ("l1_q", 1024), ("l1_k", 1024), ("l1_v", 1024), ("l1_o", 1024),
                  ("l1_d1", 256), ("l1_d2", 256), ("l1_base", 128), ("l1_dn", 512), ("l1_up", 512),
                  ("l2_q", 128), ("l2_k", 128), ("l2_v", 128), ("l2_o", 128),
                  ("l2_gw", 9), ("l2_wg", 1664), ("l2_wu", 1664), ("l2_wd", 1664),
                  ("l3_o", 128), ("l3_g", 384), ("l3_u", 384), ("l3_d", 352)):
    WEIGHTS[_name] = (_at, _at + _w)
    _at += _w
WEIGHTS_W = _at
LATE = WEIGHTS["l2_q"][0]
assert WEIGHTS_W - LATE <= WEIGHTS["l1_q"][0]
LOADS = [("l0_gate", "l0_gate"), ("l0_q", "l0_oe"), ("l1_q", "l1_o"), ("l1_d1", "l1_up"), ("l2_q", "l2_o"),
         ("l2_gw", "l2_wd"), ("l3_o", "l3_o"), ("l3_g", "l3_d")]

ROWS = {}
_at = 0
for _name, _w in (("gates", 8), ("l0_bias", 8), ("l0_norm", 128), ("l2_bq", 128), ("l2_bk", 128), ("l2_bv", 128),
                  ("clips", 2)):
    ROWS[_name] = (_at, _at + _w)
    _at += _w
ROWS_W = _at

COLS = {}
_at = 0
for _name, _w in (("l1_qw", 1), ("l1_kw", 1), ("l1_bd1", 2), ("l1_bd2", 8), ("l1_bdn", 4), ("l1_bbase", 1),
                  ("l1_bup", 8), ("l2_bo", 1), ("l3_bo", 1)):
    COLS[_name] = (_at, _at + _w)
    _at += _w
COLS_W = _at


def count(n):
    return n + 1


class Chain:

    def __init__(self, eng, sem, base, total):
        self.eng, self.sem, self.base, self.total, self.n = eng, sem, base, total, 0

    def link(self, ins):
        self.n += 1
        ins.then_inc(self.sem, 1)
        self.eng.wait_ge(self.sem, count(self.base + self.n))

    def done(self):
        assert self.n == self.total, (self.n, self.total)


class Core:

    def __init__(self, nc, ctx):
        self.nc, self.ctx = nc, ctx
        self.x = self.sb(ctx, "x_all", [P, TILES, D])
        self.ctx_tok = self.sb(ctx, "ctx_all", [P, TILES, D])
        self.xnT = self.sb(ctx, "xnT_all", [P, TILES * P])
        self.ctxT = self.sb(ctx, "ctxT_all", [P, TILES * P])
        self.w_all = self.sb(ctx, "w_all", [P, LATE])
        self.consts = self.sb(ctx, "consts", [P, CONST_W])
        self.rows = self.sb(ctx, "rows", [P, ROWS_W])
        self.cols = self.sb(ctx, "cols", [P, COLS_W])
        self.tanh_g = self.sb(ctx, "tanh_g", [P, 8])
        self.ident_bf = self.sb(ctx, "ident_bf", [P, P], BF16)
        self.half = self.sb(ctx, "minus_half", [P, 128])
        self.halves = [[self.sem(f"counter{h}_{i}") for i in range(COUNTERS)] for h in range(2)]
        self.x_loaded = self.sem("x_loaded")
        self.ctx_loaded = self.sem("ctx_loaded")
        self.ctx_sems = [self.sem(f"ctx_{event}") for event in ("staged", "turned", "copied")]
        self.small_loaded = self.sem("small_loaded")
        self.w_loaded = [self.sem(f"w_loaded{i}") for i in range(len(LOADS))]
        self.st = self.sb(ctx, "stats", [P, TILES, 6])
        self.mv = self.sb(ctx, "mean_rstd", [P, 6, TILES])
        self.xn = self.sb(ctx, "xn", [P, G, D])

    def sb(self, ctx, name, shape, dt=F32):
        return ctx.enter_context(self.nc.sbuf_tensor(name, shape, dt))

    def ps(self, ctx, name, shape=(P, 512), dt=F32):
        return ctx.enter_context(self.nc.psum_tensor(name, list(shape), dt))

    def sem(self, name):
        return self.ctx.enter_context(self.nc.semaphore(name))

    def counters(self, k):
        half = iter(self.halves[k % 2])
        return lambda event: next(half)

    def renew(self, sp, k):
        half = self.halves[k % 2]
        first, last = half[0].num, half[-1].num
        assert last - first == COUNTERS - 1
        sp.sem_clear(range(first, last + 1))
        for sem in half:
            sp.sem_inc(sem, 1)

    def const(self, name, parts=P):
        a, b = CONST[name]
        return self.consts[0:parts, a:b]

    def w(self, name):
        a, b = WEIGHTS[name]
        if a >= LATE:
            a, b = a - LATE, b - LATE
        return self.w_all[:, a:b]

    def row(self, name):
        a, b = ROWS[name]
        return self.rows[:, a:b]

    def col(self, name):
        a, b = COLS[name]
        return self.cols[:, a:b]


def bcast(ap, axis, n):
    ap = ap.unsqueeze(axis)
    shape = list(ap.shape)
    shape[axis] = n
    return ap.broadcast_to(shape)


class NormSems:

    def __init__(self, sem):
        self.stats = sem("statistics of a tile")
        self.chain = sem("chain")
        self.var = sem("variances, means")
        self.rstd = sem("1 / deviations")
        self.xn = sem("xn of a tile")
        self.turned = sem("a tile turned")
        self.ready = sem("xnT of a group")


def norm_vector(core, nc, eng, s, eps=1e-5):
    with eng.Fori(0, GROUPS) as g:
        for j in range(G):
            nc.vector.bn_stats(core.st[:, g * G + j, :], core.x[:, g * G + j, :]).then_inc(s.stats, 1)
    eng.wait_ge(s.stats, count(TILES))
    ch = Chain(eng, s.chain, 0, 5)
    me, mo = core.st[:, :, 1], core.st[:, :, 4]
    ch.link(nc.vector.tensor_tensor(core.mv[:, 2, :], me, mo, ALU.subtract))
    ch.link(nc.vector.tensor_tensor(core.mv[:, 3, :], core.st[:, :, 2], core.st[:, :, 5], ALU.add))
    ch.link(nc.vector.scalar_tensor_tensor(core.mv[:, 4, :], core.mv[:, 2, :], 0.25, core.mv[:, 2, :],
                                           ALU.mult, ALU.mult))
    ch.link(nc.vector.tensor_scalar(core.mv[:, 5, :], core.mv[:, 3, :], 1.0 / D, eps, ALU.mult, ALU.add))
    ch.link(nc.vector.tensor_tensor(core.mv[:, 2, :], me, mo, ALU.add))
    ch.done()
    nc.vector.tensor_tensor(core.mv[:, 3, :], core.mv[:, 4, :], core.mv[:, 5, :], ALU.add).then_inc(s.var, 1)
    nc.vector.tensor_scalar(core.mv[:, 0, :], core.mv[:, 2, :], 0.5, None, ALU.mult).then_inc(s.var, 1)
    eng.wait_ge(s.var, count(2))
    eng.wait_ge(s.rstd, count(1))
    with eng.Fori(0, GROUPS) as g:
        eng.wait_ge(s.turned, count(g * G))
        for j in range(G):
            nc.vector.tensor_scalar(core.xn[:, j, :], core.x[:, g * G + j, :], core.mv[:, 0, bass.ds(g * G + j, 1)],
                                    core.mv[:, 1, bass.ds(g * G + j, 1)], ALU.subtract, ALU.mult).then_inc(s.xn, 1)


def norm_gpsimd(core, nc, eng, s):
    eng.wait_ge(s.var, count(1))
    nc.gpsimd.tensor_tensor(core.mv[:, 1, :], core.mv[:, 3, :], core.half[:, 0:TILES], ALU.pow).then_inc(s.rstd, 1)


def norm_tensor(core, nc, eng, s, bank):
    with eng.Fori(0, GROUPS) as g:
        eng.wait_ge(s.ready, count(g))
        for j in range(G):
            eng.wait_ge(s.xn, count(g * G + j + 1))
            nc.tensor.transpose(bank[:, j * P:(j + 1) * P], core.xn[:, j, :], core.const("ident")).then_inc(s.turned, 1)


def norm_scalar(core, nc, eng, s, bank):
    with eng.Fori(0, GROUPS) as g:
        eng.wait_ge(s.turned, count(g * G + G))
        nc.scalar.activation(core.xnT[:, bass.ds(g * GT, GT)], bank[:, :], ACT.Copy).then_inc(s.ready, 1)


def residual_tensor(core, nc, eng, yT, bank, turned):
    for j in range(G):
        ins = nc.tensor.transpose(bank[:, j * P:(j + 1) * P], yT[:, j * P:(j + 1) * P], core.const("ident"))
    ins.then_inc(turned, 1)


def residual_vector(core, nc, g, k, bank, done):
    xs = core.x[:, bass.ds(g * G, G), :]
    nc.vector.scalar_tensor_tensor(xs, bank[:, :].rearrange("p (j d) -> p j d", j=G), core.tanh_g[:, k:k + 1], xs,
                                   ALU.mult, ALU.add).then_inc(done, 1)


def onehot_links(core, nc, ch, out, val, m, eq, prio, op=ALU.max):
    n = list(val.shape)
    last = len(n) - 1
    ch.link(nc.vector.tensor_reduce(m, val, AX.X, op))
    ch.link(nc.vector.tensor_tensor(eq, val, bcast(m, last, 8), ALU.is_equal))
    ch.link(nc.vector.tensor_tensor(eq, eq, prio, ALU.mult))
    ch.link(nc.vector.tensor_reduce(m, eq, AX.X, ALU.max))
    ch.link(nc.vector.tensor_tensor(out, eq, bcast(m, last, 8), ALU.is_equal))


def setup(core, nc, d):
    with nc.Block() as block:
        prep, tanh_ready = core.sem("setup_prep"), core.sem("tanh_ready")

        @block.sync
        def _(sp):
            for sem in core.halves[0] + core.halves[1] + core.ctx_sems:
                sp.sem_inc(sem, 1)
            sp.dma_start(core.consts[:, :], d["consts"]).then_inc(core.small_loaded, 16)
            sp.dma_start(core.cols[:, :], d["cols"]).then_inc(core.small_loaded, 16)
            sp.dma_start(core.rows[:, :], d["rows"].broadcast_to([P, ROWS_W])).then_inc(core.small_loaded, 16)
            sp.dma_start(core.x[:, :, :], d["x"].rearrange("(n p) d -> p n d", p=P)).then_inc(core.x_loaded, 16)
            sp.dma_start(core.ctx_tok[:, :, :],
                         d["ctx"].rearrange("(n p) d -> p n d", p=P)).then_inc(core.ctx_loaded, 16)
            for i, (first, last) in enumerate(LOADS[0:4]):
                a, b = WEIGHTS[first][0], WEIGHTS[last][1]
                sp.dma_start(core.w_all[:, a:b], d["weights"][:, a:b]).then_inc(core.w_loaded[i], 16)
            sp.wait_ge(core.small_loaded, 48)
            sp.wait_ge(core.x_loaded, 16)
            sp.wait_ge(core.ctx_loaded, 16)

        @block.gpsimd
        def _(pool):
            nc.gpsimd.memset(core.half[:, :], -0.5).then_inc(prep, 1)
            pool.wait_ge(core.small_loaded, 48)
            nc.gpsimd.tensor_copy(core.ident_bf[:, :], core.const("ident")).then_inc(prep, 1)
            pool.wait_ge(prep, 2)

        @block.scalar
        def _(act):
            act.wait_ge(core.small_loaded, 48)
            nc.scalar.activation(core.tanh_g[:, :], core.row("gates"), ACT.Tanh).then_inc(tanh_ready, 1)


def late_weights(core, nc, d):
    with nc.Block() as block:
        @block.sync
        def _(sp):
            for i in range(2):
                sp.wait_ge(core.w_loaded[i], 16)
            for i, (first, last) in enumerate(LOADS[4:]):
                a, b = WEIGHTS[first][0], WEIGHTS[last][1]
                sp.dma_start(core.w_all[:, a - LATE:b - LATE], d["weights"][:, a:b]).then_inc(core.w_loaded[4 + i], 16)


def turn_context(core, nc):
    with ExitStack() as ctx:
        bank = core.ps(ctx, "turn_bank")
        stage = core.sb(ctx, "turn_stage", [P, G, D])
        staged, turned, copied = core.ctx_sems
        with nc.Block() as block:
            @block.gpsimd
            def _(pool):
                with pool.Fori(0, GROUPS) as g:
                    pool.wait_ge(turned, count(g))
                    nc.gpsimd.tensor_copy(stage[:, :, :], core.ctx_tok[:, bass.ds(g * G, G), :]).then_inc(staged, 1)

            @block.tensor
            def _(pe):
                with pe.Fori(0, GROUPS) as g:
                    pe.wait_ge(staged, count(g + 1))
                    pe.wait_ge(copied, count(g))
                    for j in range(G):
                        ins = nc.tensor.transpose(bank[:, j * P:(j + 1) * P], stage[:, j, :], core.const("ident"))
                    ins.then_inc(turned, 1)

            @block.scalar
            def _(act):
                with act.Fori(0, GROUPS) as g:
                    act.wait_ge(turned, count(g + 1))
                    nc.scalar.activation(core.ctxT[:, bass.ds(g * GT, GT)], bank[:, :], ACT.Copy).then_inc(copied, 1)


def l0_xattn(core, nc, d):
    NH, DH = 4, 32
    N = G * NH
    wg = core.w("l0_gate").rearrange("p (i n) -> p i n", i=3)
    scratch = nc.dram_tensor("running_max", (2, TILES * NH * SEQ), F32).ap()
    with ExitStack() as ctx:
        sb = lambda name, shape, dt=F32: core.sb(ctx, "l0x_" + name, shape, dt)
        ps = lambda name, shape=(P, 512), dt=F32: core.ps(ctx, "l0x_" + name, shape, dt)
        sem = core.counters(0)
        xs, cs = sb("xs", [P, GT]), sb("cs", [P, GT])
        gates = sb("gates", [P, TILES, 2 * NH])
        f = sb("f", [P, 3, TILES, NH])
        logf = sb("logf", [P, TILES * NH])
        csum = sb("csum", [P, TILES * NH])
        a = sb("a", [P, TILES * NH])
        aT = sb("aT", [P, P])
        mT = sb("mT", [P, P])
        top = sb("top", [P, TILES * NH])
        floor = sb("floor", [P, TILES * NH])
        m_b = sb("m_b", [P, N, SEQ])
        expo = sb("expo", [P, 2, N, SEQ])
        decay = sb("decay", [P, N, SEQ])
        cmat = sb("cmat", [P, N, SEQ])
        va = sb("va", [P, N, DH + 1])
        den = sb("den", [P, 4, N])
        hs = sb("hs", [P, N, DH])
        cen = sb("cen", [P, N, DH])
        sq = sb("sq", [P, N, DH])
        mom = sb("mom", [P, 4, N])
        hn = sb("hn", [P, 2, N, DH])
        score = [ps(f"score{h}") for h in range(NH)]
        po = [ps(f"po{i}") for i in range(2)]
        misc, gbank = ps("misc"), ps("gbank")
        ns = NormSems(sem)
        staged, gate_done, gates_ready = sem("staged"), sem("gate_done"), sem("gates_ready")
        abs_done, exp_f_done, ln_done, logf_ready = sem("abs_done"), sem("exp_f_done"), sem("ln_done"), sem("logf_ready")
        sum_done, chain, a_ready, a_turned, scan_done = (sem("sum_done"), sem("chain"), sem("a_ready"), sem("a_turned"),
                                                         sem("scan_done"))
        m_turned, floor_in, floor_ready, m_stored = sem("m_turned"), sem("floor_in"), sem("floor_ready"), core.sem("m_stored")
        m_loaded, part_done, expo_ready, decay_ready = core.sem("m_loaded"), sem("part_done"), sem("expo_ready"), sem("decay_ready")
        qk_done, cmat_ready, va_ready, pv_done = sem("qk_done"), sem("cmat_ready"), sem("va_ready"), sem("pv_done")
        ones_set, abs_sum, tail, var_ready, rstd_ready = (sem("ones_set"), sem("abs_sum"), sem("tail"), sem("var_ready"),
                                                          sem("rstd_ready"))
        sq_done, cen_done, res_done, may_pv = sem("sq_done"), sem("cen_done"), sem("res_done"), sem("may_pv")
        out_read = sem("out_read")

        with nc.Block() as block:
            @block.sync
            def _(sp):
                core.renew(sp, 1)
                sp.wait_ge(scan_done, count(2))
                sp.dma_start(scratch.rearrange("b (n s) -> n b s", s=SEQ), mT[:, :].rearrange("n (b s) -> n b s", b=2))\
                    .then_inc(m_stored, 16)
                sp.wait_ge(m_stored, 16)
                with sp.Fori(0, GROUPS) as g:
                    sp.wait_ge(part_done, count(g))
                    for b in range(2):
                        sp.dma_start(m_b[b * SEQ:(b + 1) * SEQ, :, :].rearrange("p n s -> p (n s)"),
                                     scratch[b:b + 1, bass.ds(g * N * SEQ, N * SEQ)].broadcast_to([SEQ, N * SEQ]))\
                            .then_inc(m_loaded, 16)

            @block.gpsimd
            def _(pool):
                nc.gpsimd.memset(va[:, :, :], 1.0).then_inc(ones_set, 1)
                norm_gpsimd(core, nc, pool, ns)
                with pool.Fori(0, GROUPS) as g:
                    pool.wait_ge(ns.ready, count(g + 1))
                    pool.wait_ge(gate_done, count(g))
                    nc.gpsimd.tensor_copy(xs[:, :], core.xnT[:, bass.ds(g * GT, GT)]).then_inc(staged, 1)
                    nc.gpsimd.tensor_copy(cs[:, :], core.ctxT[:, bass.ds(g * GT, GT)]).then_inc(staged, 1)
                pool.wait_ge(ones_set, count(1))
                pool.wait_ge(gate_done, count(GROUPS))
                with pool.Fori(0, GROUPS) as g:
                    pool.wait_ge(qk_done, count(g * NH))
                    nc.gpsimd.tensor_copy(xs[:, :], core.xnT[:, bass.ds(g * GT, GT)]).then_inc(staged, 1)
                    nc.gpsimd.tensor_copy(cs[:, :], core.ctxT[:, bass.ds(g * GT, GT)]).then_inc(staged, 1)
                    pool.wait_ge(pv_done, count(g))
                    nc.gpsimd.tensor_copy(va[:, :, 0:DH], core.ctx_tok[:, bass.ds(g * G, G), :].rearrange(
                        "p j (h e) -> p (j h) e", h=NH)).then_inc(va_ready, 1)
                    pool.wait_ge(m_loaded, g * 32 + 32)
                    pool.wait_ge(expo_ready, count(g))
                    nc.gpsimd.tensor_tensor(expo[:, 0, :, :], bcast(core.const("caus_t"), 1, N), m_b[:, :, :],
                                            ALU.subtract).then_inc(part_done, 1)
                    pool.wait_ge(var_ready, count(g + 1))
                    nc.gpsimd.tensor_tensor(mom[:, 3, :], mom[:, 2, :], core.half[:, 0:N], ALU.pow).then_inc(rstd_ready, 1)

            @block.tensor
            def _(pe):
                norm_tensor(core, nc, pe, ns, misc)
                pe.wait_ge(core.w_loaded[0], 16)
                with pe.Fori(0, GROUPS) as g:
                    pe.wait_ge(staged, count(g * 2 + 2))
                    pe.wait_ge(gates_ready, count(g))
                    for j in range(G):
                        for i, src in enumerate((xs, cs, cs)):
                            ins = nc.tensor.matmul(gbank[:, j * 8:j * 8 + 8], src[:, j * P:(j + 1) * P], wg[:, i, :],
                                                   start=(i == 0), stop=(i == 2))
                    ins.then_inc(gate_done, 1)
                pe.wait_ge(ns.ready, count(GROUPS))
                pe.wait_ge(gates_ready, count(GROUPS))
                pe.wait_ge(logf_ready, count(1))
                nc.tensor.matmul(gbank[:, 0:P], core.const("tri"), logf[:, :], start=True, stop=True).then_inc(sum_done, 1)
                pe.wait_ge(a_ready, count(1))
                nc.tensor.transpose(misc[:, 0:P], a[:, :], core.const("ident")).then_inc(a_turned, 1)
                pe.wait_ge(scan_done, count(2))
                nc.tensor.transpose(misc[:, 0:P], mT[:, :], core.const("ident")).then_inc(m_turned, 1)
                with pe.Fori(0, GROUPS) as g:
                    pe.wait_ge(staged, count(GROUPS * 2 + g * 2 + 2))
                    pe.wait_ge(cmat_ready, count(g * NH))
                    for h in range(NH):
                        r = slice(h * DH, (h + 1) * DH)
                        for t in range(G):
                            for b in range(2):
                                c = slice(t * P + b * SEQ, t * P + (b + 1) * SEQ)
                                ins = nc.tensor.matmul(score[h][b * SEQ:(b + 1) * SEQ, t * SEQ:(t + 1) * SEQ],
                                                       cs[r, c], xs[r, c], start=True, stop=True)
                        ins.then_inc(qk_done, 1)
                    pe.wait_ge(cmat_ready, count((g + 1) * NH))
                    pe.wait_ge(va_ready, count(g + 1))
                    pe.wait_ge(out_read, count(g * 2))
                    pe.sem_inc(may_pv, 1)
                    for t in range(G):
                        for h in range(NH):
                            n = t * NH + h
                            for b in range(2):
                                r = slice(b * SEQ, (b + 1) * SEQ)
                                ins = nc.tensor.matmul(po[t // 2][r, (n % 8) * (DH + 1):(n % 8 + 1) * (DH + 1)],
                                                       cmat[r, n, :], va[r, n, :], start=True, stop=True)
                    ins.then_inc(pv_done, 1)

            @block.scalar
            def _(act):
                norm_scalar(core, nc, act, ns, misc)
                act.wait_ge(gates_ready, count(GROUPS))
                fg = gates[:, :, NH:2 * NH]
                nc.scalar.activation(f[:, 0, :, :], fg, ACT.Abs).then_inc(abs_done, 1)
                act.wait_ge(abs_done, count(1))
                nc.scalar.activation(f[:, 1, :, :], f[:, 0, :, :], ACT.Exp, scale=-1.0).then_inc(exp_f_done, 1)
                act.wait_ge(exp_f_done, count(1))
                nc.scalar.activation(f[:, 2, :, :], f[:, 1, :, :], ACT.Ln, bias=1.0).then_inc(ln_done, 1)
                act.wait_ge(floor_in, count(1))
                nc.scalar.activation(floor[:, :], top[:, :], ACT.Exp, scale=-1.0).then_inc(floor_ready, 1)
                with act.Fori(0, GROUPS) as g:
                    act.wait_ge(expo_ready, count(g + 1))
                    act.wait_ge(cmat_ready, count(g * NH))
                    nc.scalar.activation(decay[:, :, :], expo[:, 1, :, :], ACT.Exp).then_inc(decay_ready, 1)
                    act.wait_ge(pv_done, count(g + 1))
                    act.wait_ge(out_read, count(g * 2))
                    for i in range(2):
                        ins = nc.scalar.activation(den[:, 0, i * 8:(i + 1) * 8],
                                                   po[i][:, 0:8 * (DH + 1)].rearrange("p (n e) -> p n e", n=8)[:, :, DH],
                                                   ACT.Abs)
                    ins.then_inc(abs_sum, 1)
                    act.wait_ge(cen_done, count(g + 1))
                    act.wait_ge(var_ready, count(g))
                    nc.scalar.activation(sq[:, :, :], cen[:, :, :], ACT.Square).then_inc(sq_done, 1)

            @block.vector
            def _(dve):
                norm_vector(core, nc, dve, ns)
                with dve.Fori(0, GROUPS) as g:
                    dve.wait_ge(gate_done, count(g + 1))
                    nc.vector.tensor_tensor(gates[:, bass.ds(g * G, G), :],
                                            gbank[:, 0:G * 8].rearrange("p (j n) -> p j n", j=G),
                                            bcast(core.row("l0_bias"), 1, G), ALU.add).then_inc(gates_ready, 1)
                flat = lambda t: t.rearrange("p n h -> p (n h)")
                dve.wait_ge(ln_done, count(1))
                nc.vector.scalar_tensor_tensor(logf[:, :].rearrange("p (n h) -> p n h", h=NH), gates[:, :, NH:2 * NH], 0.0,
                                               f[:, 2, :, :], ALU.min, ALU.subtract).then_inc(logf_ready, 1)
                ch = Chain(dve, chain, 0, 2)
                dve.wait_ge(sum_done, count(1))
                ch.link(nc.vector.tensor_copy(csum[:, :], gbank[:, 0:P]))
                nc.vector.tensor_tensor(a[:, :].rearrange("p (n h) -> p n h", h=NH), gates[:, :, 0:NH],
                                        csum[:, :].rearrange("p (n h) -> p n h", h=NH), ALU.subtract).then_inc(a_ready, 1)
                dve.wait_ge(a_turned, count(1))
                ch.link(nc.vector.tensor_copy(aT[:, :], misc[:, 0:P]))
                ch.done()
                for b in range(2):
                    r = slice(b * SEQ, (b + 1) * SEQ)
                    nc.vector.tensor_tensor_scan(mT[:, r], aT[:, r], aT[:, r], -3e38, ALU.max, ALU.max)\
                        .then_inc(scan_done, 1)
                dve.wait_ge(m_turned, count(1))
                nc.vector.tensor_tensor(top[:, :], misc[:, 0:P], csum[:, :], ALU.add).then_inc(floor_in, 1)
                dve.wait_ge(a_ready, count(1))
                dve.wait_ge(floor_ready, count(1))
                with dve.Fori(0, GROUPS) as g:
                    dve.wait_ge(part_done, count(g + 1))
                    dve.wait_ge(decay_ready, count(g))
                    nc.vector.tensor_tensor(expo[:, 1, :, :], expo[:, 0, :, :], bcast(a[:, bass.ds(g * N, N)], 2, SEQ),
                                            ALU.add).then_inc(expo_ready, 1)
                    dve.wait_ge(decay_ready, count(g + 1))
                    dve.wait_ge(pv_done, count(g))
                    for h in range(NH):
                        dve.wait_ge(qk_done, count(g * NH + h + 1))
                        at_h = lambda t: t[:, :, :].rearrange("p (t h) s -> p t h s", h=NH)[:, :, h, :]
                        nc.vector.tensor_tensor(at_h(cmat), score[h][:, 0:G * SEQ].rearrange("p (t s) -> p t s", t=G),
                                                at_h(decay), ALU.mult).then_inc(cmat_ready, 1)
                    ch = Chain(dve, tail, g * 9, 9)
                    dve.wait_ge(abs_sum, count(g + 1))
                    ch.link(nc.vector.tensor_tensor(den[:, 1, :], den[:, 0, :], floor[:, bass.ds(g * N, N)], ALU.max))
                    ch.link(nc.vector.tensor_scalar(den[:, 2, :], den[:, 1, :], 1e-6, None, ALU.add))
                    ch.link(nc.vector.reciprocal(den[:, 3, :], den[:, 2, :]))
                    for i in range(2):
                        nc.vector.tensor_tensor(hs[:, i * 8:(i + 1) * 8, :],
                                                po[i][:, 0:8 * (DH + 1)].rearrange("p (n e) -> p n e", n=8)[:, :, 0:DH],
                                                bcast(den[:, 3, i * 8:(i + 1) * 8], 2, DH), ALU.mult).then_inc(out_read, 1)
                    dve.wait_ge(out_read, count(g * 2 + 2))
                    ch.link(nc.vector.tensor_reduce(mom[:, 0, :], hs[:, :, :], AX.X, ALU.add))
                    ch.link(nc.vector.tensor_scalar(mom[:, 1, :], mom[:, 0, :], 1.0 / DH, None, ALU.mult))
                    nc.vector.tensor_tensor(cen[:, :, :], hs[:, :, :], bcast(mom[:, 1, :], 2, DH), ALU.subtract)\
                        .then_inc(cen_done, 1)
                    dve.wait_ge(sq_done, count(g + 1))
                    ch.link(nc.vector.tensor_reduce(mom[:, 0, :], sq[:, :, :], AX.X, ALU.add))
                    nc.vector.tensor_scalar(mom[:, 2, :], mom[:, 0, :], 1.0 / DH, 1e-6, ALU.mult, ALU.add)\
                        .then_inc(var_ready, 1)
                    dve.wait_ge(rstd_ready, count(g + 1))
                    ch.link(nc.vector.tensor_tensor(hn[:, 0, :, :], cen[:, :, :], bcast(mom[:, 3, :], 2, DH), ALU.mult))
                    per_tile = lambda t: t.rearrange("p (j h) e -> p j (h e)", j=G)
                    ch.link(nc.vector.tensor_tensor(per_tile(hn[:, 1, :, :]), per_tile(hn[:, 0, :, :]),
                                                    bcast(core.row("l0_norm"), 1, G), ALU.mult))
                    x_g = core.x[:, bass.ds(g * G, G), :]
                    ch.link(nc.vector.scalar_tensor_tensor(x_g, per_tile(hn[:, 1, :, :]), core.tanh_g[:, 0:1], x_g,
                                                           ALU.mult, ALU.add))
                    ch.done()


def l0_ffn(core, nc):
    H, HD, E = 8, 64, 8
    C = H // 2
    wq, wk, wg = core.w("l0_q"), core.w("l0_k"), core.w("l0_g")
    ve = core.w("l0_ve").rearrange("p (e n) -> p e n", e=E)
    oe = core.w("l0_oe").rearrange("p (e c n) -> p e c n", e=E, c=C)
    with ExitStack() as ctx:
        sb = lambda name, shape, dt=F32: core.sb(ctx, "l0f_" + name, shape, dt)
        ps = lambda name, shape=(P, 512), dt=F32: core.ps(ctx, "l0f_" + name, shape, dt)
        sem = core.counters(1)
        causal = sb("causal", [P, SEQ], BF16)
        spread = sb("spread", [H * E, C, E, P], BF16)
        xs = sb("xs", [P, GT])
        lg = sb("logits", [P, G * H, E])
        top = sb("top", [P, 3, G * H])
        eq = sb("eq", [P, G * H, E])
        oh = sb("oh", [P, G * H, E])
        oh_bf = sb("oh_bf", [P, G, P], BF16)
        ohT = sb("ohT", [H * E, GT], BF16)
        qT = sb("qT", [P, C, GT])
        kb = sb("kb", [P, G, 2, C, 2, SEQ])
        val = sb("val", [P, 2, H, HD])
        v2 = sb("v2", [P, 2, 2, C, 2, HD])
        diff = sb("diff", [P, H, SEQ])
        prob = sb("prob", [P, 2, H, SEQ])
        mx = sb("mx", [P, 2, H])
        tot = sb("tot", [P, 2, 2, H])
        probT = sb("probT", [P, C, P])
        og = sb("og", [P, H * HD])
        oT = sb("oT", [P, C, GT])
        z = sb("z", [P, 2, GT])
        yT = sb("yT", [P, GT])
        work = [ps(f"work{i}") for i in range(2)]
        score = [ps(f"score{i}") for i in range(2)]
        turn, po, acc, misc = ps("turn"), ps("po"), ps("acc"), ps("misc")
        oh_turn = misc[:, 256:512].bitcast(BF16)
        ns = NormSems(sem)
        setup_done, xs_ready, lg_done, chain = sem("setup_done"), sem("xs_ready"), sem("lg_done"), sem("chain")
        top_ready, tanh_done, oh_ready, oh_turned, ohT_ready = (sem("top_ready"), sem("tanh_done"), sem("oh_ready"),
                                                                sem("oh_turned"), sem("ohT_ready"))
        qk_done, qk_copied = sem("qk_done"), sem("qk_copied")
        ve_done, pick_done, v2_ready = sem("ve_done"), sem("pick_done"), sem("v2_ready")
        score_done, sub_done, exp_done, tot_done = sem("score_done"), sem("sub_done"), sem("exp_done"), sem("tot_done")
        p_turned, pT_ready, pv_done, og_ready = sem("p_turned"), sem("pT_ready"), sem("pv_done"), sem("og_ready")
        o_turned, oT_ready, m_done, z_done = sem("o_turned"), sem("oT_ready"), sem("m_done"), sem("z_done")
        acc_done, y_ready, y_turned, res_done = sem("acc_done"), sem("y_ready"), sem("y_turned"), sem("res_done")
        gated, may_pick = sem("gated"), sem("may_pick")

        with nc.Block() as block:
            @block.sync
            def _(sp):
                core.renew(sp, 2)

            @block.gpsimd
            def _(pool):
                nc.gpsimd.tensor_copy(causal[:, :], core.const("caus_n")).then_inc(setup_done, 1)
                for c in range(C):
                    for a in range(2):
                        h = 2 * c + a
                        nc.gpsimd.tensor_copy(spread[:, c, :, a * HD:(a + 1) * HD],
                                              bcast(core.const("ident", H * E)[:, h * E:(h + 1) * E], 2, HD))\
                            .then_inc(setup_done, 1)
                nc.gpsimd.memset(oh_bf[:, :, :], 0.0).then_inc(setup_done, 1)
                nc.gpsimd.memset(kb[:, :, :, :, :, :], 0.0).then_inc(setup_done, 1)
                nc.gpsimd.memset(v2[:, :, :, :, :, :], 0.0).then_inc(setup_done, 1)
                norm_gpsimd(core, nc, pool, ns)
                with pool.Fori(0, GROUPS) as g:
                    pool.wait_ge(ns.ready, count(g + 1))
                    pool.wait_ge(ve_done, count(g * G * E))
                    nc.gpsimd.tensor_copy(xs[:, :], core.xnT[:, bass.ds(g * GT, GT)]).then_inc(xs_ready, 1)

            @block.tensor
            def _(pe):
                norm_tensor(core, nc, pe, ns, misc)
                pe.wait_ge(core.w_loaded[1], 16)
                pe.wait_ge(setup_done, count(4 + H))
                pe.wait_ge(ns.ready, count(GROUPS))
                with pe.Fori(0, GROUPS) as g:
                    x_g = core.xnT[:, bass.ds(g * GT, GT)]
                    pe.wait_ge(xs_ready, count(g + 1))
                    pe.wait_ge(res_done, count(g))
                    for j in range(G):
                        ins = nc.tensor.matmul(misc[:, j * H * E:(j + 1) * H * E], xs[:, j * P:(j + 1) * P], wg,
                                               start=True, stop=True)
                    ins.then_inc(lg_done, 1)
                    pe.wait_ge(z_done, count(g * C * E))
                    for i in range(2 * C):
                        c = i % C
                        pe.wait_ge(qk_copied, count(g * 2 * C + max(i - 1, 0)))
                        nc.tensor.matmul(work[i % 2][:, :], (wq, wk)[i // C][:, c * P:(c + 1) * P], x_g,
                                         start=True, stop=True).then_inc(qk_done, 1)
                    pe.wait_ge(oh_ready, count(g + 1))
                    for j in range(G):
                        ins = nc.tensor.transpose(oh_turn[:, j * P:(j + 1) * P], oh_bf[:, j, :], core.ident_bf[:, :])
                    ins.then_inc(oh_turned, 1)
                    pe.wait_ge(qk_copied, count((g + 1) * 2 * C))

                    def expert_values(t):
                        for e in range(E):
                            n = t * E + e
                            pe.wait_ge(pick_done, count(g * G * E + max(n - 1, 0)))
                            nc.tensor.matmul(work[n % 2][:, :], xs[:, t * P:(t + 1) * P], ve[:, e, :],
                                             start=True, stop=True).then_inc(ve_done, 1)

                    def scores(t):
                        pe.wait_ge(sub_done, count(g * G + max(t - 1, 0)))
                        nc.tensor.matmul(score[t % 2][:, :], core.ident_bf[:, :], bcast(causal[:, :], 1, H),
                                         start=True, stop=False, skip_group_check=True)
                        for c in range(C):
                            for b in range(2):
                                ins = nc.tensor.matmul(score[t % 2][b * SEQ:(b + 1) * SEQ, c * P:(c + 1) * P],
                                                       qT[:, c, t * P + b * SEQ:t * P + (b + 1) * SEQ],
                                                       kb[:, t, b, c, :, :].rearrange("p a k -> p (a k)"),
                                                       start=False, stop=True, skip_group_check=True)
                        ins.then_inc(score_done, 1)

                    def values(t):
                        n = g * G + t
                        pe.wait_ge(exp_done, count(n + 1))
                        pe.wait_ge(oT_ready, count(n))
                        for c in range(C):
                            ins = nc.tensor.transpose(turn[:, c * P:(c + 1) * P],
                                                      prob[:, t % 2, 2 * c:2 * c + 2, :].rearrange("p a k -> p (a k)"),
                                                      core.const("ident"))
                        ins.then_inc(p_turned, 1)
                        pe.wait_ge(pT_ready, count(n + 1))
                        pe.wait_ge(og_ready, count(n))
                        pe.wait_ge(v2_ready, count(n * 4 + 4))
                        for c in range(C):
                            for b in range(2):
                                q = slice(b * SEQ, (b + 1) * SEQ)
                                ins = nc.tensor.matmul(po[q, c * P:(c + 1) * P], probT[:, c, q],
                                                       v2[:, t % 2, b, c, :, :].rearrange("p a e -> p (a e)"),
                                                       start=True, stop=True)
                        ins.then_inc(pv_done, 1)

                    def turn_out(t):
                        pe.wait_ge(og_ready, count(g * G + t + 1))
                        for c in range(C):
                            ins = nc.tensor.transpose(turn[:, c * P:(c + 1) * P], og[:, c * P:(c + 1) * P],
                                                      core.const("ident"))
                        ins.then_inc(o_turned, 1)

                    expert_values(0)
                    scores(0)
                    for t in range(G):
                        if t + 1 < G:
                            expert_values(t + 1)
                            scores(t + 1)
                        values(t)
                        turn_out(t)
                    pe.wait_ge(ohT_ready, count(g + 1))
                    pe.wait_ge(oT_ready, count(g * G + G))
                    pe.wait_ge(pick_done, count((g + 1) * G * E))
                    pe.wait_ge(y_ready, count(g))

                    def spread_mask(n):
                        pe.wait_ge(z_done, count(g * C * E + max(n - 1, 0)))
                        nc.tensor.matmul(work[n % 2][:, :], spread[:, n // E, n % E, :], ohT[:, :],
                                         start=True, stop=True).then_inc(m_done, 1)

                    spread_mask(0)
                    for n in range(C * E):
                        if n + 1 < C * E:
                            spread_mask(n + 1)
                        pe.wait_ge(z_done, count(g * C * E + n + 1))
                        nc.tensor.matmul(acc[:, :], oe[:, n % E, n // E, :], z[:, n % 2, :], start=(n == 0),
                                         stop=(n == C * E - 1)).then_inc(acc_done, 1)
                    pe.wait_ge(y_ready, count(g + 1))
                    residual_tensor(core, nc, pe, yT, misc, y_turned)

            @block.scalar
            def _(act):
                norm_scalar(core, nc, act, ns, misc)
                act.wait_ge(setup_done, count(4 + H))
                with act.Fori(0, GROUPS) as g:
                    act.wait_ge(score_done, count(g * G))
                    for i in range(C):
                        act.wait_ge(qk_done, count(g * 2 * C + i + 1))
                        nc.scalar.activation(qT[:, i, :], work[i % 2][:, :], ACT.Copy).then_inc(qk_copied, 1)
                    for c in range(C):
                        act.wait_ge(qk_done, count(g * 2 * C + C + c + 1))
                        for a in range(2):
                            r = slice(a * HD, (a + 1) * HD)
                            ins = nc.scalar.activation(kb[r, :, :, c, a, :],
                                                       work[c % 2][r, :].rearrange("p (t b k) -> p t b k", t=G, b=2),
                                                       ACT.Copy)
                        ins.then_inc(qk_copied, 1)
                    act.wait_ge(top_ready, count(g + 1))
                    nc.scalar.activation(top[:, 1, :], top[:, 0, :], ACT.Tanh, scale=0.5).then_inc(tanh_done, 1)
                    act.wait_ge(oh_turned, count(g + 1))
                    act.wait_ge(m_done, count(g * C * E))
                    nc.scalar.activation(ohT[:, :], oh_turn[0:H * E, :], ACT.Copy).then_inc(ohT_ready, 1)
                    act.wait_ge(acc_done, count(g * C * E))
                    for t in range(G):
                        n = g * G + t
                        act.wait_ge(sub_done, count(n + 1))
                        act.wait_ge(p_turned, count(g * G + max(t - 1, 0)))
                        act.wait_ge(tot_done, count(g * G + max(t - 1, 0)))
                        nc.scalar.activation(prob[:, t % 2, :, :], diff[:, :, :], ACT.Exp, scale=HD ** -0.5)\
                            .then_inc(exp_done, 1)
                        act.wait_ge(p_turned, count(n + 1))
                        act.wait_ge(pv_done, count(n))
                        nc.scalar.activation(probT[:, :, :], turn[:, :].rearrange("p (c q) -> p c q", c=C), ACT.Copy)\
                            .then_inc(pT_ready, 1)
                        act.wait_ge(o_turned, count(n + 1))
                        nc.scalar.activation(oT[:, :, t * P:(t + 1) * P], turn[:, :].rearrange("p (c q) -> p c q", c=C),
                                             ACT.Copy).then_inc(oT_ready, 1)
                    act.wait_ge(acc_done, count((g + 1) * C * E))
                    act.wait_ge(y_turned, count(g))
                    nc.scalar.activation(yT[:, :], acc[:, :], ACT.Copy).then_inc(y_ready, 1)

            @block.vector
            def _(dve):
                norm_vector(core, nc, dve, ns)
                dve.wait_ge(setup_done, count(4 + H))
                prio = bcast(core.const("prio"), 1, G * H)
                with dve.Fori(0, GROUPS) as g:
                    ch = Chain(dve, chain, g * 15, 15)
                    dve.wait_ge(lg_done, count(g + 1))
                    ch.link(nc.vector.tensor_scalar(lg[:, :, :], misc[:, 0:G * H * E].rearrange("p (n e) -> p n e", e=E),
                                                    17.4, -103.0, ALU.min, ALU.max))
                    nc.vector.tensor_reduce(top[:, 0, :], lg[:, :, :], AX.X, ALU.max).then_inc(top_ready, 1)
                    onehot_links(core, nc, ch, oh[:, :, :], lg[:, :, :], top[:, 2, :], eq[:, :, :], prio)
                    nc.vector.tensor_copy(oh_bf[:, :, 0:H * E], oh[:, :, :].rearrange("p (t h) e -> p t (h e)", t=G))\
                        .then_inc(oh_ready, 1)
                    dve.wait_ge(tanh_done, count(g + 1))
                    ch.link(nc.vector.tensor_scalar(top[:, 2, :], top[:, 1, :], 0.5, 0.5, ALU.mult, ALU.add))
                    gate = top[:, 2, :].rearrange("p (t h) -> p t h", t=G)

                    def pick(t):
                        for e in range(E):
                            n = g * G * E + t * E + e
                            dve.wait_ge(ve_done, count(n + 1))
                            w3 = work[(t * E + e) % 2][:, :].rearrange("p (h k) -> p h k", h=H)
                            if e == 0:
                                if t >= 2:
                                    dve.wait_ge(v2_ready, count((g * G + t - 1) * 4))
                                nc.vector.tensor_copy(val[:, t % 2, :, :], w3).then_inc(pick_done, 1)
                            else:
                                dve.wait_ge(pick_done, count(n))
                                dve.sem_inc(may_pick, 1)
                                m_e = bcast(oh[:, t * H:(t + 1) * H, e], 2, HD).bitcast(I32)
                                nc.vector.copy_predicated(val[:, t % 2, :, :], m_e, w3).then_inc(pick_done, 1)
                        dve.wait_ge(pick_done, count(g * G * E + (t + 1) * E))
                        dve.wait_ge(pv_done, count(g * G + max(t - 1, 0)))
                        for b in range(2):
                            for a in range(2):
                                r = slice(b * SEQ, (b + 1) * SEQ)
                                nc.vector.tensor_tensor(
                                    v2[a * SEQ:(a + 1) * SEQ, t % 2, b, :, a, :],
                                    val[r, t % 2, :, :].rearrange("p (c a) k -> p c a k", a=2)[:, :, a, :],
                                    bcast(gate[r, t, :].rearrange("p (c a) -> p c a", a=2)[:, :, a], 2, HD),
                                    ALU.mult).then_inc(v2_ready, 1)

                    def softmax(t):
                        n = g * G + t
                        s = score[t % 2][:, :].rearrange("p (h k) -> p h k", h=H)
                        dve.wait_ge(score_done, count(n + 1))
                        ch.link(nc.vector.tensor_reduce(mx[:, t % 2, :], s, AX.X, ALU.max))
                        dve.wait_ge(exp_done, count(n))
                        nc.vector.tensor_tensor(diff[:, :, :], s, bcast(mx[:, t % 2, :], 2, SEQ), ALU.subtract)\
                            .then_inc(sub_done, 1)

                    def normalise(t):
                        n = g * G + t
                        dve.wait_ge(exp_done, count(n + 1))
                        ch.link(nc.vector.tensor_reduce(tot[:, t % 2, 0, :], prob[:, t % 2, :, :], AX.X, ALU.add))
                        nc.vector.reciprocal(tot[:, t % 2, 1, :], tot[:, t % 2, 0, :]).then_inc(tot_done, 1)
                        dve.wait_ge(tot_done, count(n + 1))
                        nc.vector.tensor_tensor(tot[:, t % 2, 0, :], tot[:, t % 2, 1, :], gate[:, t, :], ALU.mult)\
                            .then_inc(gated, 1)
                        dve.wait_ge(gated, count(n + 1))
                        dve.wait_ge(pv_done, count(n + 1))
                        dve.wait_ge(o_turned, count(n))
                        nc.vector.tensor_tensor(og[:, :].rearrange("p (h e) -> p h e", h=H),
                                                po[:, :].rearrange("p (h e) -> p h e", h=H),
                                                bcast(tot[:, t % 2, 0, :], 2, HD), ALU.mult).then_inc(og_ready, 1)

                    pick(0)
                    softmax(0)
                    for t in range(G):
                        if t + 1 < G:
                            pick(t + 1)
                            softmax(t + 1)
                        normalise(t)
                    ch.done()
                    dve.wait_ge(oT_ready, count(g * G + G))
                    for n in range(C * E):
                        dve.wait_ge(m_done, count(g * C * E + n + 1))
                        dve.wait_ge(acc_done, count(g * C * E + max(n - 1, 0)))
                        nc.vector.tensor_tensor(z[:, n % 2, :], oT[:, n // E, :], work[n % 2][:, :], ALU.mult)\
                            .then_inc(z_done, 1)
                    dve.wait_ge(y_turned, count(g + 1))
                    residual_vector(core, nc, g, 1, misc, res_done)


def after(eng, sem, value):
    if not isinstance(value, int) or value > 0:
        eng.wait_ge(sem, count(value))


def l1_xattn(core, nc, d):
    H, HD = 16, 64
    C, W = H // 2, H * HD
    wq, wk, wv = core.w("l1_q"), core.w("l1_k"), core.w("l1_v")
    wo = core.w("l1_o").rearrange("p (c d) -> p c d", c=C)
    with ExitStack() as ctx:
        sb = lambda name, shape, dt=F32: core.sb(ctx, "l1x_" + name, shape, dt)
        ps = lambda name, shape=(P, 1024), dt=F32: core.ps(ctx, "l1x_" + name, shape, dt)
        sem = core.counters(2)
        lens_i = sb("lens_i", [P, TILES], I32)
        lens = sb("lens", [P, TILES])
        mask = sb("mask", [P, SEQ], BF16)
        xs, cs = sb("xs", [P, P]), sb("cs", [P, P])
        sq = sb("sq", [P, W])
        ms = sb("ms", [P, 4, H])
        rs = sb("rs", [P, 2, H])
        normed = sb("normed", [P, W])
        qT, kT = sb("qT", [P, C, P]), sb("kT", [P, C, P])
        v2 = sb("v2", [P, 2, C, 2, HD])
        diff = sb("diff", [P, 2, C, SEQ])
        prob = sb("prob", [P, C, 2, SEQ])
        mx = sb("mx", [P, 2, H])
        tot = sb("tot", [P, 4, H])
        probT = sb("probT", [P, C, P])
        og = sb("og", [P, W])
        oT = sb("oT", [P, C, P])
        proj, turn, score, po = ps("proj"), ps("turn"), ps("score"), ps("po")
        ns = NormSems(sem)
        lens_loaded, chain, xs_ready, mask_ready = core.sem("lens_loaded"), sem("chain"), sem("xs_ready"), sem("mask_ready")
        proj_done = [sem(f"proj_done{i}") for i in range(3)]
        sq_done = [sem(f"sq_done{i}") for i in range(2)]
        ms_ready = [sem(f"ms_ready{i}") for i in range(2)]
        rs_ready = [sem(f"rs_ready{i}") for i in range(2)]
        normed_ready = [sem(f"normed_ready{i}") for i in range(2)]
        qk_turned = [sem(f"qk_turned{i}") for i in range(2)]
        qkT_ready = [sem(f"qkT_ready{i}") for i in range(2)]
        v_ready = sem("v_ready")
        score_done, max_done, sub_done, exp_done = sem("score_done"), sem("max_done"), sem("sub_done"), sem("exp_done")
        tot_done, p_turned, pT_ready, pv_done = sem("tot_done"), sem("p_turned"), sem("pT_ready"), sem("pv_done")
        og_ready, o_turned, oT_ready, y_done, res_done = (sem("og_ready"), sem("o_turned"), sem("oT_ready"),
                                                          sem("y_done"), sem("res_done"))

        lens_ready, inv_done, v2_zero = sem("lens_ready"), sem("inv_done"), sem("v2_zero")
        sum_done = [sem(f"sum_done{i}") for i in range(2)]

        with nc.Block() as block:
            @block.sync
            def _(sp):
                core.renew(sp, 3)
                for b in range(2):
                    sp.dma_start(lens_i[b * SEQ:(b + 1) * SEQ, :],
                                 d["lens"][b:b + 1, :].broadcast_to([SEQ, TILES]))\
                        .then_inc(lens_loaded, 16)

            @block.gpsimd
            def _(pool):
                nc.gpsimd.memset(v2[:, :, :, :, :], 0.0).then_inc(v2_zero, 1)
                norm_gpsimd(core, nc, pool, ns)

                def stage(u):
                    pool.wait_ge(ns.ready, count(GROUPS))
                    after(pool, proj_done[2], u)
                    nc.gpsimd.tensor_copy(xs[:, :], core.xnT[:, bass.ds(u * P, P)]).then_inc(xs_ready, 1)
                    nc.gpsimd.tensor_copy(cs[:, :], core.ctxT[:, bass.ds(u * P, P)]).then_inc(xs_ready, 1)

                def inverse_rms(u):
                    for i in range(2):
                        pool.wait_ge(ms_ready[i], count(u + 1))
                        nc.gpsimd.tensor_tensor(rs[:, i, :], ms[:, 2 + i, :], core.half[:, 0:H], ALU.pow)\
                            .then_inc(rs_ready[i], 1)

                stage(0)
                inverse_rms(0)
                with pool.Fori(1, TILES) as u:
                    stage(u)
                    inverse_rms(u)

            @block.tensor
            def _(pe):
                norm_tensor(core, nc, pe, ns, po)
                pe.wait_ge(core.w_loaded[2], 16)
                pe.wait_ge(ns.ready, count(GROUPS))

                def project(u, i):
                    src, w = ((xs, wq), (cs, wk), (cs, wv))[i]
                    if i == 0:
                        pe.wait_ge(xs_ready, count(u * 2 + 2))
                        after(pe, v_ready, u * 4)
                    else:
                        pe.wait_ge(normed_ready[i - 1], count(u + 1))
                    for half in range(2):
                        ins = nc.tensor.matmul(proj[:, half * 512:(half + 1) * 512], src[:, :],
                                               w[:, half * 512:(half + 1) * 512], start=True, stop=True)
                    ins.then_inc(proj_done[i], 1)

                def turn_qk(u, i):
                    pe.wait_ge(normed_ready[i], count(u + 1))
                    if i == 0:
                        after(pe, pT_ready, u)
                    else:
                        pe.wait_ge(qkT_ready[0], count(u + 1))
                    for c in range(C):
                        ins = nc.tensor.transpose(turn[:, c * P:(c + 1) * P], normed[:, c * P:(c + 1) * P],
                                                  core.const("ident"))
                    ins.then_inc(qk_turned[i], 1)

                def scores(t):
                    pe.wait_ge(qkT_ready[0], count(t + 1))
                    pe.wait_ge(qkT_ready[1], count(t + 1))
                    pe.wait_ge(mask_ready, count(t + 1))
                    pe.wait_ge(res_done, count(t))
                    for half in range(2):
                        nc.tensor.matmul(score[:, half * 512:(half + 1) * 512], core.ident_bf[:, :],
                                         bcast(mask[:, :], 1, C), start=True, stop=False, skip_group_check=True)
                    for c in range(C):
                        for half in range(2):
                            r = slice(half * SEQ, (half + 1) * SEQ)
                            for b in range(2):
                                q = slice(b * SEQ, (b + 1) * SEQ)
                                ins = nc.tensor.matmul(score[q, half * 512 + c * SEQ:half * 512 + (c + 1) * SEQ],
                                                       qT[r, c, q], kT[r, c, q], start=False, stop=True,
                                                       skip_group_check=True)
                    ins.then_inc(score_done, 1)

                def turn_probs(t):
                    pe.wait_ge(exp_done, count(t + 1))
                    pe.wait_ge(oT_ready, count(t))
                    for c in range(C):
                        ins = nc.tensor.transpose(turn[:, c * P:(c + 1) * P],
                                                  prob[:, c, :, :].rearrange("p a k -> p (a k)"), core.const("ident"))
                    ins.then_inc(p_turned, 1)

                def values(t):
                    pe.wait_ge(pT_ready, count(t + 1))
                    pe.wait_ge(v_ready, count(t * 4 + 4))
                    pe.wait_ge(og_ready, count(t))
                    for c in range(C):
                        for b in range(2):
                            q = slice(b * SEQ, (b + 1) * SEQ)
                            ins = nc.tensor.matmul(po[q, c * P:(c + 1) * P], probT[:, c, q],
                                                   v2[:, b, c, :, :].rearrange("p a e -> p (a e)"), start=True, stop=True)
                    ins.then_inc(pv_done, 1)

                def turn_out(t):
                    pe.wait_ge(og_ready, count(t + 1))
                    for c in range(C):
                        ins = nc.tensor.transpose(turn[:, c * P:(c + 1) * P], og[:, c * P:(c + 1) * P],
                                                  core.const("ident"))
                    ins.then_inc(o_turned, 1)

                def project_out(t):
                    pe.wait_ge(oT_ready, count(t + 1))
                    for c in range(C):
                        ins = nc.tensor.matmul(score[:, 0:D], oT[:, c, :], wo[:, c, :], start=(c == 0), stop=(c == C - 1))
                    ins.then_inc(y_done, 1)

                project(0, 0)
                project(0, 1)
                turn_qk(0, 0)
                turn_qk(0, 1)
                project(0, 2)
                with pe.Fori(0, TILES - 1) as t:
                    scores(t)
                    project(t + 1, 0)
                    turn_probs(t)
                    project(t + 1, 1)
                    turn_qk(t + 1, 0)
                    values(t)
                    turn_qk(t + 1, 1)
                    project(t + 1, 2)
                    pe.wait_ge(qkT_ready[1], count(t + 2))
                    turn_out(t)
                    project_out(t)
                scores(TILES - 1)
                turn_probs(TILES - 1)
                values(TILES - 1)
                turn_out(TILES - 1)
                project_out(TILES - 1)

            @block.scalar
            def _(act):
                norm_scalar(core, nc, act, ns, po[:, 0:512])
                act.wait_ge(lens_loaded, 32)
                act.wait_ge(v2_zero, count(1))
                nc.scalar.activation(lens[:, :], lens_i[:, :], ACT.Copy).then_inc(lens_ready, 1)

                def square(u, i):
                    act.wait_ge(proj_done[i], count(u + 1))
                    after(act, ms_ready[1 - i], u + i)
                    nc.scalar.activation(sq[:, :], proj[:, :], ACT.Square).then_inc(sq_done[i], 1)

                def copy_qkT(u, i):
                    act.wait_ge(qk_turned[i], count(u + 1))
                    after(act, score_done, u)
                    nc.scalar.activation((qT, kT)[i][:, :, :], turn[:, :].rearrange("p (c q) -> p c q", c=C), ACT.Copy,
                                         scale=core.col(("l1_qw", "l1_kw")[i])).then_inc(qkT_ready[i], 1)

                def copy_v(u):
                    act.wait_ge(proj_done[2], count(u + 1))
                    after(act, pv_done, u)
                    for b in range(2):
                        for half in range(2):
                            nc.scalar.activation(v2[half * SEQ:(half + 1) * SEQ, b, :, half, :],
                                                 proj[b * SEQ:(b + 1) * SEQ, :].rearrange(
                                                     "p (c two e) -> p c two e", c=C, two=2)[:, :, half, :],
                                                 ACT.Copy).then_inc(v_ready, 1)

                def exp(t):
                    act.wait_ge(sub_done, count(t + 1))
                    act.wait_ge(p_turned, count(t))
                    act.wait_ge(tot_done, count(t))
                    nc.scalar.activation(prob[:, :, :, :].rearrange("p c a k -> p a c k"), diff[:, :, :, :], ACT.Exp,
                                         scale=HD ** -0.5).then_inc(exp_done, 1)

                def copy_pT(t):
                    act.wait_ge(p_turned, count(t + 1))
                    act.wait_ge(pv_done, count(t))
                    nc.scalar.activation(probT[:, :, :], turn[:, :].rearrange("p (c q) -> p c q", c=C), ACT.Copy)\
                        .then_inc(pT_ready, 1)

                def copy_oT(t):
                    act.wait_ge(o_turned, count(t + 1))
                    act.wait_ge(y_done, count(t))
                    nc.scalar.activation(oT[:, :, :], turn[:, :].rearrange("p (c q) -> p c q", c=C), ACT.Copy)\
                        .then_inc(oT_ready, 1)

                square(0, 0)
                square(0, 1)
                copy_qkT(0, 0)
                copy_qkT(0, 1)
                copy_v(0)
                with act.Fori(0, TILES - 1) as t:
                    exp(t)
                    square(t + 1, 0)
                    copy_pT(t)
                    square(t + 1, 1)
                    copy_qkT(t + 1, 0)
                    copy_qkT(t + 1, 1)
                    copy_v(t + 1)
                    copy_oT(t)
                exp(TILES - 1)
                copy_pT(TILES - 1)
                copy_oT(TILES - 1)

            @block.vector
            def _(dve):
                norm_vector(core, nc, dve, ns)
                dve.wait_ge(lens_ready, count(1))

                def key_mask(t):
                    after(dve, score_done, t)
                    nc.vector.tensor_scalar(mask[:, :], core.const("iota"), lens[:, bass.ds(t, 1)], NEG,
                                            ALU.is_ge, ALU.mult).then_inc(mask_ready, 1)

                def mean_square(u, i):
                    dve.wait_ge(sq_done[i], count(u + 1))
                    after(dve, rs_ready[i], u)
                    nc.vector.tensor_reduce(ms[:, i, :], sq[:, :].rearrange("p (h e) -> p h e", h=H), AX.X, ALU.add)\
                        .then_inc(sum_done[i], 1)
                    dve.wait_ge(sum_done[i], count(u + 1))
                    nc.vector.tensor_scalar(ms[:, 2 + i, :], ms[:, i, :], 1.0 / HD, 1e-5, ALU.mult, ALU.add)\
                        .then_inc(ms_ready[i], 1)

                def normalise_qk(u, i):
                    dve.wait_ge(rs_ready[i], count(u + 1))
                    after(dve, qk_turned[1 - i], u + i)
                    nc.vector.tensor_tensor(normed[:, :].rearrange("p (h e) -> p h e", h=H),
                                            proj[:, :].rearrange("p (h e) -> p h e", h=H),
                                            bcast(rs[:, i, :], 2, HD), ALU.mult).then_inc(normed_ready[i], 1)

                def softmax(t):
                    s = score[:, :].rearrange("p (h k) -> p h k", h=H)
                    dve.wait_ge(score_done, count(t + 1))
                    dve.wait_ge(sub_done, count(t))
                    nc.vector.tensor_reduce(mx[:, 0, :], s, AX.X, ALU.max).then_inc(max_done, 1)
                    dve.wait_ge(max_done, count(t + 1))
                    dve.wait_ge(exp_done, count(t))
                    nc.vector.tensor_tensor(diff[:, :, :, :].rearrange("p a c k -> p (a c) k"), s,
                                            bcast(mx[:, 0, :], 2, SEQ), ALU.subtract).then_inc(sub_done, 1)

                def totals(t):
                    dve.wait_ge(exp_done, count(t + 1))
                    dve.wait_ge(og_ready, count(t))
                    nc.vector.tensor_reduce(tot[:, 0, :], prob[:, :, :, :].rearrange("p c a k -> p (c a) k"), AX.X, ALU.add)\
                        .then_inc(tot_done, 1)
                    dve.wait_ge(tot_done, count(t + 1))
                    nc.vector.reciprocal(tot[:, 1, :], tot[:, 0, :]).then_inc(inv_done, 1)

                def scale_out(t):
                    dve.wait_ge(inv_done, count(t + 1))
                    dve.wait_ge(pv_done, count(t + 1))
                    dve.wait_ge(o_turned, count(t))
                    nc.vector.tensor_tensor(og[:, :].rearrange("p (h e) -> p h e", h=H),
                                            po[:, :].rearrange("p (h e) -> p h e", h=H),
                                            bcast(tot[:, 1, :], 2, HD), ALU.mult)\
                        .then_inc(og_ready, 1)

                def add_to_x(t):
                    dve.wait_ge(y_done, count(t + 1))
                    xt = core.x[:, bass.ds(t, 1), :].rearrange("p one d -> p (one d)")
                    nc.vector.scalar_tensor_tensor(xt, score[:, 0:D], core.tanh_g[:, 2:3], xt, ALU.mult, ALU.add)\
                        .then_inc(res_done, 1)

                key_mask(0)
                mean_square(0, 0)
                normalise_qk(0, 0)
                mean_square(0, 1)
                normalise_qk(0, 1)
                with dve.Fori(0, TILES - 1) as t:
                    softmax(t)
                    key_mask(t + 1)
                    mean_square(t + 1, 0)
                    normalise_qk(t + 1, 0)
                    totals(t)
                    mean_square(t + 1, 1)
                    normalise_qk(t + 1, 1)
                    scale_out(t)
                    add_to_x(t)
                softmax(TILES - 1)
                totals(TILES - 1)
                scale_out(TILES - 1)
                add_to_x(TILES - 1)


def l1_ffn(core, nc):
    E, H, R = 8, 32, 64
    B = GT // SEQ
    w_d1, w_base, w_dn = core.w("l1_d1"), core.w("l1_base"), core.w("l1_dn")
    w_d2 = core.w("l1_d2").rearrange("p (c d) -> p c d", c=2)
    w_up = core.w("l1_up").rearrange("p (c d) -> p c d", c=4)
    bd1, bd2, bdn, bup = core.col("l1_bd1"), core.col("l1_bd2"), core.col("l1_bdn"), core.col("l1_bup")
    with ExitStack() as ctx:
        sb = lambda name, shape, dt=F32: core.sb(ctx, "l1f_" + name, shape, dt)
        ps = lambda name, shape=(P, 512), dt=F32: core.ps(ctx, "l1f_" + name, shape, dt)
        sem = core.counters(3)
        ones = sb("ones", [P, P])
        h1 = sb("h1", [P, 2, GT])
        diff = sb("diff", [P, 2, GT])
        sq = sb("sq", [P, 2, GT])
        sums = sb("sums", [P, E, B])
        loss = sb("loss", [P, B, E])
        m = sb("m", [P, B])
        eq = sb("eq", [P, B, E])
        oh = sb("oh", [P, B, E])
        mask = sb("mask", [P, 4, B])
        bias = sb("bias", [P, 2, B])
        a = sb("a", [P, 4, GT])
        am = sb("am", [P, 4, GT])
        yT = sb("yT", [P, GT])
        ph = [ps(f"ph{i}") for i in range(2)]
        pr = [ps(f"pr{i}") for i in range(2)]
        pa = [ps(f"pa{i}") for i in range(2)]
        acc, misc = ps("acc"), ps("misc")
        ns = NormSems(sem)
        ones_ready, h1_done, h1_ready, recon_done = sem("ones_ready"), sem("h1_done"), sem("h1_ready"), sem("recon_done")
        diff_done, sq_done, red_done, loss_done = sem("diff_done"), sem("sq_done"), sem("red_done"), sem("loss_done")
        chain, mask_ready, a_done, a_ready = sem("chain"), sem("mask_ready"), sem("a_done"), sem("a_ready")
        am_ready, acc_done, y_ready, y_turned = sem("am_ready"), sem("acc_done"), sem("y_ready"), sem("y_turned")
        res_done, bias_ready = sem("res_done"), sem("bias_ready")

        with nc.Block() as block:
            @block.sync
            def _(sp):
                core.renew(sp, 4)

            @block.gpsimd
            def _(pool):
                nc.gpsimd.memset(ones[:, :], 1.0).then_inc(ones_ready, 1)
                norm_gpsimd(core, nc, pool, ns)
                with pool.Fori(0, GROUPS) as g:
                    pool.wait_ge(mask_ready, count(g * 2 + 2))
                    pool.wait_ge(acc_done, count(g))
                    for c in range(4):
                        pool.wait_ge(a_ready, count(g * 4 + c + 1))
                        nc.gpsimd.tensor_tensor(am[:, c, :].rearrange("p (b t) -> p b t", b=B),
                                                a[:, c, :].rearrange("p (b t) -> p b t", b=B),
                                                bcast(mask[:, c, :], 2, SEQ), ALU.mult).then_inc(am_ready, 1)

            @block.tensor
            def _(pe):
                norm_tensor(core, nc, pe, ns, misc)
                pe.wait_ge(core.w_loaded[3], 16)
                pe.wait_ge(ones_ready, count(1))
                pe.wait_ge(ns.ready, count(GROUPS))
                with pe.Fori(0, GROUPS) as g:
                    x_g = core.xnT[:, bass.ds(g * GT, GT)]
                    pe.wait_ge(h1_ready, count(g * 2))
                    for c in range(2):
                        nc.tensor.matmul(ph[c][:, :], w_d1[:, c * P:(c + 1) * P], x_g, start=True, stop=True)\
                            .then_inc(h1_done, 1)
                    for e in range(E):
                        r, c = H * (e % 4), e // 4
                        pe.wait_ge(h1_ready, count(g * 2 + c + 1))
                        pe.wait_ge(diff_done, count(g * E + max(e - 1, 0)))
                        nc.tensor.matmul(pr[e % 2][:, :], w_d2[r:r + H, c, :], h1[r:r + H, c, :],
                                         start=True, stop=True).then_inc(recon_done, 1)
                    for c in range(4):
                        pe.wait_ge(a_ready, count(g * 4 + max(c - 1, 0)))
                        nc.tensor.matmul(pa[c % 2][:, :], w_dn[:, c * P:(c + 1) * P], x_g, start=True, stop=True)\
                            .then_inc(a_done, 1)
                    pe.wait_ge(red_done, count(g * E + E))
                    pe.wait_ge(res_done, count(g))
                    nc.tensor.matmul(misc[:, 0:E * B], ones[:, :], sums[:, :, :].rearrange("p e b -> p (e b)"),
                                     start=True, stop=True).then_inc(loss_done, 1)
                    pe.wait_ge(y_ready, count(g))
                    nc.tensor.matmul(acc[:, :], w_base, x_g, start=True, stop=False)
                    for c in range(4):
                        pe.wait_ge(am_ready, count(g * 4 + c + 1))
                        ins = nc.tensor.matmul(acc[:, :], w_up[:, c, :], am[:, c, :], start=False, stop=(c == 3))
                    ins.then_inc(acc_done, 1)
                    pe.wait_ge(y_ready, count(g + 1))
                    residual_tensor(core, nc, pe, yT, misc, y_turned)

            @block.scalar
            def _(act):
                norm_scalar(core, nc, act, ns, misc)
                with act.Fori(0, GROUPS) as g:
                    act.wait_ge(recon_done, count(g * E))
                    for c in range(2):
                        act.wait_ge(h1_done, count(g * 2 + c + 1))
                        nc.scalar.activation(h1[:, c, :], ph[c][:, :], ACT.Relu, bias=bd1[:, c:c + 1])\
                            .then_inc(h1_ready, 1)
                    for e in range(E):
                        act.wait_ge(diff_done, count(g * E + e + 1))
                        act.wait_ge(red_done, count(g * E + max(e - 1, 0)))
                        nc.scalar.activation(sq[:, e % 2, :], diff[:, e % 2, :], ACT.Square).then_inc(sq_done, 1)
                    act.wait_ge(am_ready, count(g * 4))
                    for c in range(4):
                        act.wait_ge(a_done, count(g * 4 + c + 1))
                        nc.scalar.activation(a[:, c, :], pa[c % 2][:, :], ACT.Relu, bias=bdn[:, c:c + 1])\
                            .then_inc(a_ready, 1)

            @block.vector
            def _(dve):
                norm_vector(core, nc, dve, ns)
                with dve.Fori(0, GROUPS) as g:
                    x_g = core.xnT[:, bass.ds(g * GT, GT)]

                    def reduce(e):
                        dve.wait_ge(sq_done, count(g * E + e + 1))
                        nc.vector.tensor_reduce(sums[:, e, :], sq[:, e % 2, :].rearrange("p (b t) -> p b t", b=B),
                                                AX.X, ALU.add).then_inc(red_done, 1)

                    dve.wait_ge(loss_done, count(g))
                    for e in range(E):
                        dve.wait_ge(recon_done, count(g * E + e + 1))
                        dve.wait_ge(sq_done, count(g * E + max(e - 1, 0)))
                        nc.vector.scalar_tensor_tensor(diff[:, e % 2, :], pr[e % 2][:, :], bd2[:, e:e + 1], x_g,
                                                       ALU.add, ALU.subtract).then_inc(diff_done, 1)
                        if e:
                            reduce(e - 1)
                    reduce(E - 1)
                    ch = Chain(dve, chain, g * 8, 8)
                    dve.wait_ge(loss_done, count(g + 1))
                    ch.link(nc.vector.tensor_copy(loss[:, :, :], misc[:, 0:E * B].rearrange("p (e b) -> p b e", e=E)))
                    onehot_links(core, nc, ch, oh[:, :, :], loss[:, :, :], m[:, :], eq[:, :, :],
                                 bcast(core.const("prio"), 1, B), ALU.min)
                    dve.wait_ge(am_ready, count(g * 4))
                    nc.vector.tensor_copy(mask[0:R, :, :], oh[0:R, :, :].rearrange("p b (c q) -> p c b q", q=2)[:, :, :, 0])\
                        .then_inc(mask_ready, 1)
                    nc.vector.tensor_copy(mask[R:P, :, :], oh[R:P, :, :].rearrange("p b (c q) -> p c b q", q=2)[:, :, :, 1])\
                        .then_inc(mask_ready, 1)
                    ch.link(nc.vector.tensor_tensor(eq[:, :, :], oh[:, :, :], bcast(bup, 1, B), ALU.mult))
                    ch.link(nc.vector.tensor_reduce(bias[:, 0, :], eq[:, :, :], AX.X, ALU.add))
                    ch.done()
                    nc.vector.tensor_scalar(bias[:, 1, :], bias[:, 0, :], core.col("l1_bbase"), None, ALU.add)\
                        .then_inc(bias_ready, 1)
                    dve.wait_ge(bias_ready, count(g + 1))
                    dve.wait_ge(acc_done, count(g + 1))
                    dve.wait_ge(y_turned, count(g))
                    nc.vector.tensor_tensor(yT[:, :].rearrange("p (b t) -> p b t", b=B),
                                            acc[:, :].rearrange("p (b t) -> p b t", b=B),
                                            bcast(bias[:, 1, :], 2, SEQ), ALU.add).then_inc(y_ready, 1)
                    dve.wait_ge(y_turned, count(g + 1))
                    residual_vector(core, nc, g, 3, misc, res_done)


def narrow_attention(core, nc, d, k, own):
    H, HD = 16, 8
    C = H // 2
    SCALE = HD ** -0.5 if own else float(D) ** -0.5
    load = 4 if own else 6
    wo = core.w("l2_o") if own else core.w("l3_o")
    bo = core.col("l2_bo") if own else core.col("l3_bo")
    pre = f"a{k}_"
    with ExitStack() as ctx:
        sb = lambda name, shape, dt=F32: core.sb(ctx, pre + name, shape, dt)
        ps = lambda name, shape=(P, 512), dt=F32: core.ps(ctx, pre + name, shape, dt)
        sem = core.counters(k)
        qT = sb("qT", [P, GT])
        km = sb("km", [P, G, 2, 4, SEQ])
        v2 = sb("v2", [P, G, 2, C, 2 * HD])
        diff = sb("diff", [P, H, SEQ])
        prob = sb("prob", [P, 2, H, SEQ])
        mx = sb("mx", [P, 2, H])
        tot = sb("tot", [P, 2, 2, H])
        probT = sb("probT", [P, C, P])
        og = sb("og", [P, D])
        oT = sb("oT", [P, GT])
        yT = sb("yT", [P, GT])
        score = [ps(f"score{i}", (P, 1024)) for i in range(2)]
        pT = ps("pT", (P, 1024))
        po, misc = ps("po"), ps("misc")
        ns = NormSems(sem)
        v2_zero, chain = sem("v2_zero"), sem("chain")
        staged, q_ready, km_ready, v_ready = sem("staged"), sem("q_ready"), sem("km_ready"), sem("v_ready")
        score_done, sub_done, exp_done, tot_done = sem("score_done"), sem("sub_done"), sem("exp_done"), sem("tot_done")
        p_turned, pT_ready, pv_done, og_ready = sem("p_turned"), sem("pT_ready"), sem("pv_done"), sem("og_ready")
        o_turned, oT_ready, acc_done, y_ready = sem("o_turned"), sem("oT_ready"), sem("acc_done"), sem("y_ready")
        y_turned, res_done, strip_done = sem("y_turned"), sem("res_done"), sem("strip_done")
        if own:
            wq, wk, wv = core.w("l2_q"), core.w("l2_k"), core.w("l2_v")
            xs, cs = sb("xs", [P, GT]), sb("cs", [P, GT])
            qk = sb("qk", [P, 2, G, D])
            cosd = sb("cosd", [P, 2, G, D])
            sind = sb("sind", [P, 2, G, D])
            roped = sb("roped", [P, 2, G, D])
            proj_done, qk_ready, rope_ready, qk_turned = sem("proj_done"), sem("qk_ready"), sem("rope_ready"), sem("qk_turned")
            rchain = sem("rchain")
        else:
            mask_in = sb("mask_in", [P, TILES, SEQ], I32)
            mask_bf = sb("mask_bf", [P, G, SEQ], BF16)
            mask_loaded, mask_ready = core.sem("mask_loaded"), sem("mask_ready")

        with nc.Block() as block:
            @block.sync
            def _(sp):
                core.renew(sp, k + 1)
                if not own:
                    sp.dma_start(mask_in[:, :, :], d["mask"].rearrange("(n p) k -> p n k", p=P)).then_inc(mask_loaded, 16)

            @block.gpsimd
            def _(pool):
                nc.gpsimd.memset(v2[:, :, :, :, :], 0.0).then_inc(v2_zero, 1)
                norm_gpsimd(core, nc, pool, ns)
                if own:
                    with pool.Fori(0, GROUPS) as g:
                        pool.wait_ge(ns.ready, count(g + 1))
                        pool.wait_ge(proj_done, count(g * 3))
                        nc.gpsimd.tensor_copy(xs[:, :], core.xnT[:, bass.ds(g * GT, GT)]).then_inc(staged, 1)
                        nc.gpsimd.tensor_copy(cs[:, :], core.ctxT[:, bass.ds(g * GT, GT)]).then_inc(staged, 1)
                        ch = Chain(pool, rchain, g * 6, 6)
                        for i in range(2):
                            pool.wait_ge(qk_ready, count(g * 2 + i + 1))
                            pool.wait_ge(qk_turned, count(g * 2))
                            even = lambda t: t.rearrange("p j (n two) -> p j n two", two=2)[:, :, :, 0]
                            odd = lambda t: t.rearrange("p j (n two) -> p j n two", two=2)[:, :, :, 1]
                            cos, sin = bcast(core.const("rope_c"), 1, G), bcast(core.const("rope_s"), 1, G)
                            x_i, s_i = qk[:, i, :, :], sind[:, i, :, :]
                            ch.link(nc.gpsimd.tensor_tensor(cosd[:, i, :, :], x_i, cos, ALU.mult))
                            ch.link(nc.gpsimd.tensor_tensor(even(s_i), odd(x_i), even(sin), ALU.mult))
                            ch.link(nc.gpsimd.tensor_tensor(odd(s_i), even(x_i), odd(sin), ALU.mult))
                            nc.gpsimd.tensor_tensor(roped[:, i, :, :], cosd[:, i, :, :], s_i, ALU.add)\
                                .then_inc(rope_ready, 1)
                        ch.done()

            @block.tensor
            def _(pe):
                norm_tensor(core, nc, pe, ns, misc)
                pe.wait_ge(core.w_loaded[load], 16)
                pe.wait_ge(ns.ready, count(GROUPS))
                with pe.Fori(0, GROUPS) as g:
                    if own:
                        pe.wait_ge(staged, count(g * 2 + 2))
                        pe.wait_ge(sub_done, count(g * G))
                        for i, (src, w) in enumerate(((xs, wq), (cs, wk), (cs, wv))):
                            for j in range(G):
                                ins = nc.tensor.matmul(score[i // 2][:, (i % 2) * 512 + j * P:(i % 2) * 512 + (j + 1) * P],
                                                       src[:, j * P:(j + 1) * P], w, start=True, stop=True)
                            ins.then_inc(proj_done, 1)
                        for i in range(2):
                            pe.wait_ge(rope_ready, count(g * 2 + i + 1))
                            for j in range(G):
                                ins = nc.tensor.transpose(score[0][:, i * 512 + j * P:i * 512 + (j + 1) * P],
                                                          roped[:, i, j, :], core.const("ident"))
                            ins.then_inc(qk_turned, 1)
                    pe.wait_ge(q_ready, count(g + 1))
                    pe.wait_ge(km_ready, count(g * 4 + 4))
                    if not own:
                        pe.wait_ge(mask_ready, count(g + 1))

                    def scores(t):
                        s = score[t % 2]
                        pe.wait_ge(sub_done, count(g * G + max(t - 1, 0)))
                        if own and t == 1:
                            pe.wait_ge(v_ready, count(g * 4 + 4))
                        if not own:
                            for half in range(2):
                                nc.tensor.matmul(s[:, half * 512:(half + 1) * 512], core.ident_bf[:, :],
                                                 bcast(mask_bf[:, t, :], 1, C), start=True, stop=False,
                                                 skip_group_check=True)
                        for strip in (0, 2, 1, 3):
                            if strip == 1:
                                ins.then_inc(strip_done, 1)
                                pe.wait_ge(strip_done, count(g * G + t + 1))
                            for b in range(2):
                                r = 32 * strip
                                ins = nc.tensor.matmul(
                                    s[b * SEQ:(b + 1) * SEQ, strip * 256:(strip + 1) * 256],
                                    qT[r:r + 32, t * P + b * SEQ:t * P + (b + 1) * SEQ],
                                    km[r:r + 32, t, b, :, :].rearrange("p a k -> p (a k)"),
                                    start=own, stop=True, skip_group_check=True)
                        ins.then_inc(score_done, 1)

                    def values(t):
                        n = g * G + t
                        pe.wait_ge(exp_done, count(n + 1))
                        pe.wait_ge(pT_ready, count(n))
                        for c in range(C):
                            ins = nc.tensor.transpose(pT[:, c * P:(c + 1) * P],
                                                      prob[:, t % 2, 2 * c:2 * c + 2, :].rearrange("p a k -> p (a k)"),
                                                      core.const("ident"))
                        ins.then_inc(p_turned, 1)
                        pe.wait_ge(pT_ready, count(n + 1))
                        pe.wait_ge(og_ready, count(n))
                        if t == 0:
                            pe.wait_ge(v_ready, count(g * 4 + 4))
                        for b in range(2):
                            for c in range(C):
                                ins = nc.tensor.matmul(po[b * SEQ:(b + 1) * SEQ, c * 2 * HD:(c + 1) * 2 * HD],
                                                       probT[:, c, b * SEQ:(b + 1) * SEQ], v2[:, t, b, c, :],
                                                       start=True, stop=True)
                        ins.then_inc(pv_done, 1)

                    def outputs(t):
                        pe.wait_ge(og_ready, count(g * G + t + 1))
                        if t == 0:
                            pe.wait_ge(res_done, count(g))
                        else:
                            pe.wait_ge(oT_ready, count(g * G + t))
                        nc.tensor.transpose(misc[:, t * P:(t + 1) * P], og[:, :], core.const("ident"))\
                            .then_inc(o_turned, 1)

                    scores(0)
                    for t in range(G):
                        if t + 1 < G:
                            scores(t + 1)
                        values(t)
                        outputs(t)
                    pe.wait_ge(oT_ready, count(g * G + G))
                    nc.tensor.matmul(po[:, :], wo, oT[:, :], start=True, stop=True).then_inc(acc_done, 1)
                    pe.wait_ge(y_ready, count(g + 1))
                    residual_tensor(core, nc, pe, yT, misc, y_turned)

            @block.scalar
            def _(act):
                norm_scalar(core, nc, act, ns, misc)
                with act.Fori(0, GROUPS) as g:
                    act.wait_ge(score_done, count(g * G))
                    if own:
                        act.wait_ge(qk_turned, count(g * 2 + 1))
                        act.wait_ge(qk_turned, count(g * 2 + 2))
                        nc.scalar.activation(qT[:, :], score[0][:, 0:512], ACT.Copy).then_inc(q_ready, 1)
                        keys = score[0][:, 512:1024]
                    else:
                        act.wait_ge(ns.ready, count(g + 1))
                        nc.scalar.activation(qT[:, :], core.xnT[:, bass.ds(g * GT, GT)], ACT.Copy).then_inc(q_ready, 1)
                        keys = core.ctxT[:, bass.ds(g * GT, GT)]
                    for a in range(4):
                        nc.scalar.activation(km[:, :, :, a, :], keys.rearrange("p (t b k) -> p t b k", t=G, b=2),
                                             ACT.Copy, scale=core.const("hm")[:, a:a + 1]).then_inc(km_ready, 1)
                    for t in range(G):
                        n = g * G + t
                        act.wait_ge(sub_done, count(n + 1))
                        act.wait_ge(p_turned, count(g * G + max(t - 1, 0)))
                        act.wait_ge(tot_done, count(g * G + max(t - 1, 0)))
                        nc.scalar.activation(prob[:, t % 2, :, :], diff[:, :, :], ACT.Exp, scale=SCALE)\
                            .then_inc(exp_done, 1)
                        act.wait_ge(p_turned, count(n + 1))
                        act.wait_ge(pv_done, count(n))
                        nc.scalar.activation(probT[:, :, :], pT[:, :].rearrange("p (c q) -> p c q", c=C), ACT.Copy)\
                            .then_inc(pT_ready, 1)
                        act.wait_ge(o_turned, count(n + 1))
                        nc.scalar.activation(oT[:, t * P:(t + 1) * P], misc[:, t * P:(t + 1) * P], ACT.Copy)\
                            .then_inc(oT_ready, 1)
                    act.wait_ge(acc_done, count(g + 1))
                    nc.scalar.activation(yT[:, :], po[:, :], ACT.Identity, bias=bo).then_inc(y_ready, 1)

            @block.vector
            def _(dve):
                dve.wait_ge(v2_zero, count(1))
                norm_vector(core, nc, dve, ns)
                if not own:
                    dve.wait_ge(mask_loaded, 16)
                with dve.Fori(0, GROUPS) as g:
                    if own:
                        for i, (w, bias) in enumerate((("q", "l2_bq"), ("k", "l2_bk"))):
                            dve.wait_ge(proj_done, count(g * 3 + i + 1))
                            dve.wait_ge(rope_ready, count(g * 2))
                            nc.vector.tensor_tensor(qk[:, i, :, :], score[0][:, i * 512:(i + 1) * 512].rearrange(
                                "p (j n) -> p j n", j=G), bcast(core.row(bias), 1, G), ALU.add).then_inc(qk_ready, 1)
                        dve.wait_ge(proj_done, count(g * 3 + 3))
                    else:
                        dve.wait_ge(score_done, count(g * G))
                        nc.vector.tensor_scalar(mask_bf[:, :, :], mask_in[:, bass.ds(g * G, G), :], 0, NEG,
                                                ALU.is_equal, ALU.mult).then_inc(mask_ready, 1)
                    dve.wait_ge(pv_done, count(g * G))
                    for b in range(2):
                        half = slice(b * SEQ, (b + 1) * SEQ)
                        for q in range(2):
                            dst = v2[q * SEQ:(q + 1) * SEQ, :, b, :, q * HD:(q + 1) * HD]
                            if own:
                                src = score[1][half, 0:512].rearrange("p (j c q e) -> p j c q e", j=G, c=C, q=2)[:, :, :, q, :]
                                bias = bcast(core.row("l2_bv")[half, :].rearrange("p (c q e) -> p c q e", c=C, q=2)
                                             [:, :, q, :], 1, G)
                                nc.vector.tensor_tensor(dst, src, bias, ALU.add).then_inc(v_ready, 1)
                            else:
                                src = core.ctx_tok[half, bass.ds(g * G, G), :].rearrange(
                                    "p j (c q e) -> p j c q e", c=C, q=2)[:, :, :, q, :]
                                nc.vector.tensor_copy(dst, src).then_inc(v_ready, 1)
                    ch = Chain(dve, chain, g * G * 2, G * 2)

                    def softmax(t):
                        n = g * G + t
                        s = score[t % 2][:, :].rearrange("p (h k) -> p h k", h=H)
                        dve.wait_ge(score_done, count(n + 1))
                        ch.link(nc.vector.tensor_reduce(mx[:, t % 2, :], s, AX.X, ALU.max))
                        dve.wait_ge(exp_done, count(n))
                        nc.vector.tensor_tensor(diff[:, :, :], s, bcast(mx[:, t % 2, :], 2, SEQ), ALU.subtract)\
                            .then_inc(sub_done, 1)

                    def normalise(t):
                        n = g * G + t
                        dve.wait_ge(exp_done, count(n + 1))
                        ch.link(nc.vector.tensor_reduce(tot[:, t % 2, 0, :], prob[:, t % 2, :, :], AX.X, ALU.add))
                        nc.vector.reciprocal(tot[:, t % 2, 1, :], tot[:, t % 2, 0, :]).then_inc(tot_done, 1)
                        dve.wait_ge(tot_done, count(n + 1))
                        dve.wait_ge(pv_done, count(n + 1))
                        dve.wait_ge(o_turned, count(n))
                        nc.vector.tensor_tensor(og[:, :].rearrange("p (h e) -> p h e", h=H),
                                                po[:, 0:D].rearrange("p (h e) -> p h e", h=H),
                                                bcast(tot[:, t % 2, 1, :], 2, HD), ALU.mult).then_inc(og_ready, 1)

                    softmax(0)
                    for t in range(G):
                        if t + 1 < G:
                            softmax(t + 1)
                        normalise(t)
                    ch.done()
                    dve.wait_ge(y_turned, count(g + 1))
                    residual_vector(core, nc, g, k, misc, res_done)


def l2_ffn(core, nc, d):
    E, I = 8, 176
    CH = -(-(E + 1) * I // P)
    wg, wu, wd, gw = core.w("l2_wg"), core.w("l2_wu"), core.w("l2_wd"), core.w("l2_gw")
    with ExitStack() as ctx:
        sb = lambda name, shape, dt=F32: core.sb(ctx, "l2f_" + name, shape, dt)
        ps = lambda name, shape=(P, 512), dt=F32: core.ps(ctx, "l2f_" + name, shape, dt)
        sem = core.counters(5)
        xs = sb("xs", [P, GT])
        sel_bf = sb("sel_bf", [3 * (E + 1), CH * P], BF16)
        lg = sb("logits", [P, G, E + 1])
        oh = sb("onehots", [P, 2, G, E])
        eq = sb("eq", [P, G, E])
        l2 = sb("second", [P, G, E])
        m = sb("m", [P, 4, G])
        th = sb("th", [P, 2, G])
        comb = sb("comb", [P, G, E + 1])
        parts = sb("parts", [P, G, 3, E + 1], BF16)
        rest = sb("rest", [P, G, E + 1])
        combT = sb("combT", [3 * (E + 1), GT], BF16)
        work = sb("work", [P, 6, GT])
        act_g, hu, hid = work[:, 0:2, :], work[:, 2:4, :], work[:, 4:6, :]
        sel_in = work[0:3 * (E + 1), :, :].rearrange("p a t -> p (a t)")[:, 0:CH * P]
        yT = sb("yT", [P, GT])
        pg = [ps(f"pg{i}") for i in range(2)]
        pu = [ps(f"pu{i}") for i in range(2)]
        pc = [ps(f"pc{i}") for i in range(2)]
        acc = ps("acc")
        misc = ps("misc")
        pl = misc[:, 0:64].rearrange("p (j e) -> p j e", j=G)
        pct = misc[0:3 * (E + 1), 64:64 + GT // 2].bitcast(BF16)
        ns = NormSems(sem)
        xs_ready, lg_done, chain, w_in, th_done = sem("xs_ready"), sem("lg_done"), sem("chain"), sem("w_in"), sem("th_done")
        comb_split, comb_turned, comb_ready = sem("comb_split"), sem("comb_turned"), sem("comb_ready")
        gu_done, silu_done, h_done, acc_done = sem("gu_done"), sem("silu_done"), sem("h_done"), sem("acc_done")
        y_ready, y_turned, res_done, sel_ready = sem("y_ready"), sem("y_turned"), sem("res_done"), sem("sel_ready")
        hchain, silu_used = sem("hchain"), sem("silu_used")

        sel_loaded = core.sem("sel_loaded")

        with nc.Block() as block:
            @block.sync
            def _(sp):
                core.renew(sp, 6)
                sp.dma_start(sel_in, d["sel"]).then_inc(sel_loaded, 16)

            @block.gpsimd
            def _(pool):
                pool.wait_ge(sel_loaded, 16)
                nc.gpsimd.tensor_copy(sel_bf[:, :], sel_in).then_inc(sel_ready, 1)
                norm_gpsimd(core, nc, pool, ns)
                with pool.Fori(0, GROUPS) as g:
                    pool.wait_ge(ns.ready, count(g + 1))
                    pool.wait_ge(lg_done, count(g))
                    nc.gpsimd.tensor_copy(xs[:, :], core.xnT[:, bass.ds(g * GT, GT)]).then_inc(xs_ready, 1)

            @block.tensor
            def _(pe):
                norm_tensor(core, nc, pe, ns, misc)
                pe.wait_ge(core.w_loaded[5], 16)
                pe.wait_ge(sel_ready, count(1))
                pe.wait_ge(ns.ready, count(GROUPS))

                def up(g, c):
                    pe.wait_ge(h_done, count(g * CH + max(c - 1, 0)))
                    x_g = core.xnT[:, bass.ds(g * GT, GT)]
                    nc.tensor.matmul(pg[c % 2][:, :], wg[:, c * P:(c + 1) * P], x_g, start=True, stop=True)
                    nc.tensor.matmul(pu[c % 2][:, :], wu[:, c * P:(c + 1) * P], x_g, start=True, stop=True)
                    if c == 0:
                        pe.wait_ge(comb_ready, count(g + 1))
                    nc.tensor.matmul(pc[c % 2][:, :], sel_bf[:, c * P:(c + 1) * P], combT[:, :],
                                     start=True, stop=True).then_inc(gu_done, 1)

                def down(g, c):
                    pe.wait_ge(h_done, count(g * CH + c + 1))
                    ins = nc.tensor.matmul(acc[:, :], wd[:, c * P:(c + 1) * P], hid[:, c % 2, :],
                                           start=(c == 0), stop=(c == CH - 1))
                    ins.then_inc(acc_done, 1)

                with pe.Fori(0, GROUPS) as g:
                    pe.wait_ge(xs_ready, count(g + 1))
                    pe.wait_ge(res_done, count(g))
                    for j in range(G):
                        ins = nc.tensor.matmul(pl[:, j, 0:E + 1], xs[:, j * P:(j + 1) * P], gw, start=True, stop=True)
                    ins.then_inc(lg_done, 1)
                    pe.wait_ge(comb_split, count(g + 1))
                    for j in range(G):
                        ins = nc.tensor.transpose(pct[:, j * P:(j + 1) * P],
                                                  parts[:, j, :, :].rearrange("p a e -> p (a e)"), core.ident_bf[:, :])
                    ins.then_inc(comb_turned, 1)
                    up(g, 0)
                    for c in range(1, CH):
                        up(g, c)
                        down(g, c - 1)
                    down(g, CH - 1)
                    pe.wait_ge(y_ready, count(g + 1))
                    residual_tensor(core, nc, pe, yT, misc, y_turned)

            @block.scalar
            def _(act):
                norm_scalar(core, nc, act, ns, misc)
                act.wait_ge(sel_ready, count(1))
                with act.Fori(0, GROUPS) as g:
                    act.wait_ge(w_in, count(g + 1))
                    nc.scalar.activation(th[:, :, :], m[:, 0:2, :], ACT.Tanh, scale=0.5).then_inc(th_done, 1)
                    act.wait_ge(comb_turned, count(g + 1))
                    nc.scalar.activation(combT[:, :], pct[:, :], ACT.Copy).then_inc(comb_ready, 1)
                    for c in range(CH):
                        act.wait_ge(gu_done, count(g * CH + c + 1))
                        nc.scalar.activation(act_g[:, c % 2, :], pg[c % 2][:, :], ACT.Silu).then_inc(silu_done, 1)
                    act.wait_ge(acc_done, count((g + 1) * CH))
                    act.wait_ge(y_turned, count(g))
                    nc.scalar.activation(yT[:, :], acc[:, :], ACT.Copy).then_inc(y_ready, 1)

            @block.vector
            def _(dve):
                norm_vector(core, nc, dve, ns)
                prio = bcast(core.const("prio"), 1, G)
                with dve.Fori(0, GROUPS) as g:
                    ch = Chain(dve, chain, g * 21, 21)
                    dve.wait_ge(lg_done, count(g + 1))
                    ch.link(nc.vector.tensor_copy(lg[:, :, :], pl[:, :, 0:E + 1]))
                    onehot_links(core, nc, ch, oh[:, 0, :, :], lg[:, :, 0:E], m[:, 2, :], eq[:, :, :], prio)
                    ch.link(nc.vector.scalar_tensor_tensor(l2[:, :, :], oh[:, 0, :, :], NEG, lg[:, :, 0:E],
                                                           ALU.mult, ALU.add))
                    onehot_links(core, nc, ch, oh[:, 1, :, :], l2[:, :, :], m[:, 3, :], eq[:, :, :], prio)
                    ch.link(nc.vector.tensor_reduce(m[:, 2, :], lg[:, :, 0:E], AX.X, ALU.max))
                    ch.link(nc.vector.tensor_reduce(m[:, 3, :], l2[:, :, :], AX.X, ALU.max))
                    ch.link(nc.vector.tensor_copy(m[:, 1, :], lg[:, :, E]))
                    nc.vector.tensor_tensor(m[:, 0, :], m[:, 2, :], m[:, 3, :], ALU.subtract).then_inc(w_in, 1)
                    dve.wait_ge(th_done, count(g + 1))
                    ch.link(nc.vector.tensor_scalar(m[:, 2, :], th[:, 0, :], 0.5, 0.5, ALU.mult, ALU.add))
                    ch.link(nc.vector.tensor_scalar(m[:, 3, :], th[:, 0, :], -0.5, 0.5, ALU.mult, ALU.add))
                    ch.link(nc.vector.tensor_scalar(comb[:, :, E], th[:, 1, :], 0.5, 0.5, ALU.mult, ALU.add))
                    ch.link(nc.vector.tensor_tensor(oh[:, 0, :, :], oh[:, 0, :, :], bcast(m[:, 2, :], 2, E), ALU.mult))
                    ch.link(nc.vector.tensor_tensor(oh[:, 1, :, :], oh[:, 1, :, :], bcast(m[:, 3, :], 2, E), ALU.mult))
                    ch.link(nc.vector.tensor_tensor(comb[:, :, 0:E], oh[:, 0, :, :], oh[:, 1, :, :], ALU.add))
                    ch.done()
                    ch2 = Chain(dve, hchain, g * 4, 4)
                    ch2.link(nc.vector.tensor_copy(parts[:, :, 0, :], comb[:, :, :]))
                    ch2.link(nc.vector.tensor_tensor(rest[:, :, :], comb[:, :, :], parts[:, :, 0, :], ALU.subtract))
                    ch2.link(nc.vector.tensor_copy(parts[:, :, 1, :], rest[:, :, :]))
                    ch2.link(nc.vector.tensor_tensor(comb[:, :, :], rest[:, :, :], parts[:, :, 1, :], ALU.subtract))
                    ch2.done()
                    nc.vector.tensor_copy(parts[:, :, 2, :], comb[:, :, :]).then_inc(comb_split, 1)
                    for c in range(CH):
                        n = g * 2 * CH + 2 * c
                        dve.wait_ge(silu_done, count(g * CH + c + 1))
                        nc.vector.tensor_tensor(hu[:, c % 2, :], act_g[:, c % 2, :], pu[c % 2][:, :], ALU.mult)\
                            .then_inc(silu_used, 1)
                        dve.wait_ge(silu_used, count(g * CH + c + 1))
                        dve.wait_ge(acc_done, count(g * CH + max(c - 1, 0)))
                        nc.vector.tensor_tensor(hid[:, c % 2, :], hu[:, c % 2, :], pc[c % 2][:, :], ALU.mult)\
                            .then_inc(h_done, 1)
                    dve.wait_ge(y_turned, count(g + 1))
                    residual_vector(core, nc, g, 5, misc, res_done)


def l3_ffn(core, nc, out):
    I, CH = 352, 3
    QMAX = 127.0
    MAGIC = 1.5 * 2.0 ** 23
    wgu = [core.w("l3_g").rearrange("p (c d) -> p c d", c=CH), core.w("l3_u").rearrange("p (c d) -> p c d", c=CH)]
    wd = core.w("l3_d")
    clips = core.row("clips")
    with ExitStack() as ctx:
        sb = lambda name, shape, dt=F32: core.sb(ctx, "l3f_" + name, shape, dt)
        ps = lambda name, shape=(P, 512), dt=F32: core.ps(ctx, "l3f_" + name, shape, dt)
        sem = core.counters(7)
        ones = sb("ones", [1, P])
        magic = sb("magic", [P, 2])
        wsc = sb("wsc", [P, 3, 8])
        wq = sb("wq", [P, 3, CH * P])
        wq_bf = sb("wq_bf", [P, 3, CH * P], BF16)
        wT = sb("wT", [P, 3, CH * P], BF16)
        sig = sb("sig", [P, 2])
        mx = sb("mx", [P, 8])
        rowmax = sb("rowmax", [1, 2])
        sc = sb("sc", [P, 24])
        part = sb("part", [P, CH])
        xq = sb("xq", [P, TILES * P], BF16)
        rnd = sb("rnd", [P, CH, GT])
        hq = sb("hq", [P, CH, GT], BF16)
        act_g = sb("act_g", [P, 2, GT])
        yT = sb("yT", [P, GT])
        prod = [core.ctx_tok[:, :, :].rearrange("p n d -> p (n d)"), core.ctxT[:, :], core.xnT[:, :]]
        pg = [ps(f"pg{i}") for i in range(2)]
        pu = [ps(f"pu{i}") for i in range(2)]
        acc, misc, small = ps("acc"), ps("misc"), ps("small")
        wbank = ps("wbank", (P, 1024), BF16)
        ns = NormSems(sem)
        chain, ready, wq_ready, wt_done, wT_ready = sem("chain"), sem("ready"), sem("wq_ready"), sem("wt_done"), sem("wT_ready")
        sig_ready, mx_ready, mx_turned, row_ready, mx_spread = (sem("sig_ready"), sem("mx_ready"), sem("mx_turned"),
                                                               sem("row_ready"), sem("mx_spread"))
        scales_ready = sem("scales_ready")
        x_scaled, x_clipped, xq_ready = sem("x_scaled"), sem("x_clipped"), sem("xq_ready")
        gu_done, silu_done, prod_done, part_done = sem("gu_done"), sem("silu_done"), sem("prod_done"), sem("part_done")
        h_scaled, h_part, hq_ready, acc_done = sem("h_scaled"), sem("h_part"), sem("hq_ready"), sem("acc_done")
        y_ready, y_turned, res_done, stored = sem("y_ready"), sem("y_turned"), sem("res_done"), sem("stored")
        consts_ready = sem("consts_ready")
        SX, RX, SH, RH, SG, SU, SY = 0, 1, 2, 3, 4, 8, 12

        def spread_max(dve, ch, k):
            dve.wait_ge(mx_turned, count(k + 1))
            nc.vector.tensor_reduce(rowmax[0:1, k:k + 1], misc[0:1, 0:P], AX.X, ALU.max).then_inc(row_ready, 1)
            dve.wait_ge(mx_spread, count(k + 1))
            ch.link(nc.vector.tensor_tensor(mx[:, 4 + k:5 + k], small[:, 0:1], sig[:, k:k + 1], ALU.mult))
            ch.link(nc.vector.tensor_scalar(sc[:, 2 * k:2 * k + 1], mx[:, 4 + k:5 + k], 1.0 / QMAX, None, ALU.mult))
            ch.link(nc.vector.reciprocal(sc[:, 2 * k + 1:2 * k + 2], sc[:, 2 * k:2 * k + 1]))

        def spread_max_tensor(pe, k):
            pe.wait_ge(mx_ready, count(k + 1))
            nc.tensor.transpose(misc[0:1, 0:P], mx[:, k:k + 1], core.const("ident")).then_inc(mx_turned, 1)
            pe.wait_ge(row_ready, count(k + 1))
            nc.tensor.matmul(small[:, 0:1], ones[:, :], rowmax[0:1, k:k + 1], start=True, stop=True)\
                .then_inc(mx_spread, 1)

        with nc.Block() as block:
            @block.gpsimd
            def _(pool):
                nc.gpsimd.memset(ones[:, :], 1.0).then_inc(consts_ready, 1)
                nc.gpsimd.memset(magic[:, 0:1], MAGIC).then_inc(consts_ready, 1)
                nc.gpsimd.memset(magic[:, 1:2], -MAGIC).then_inc(consts_ready, 1)
                nc.gpsimd.memset(wq_bf[:, 2, I:CH * P], 0.0).then_inc(consts_ready, 1)
                norm_gpsimd(core, nc, pool, ns)

            @block.tensor
            def _(pe):
                norm_tensor(core, nc, pe, ns, misc)
                pe.wait_ge(consts_ready, count(4))
                pe.wait_ge(wq_ready, count(3))
                for k in range(3):
                    for c in range(CH):
                        ins = nc.tensor.transpose(wbank[:, c * P:(c + 1) * P], wq_bf[:, k, c * P:(c + 1) * P],
                                                  core.ident_bf[:, :])
                    ins.then_inc(wt_done, 1)
                    pe.wait_ge(wT_ready, count(k + 1))
                pe.wait_ge(ns.ready, count(GROUPS))
                spread_max_tensor(pe, 0)
                with pe.Fori(0, GROUPS) as g:
                    x_g = xq[:, bass.ds(g * GT, GT)]
                    pe.wait_ge(xq_ready, count(g + 1))
                    for c in range(CH):
                        b = c % 2
                        pe.wait_ge(prod_done, count(g * CH + max(c - 1, 0)))
                        nc.tensor.matmul(pg[b][:, :], wT[:, 0, c * P:(c + 1) * P], x_g, start=True, stop=True)
                        nc.tensor.matmul(pu[b][:, :], wT[:, 1, c * P:(c + 1) * P], x_g, start=True, stop=True)\
                            .then_inc(gu_done, 1)
                spread_max_tensor(pe, 1)
                with pe.Fori(0, GROUPS) as g:
                    pe.wait_ge(hq_ready, count(g + 1))
                    pe.wait_ge(y_ready, count(g))
                    for c in range(CH):
                        ins = nc.tensor.matmul(acc[:, :], wT[:, 2, c * P:(c + 1) * P], hq[:, c, :],
                                               start=(c == 0), stop=(c == CH - 1))
                    ins.then_inc(acc_done, 1)
                    pe.wait_ge(y_ready, count(g + 1))
                    pe.wait_ge(res_done, count(g))
                    residual_tensor(core, nc, pe, yT, misc, y_turned)

            @block.scalar
            def _(act):
                norm_scalar(core, nc, act, ns, misc)
                act.wait_ge(consts_ready, count(4))
                nc.scalar.activation(sig[:, :], clips, ACT.Tanh, scale=0.5).then_inc(sig_ready, 1)
                for k in range(3):
                    act.wait_ge(wt_done, count(k + 1))
                    nc.scalar.activation(wT[:, k, :], wbank[:, 0:CH * P], ACT.Copy).then_inc(wT_ready, 1)
                act.wait_ge(scales_ready, count(1))
                with act.Fori(0, GROUPS) as g:
                    act.wait_ge(xq_ready, count(g))
                    nc.scalar.activation(rnd[:, 0, :], core.xnT[:, bass.ds(g * GT, GT)], ACT.Identity,
                                         bias=magic[:, 0:1], scale=sc[:, RX:RX + 1]).then_inc(x_scaled, 1)
                    act.wait_ge(x_clipped, count(g + 1))
                    nc.scalar.activation(xq[:, bass.ds(g * GT, GT)], rnd[:, 1, :], ACT.Identity,
                                         bias=magic[:, 1:2]).then_inc(xq_ready, 1)
                with act.Fori(0, GROUPS) as g:
                    for c in range(CH):
                        act.wait_ge(gu_done, count(g * CH + c + 1))
                        act.wait_ge(prod_done, count(g * CH + max(c - 1, 0)))
                        nc.scalar.activation(act_g[:, c % 2, :], pg[c % 2][:, :], ACT.Silu,
                                             scale=sc[:, SG + c:SG + c + 1]).then_inc(silu_done, 1)
                act.wait_ge(scales_ready, count(2))
                with act.Fori(0, GROUPS) as g:
                    act.wait_ge(hq_ready, count(g))
                    for c in range(CH):
                        ins = nc.scalar.activation(rnd[:, c, :], prod[c][:, bass.ds(g * GT, GT)], ACT.Identity,
                                                   bias=magic[:, 0:1], scale=sc[:, RH:RH + 1])
                    ins.then_inc(h_scaled, 1)
                    act.wait_ge(acc_done, count(g + 1))
                    act.wait_ge(y_turned, count(g))
                    nc.scalar.activation(yT[:, :], acc[:, :], ACT.Copy, scale=sc[:, SY:SY + 1]).then_inc(y_ready, 1)

            @block.vector
            def _(dve):
                dve.wait_ge(core.w_loaded[7], 16)
                ch = Chain(dve, chain, 0, 26)
                ch.link(nc.vector.tensor_reduce(wsc[:, 0, 0:3], wgu[0], AX.X, ALU.max, apply_absolute_value=True))
                ch.link(nc.vector.tensor_reduce(wsc[:, 0, 3:6], wgu[1], AX.X, ALU.max, apply_absolute_value=True))
                ch.link(nc.vector.tensor_reduce(wsc[:, 0, 6:7], wd, AX.X, ALU.max, apply_absolute_value=True))
                ch.link(nc.vector.tensor_scalar(wsc[:, 1, 0:7], wsc[:, 0, 0:7], 1.0 / QMAX, 1e-30, ALU.mult, ALU.max))
                ch.link(nc.vector.reciprocal(wsc[:, 2, 0:7], wsc[:, 1, 0:7]))
                for k in range(2):
                    for c in range(CH):
                        ins = nc.vector.tensor_scalar(wq[:, k, c * P:(c + 1) * P], wgu[k][:, c, :],
                                                      wsc[:, 2, 3 * k + c:3 * k + c + 1], MAGIC, ALU.mult, ALU.add)
                        ch.link(ins)
                ch.link(nc.vector.tensor_scalar(wq[:, 2, 0:I], wd, wsc[:, 2, 6:7], MAGIC, ALU.mult, ALU.add))
                dve.wait_ge(consts_ready, count(4))
                for k, n in ((0, CH * P), (1, CH * P), (2, I)):
                    ch.link(nc.vector.tensor_scalar(wq[:, k, 0:n], wq[:, k, 0:n], MAGIC, QMAX, ALU.subtract, ALU.min))
                    nc.vector.tensor_scalar(wq_bf[:, k, 0:n], wq[:, k, 0:n], -QMAX - 1.0, None, ALU.max)\
                        .then_inc(wq_ready, 1)
                norm_vector(core, nc, dve, ns)
                dve.wait_ge(sig_ready, count(1))
                ch.link(nc.vector.tensor_scalar(sig[:, :], sig[:, :], 0.5, 0.5, ALU.mult, ALU.add))
                dve.wait_ge(ns.ready, count(GROUPS))
                nc.vector.tensor_reduce(mx[:, 0:1], core.xnT[:, :], AX.X, ALU.max, apply_absolute_value=True)\
                    .then_inc(mx_ready, 1)
                spread_max(dve, ch, 0)
                ch.link(nc.vector.tensor_scalar(sc[:, SG:SG + 3], wsc[:, 1, 0:3], sc[:, SX:SX + 1], None, ALU.mult))
                nc.vector.tensor_scalar(sc[:, SU:SU + 3], wsc[:, 1, 3:6], sc[:, SX:SX + 1], None, ALU.mult)\
                    .then_inc(scales_ready, 1)
                with dve.Fori(0, GROUPS) as g:
                    dve.wait_ge(x_scaled, count(g + 1))
                    nc.vector.tensor_scalar(rnd[:, 1, :], rnd[:, 0, :], MAGIC + QMAX, MAGIC - QMAX - 1.0,
                                            ALU.min, ALU.max).then_inc(x_clipped, 1)
                dve.wait_ge(xq_ready, count(GROUPS))
                with dve.Fori(0, GROUPS) as g:
                    for c in range(CH):
                        dve.wait_ge(silu_done, count(g * CH + c + 1))
                        nc.vector.scalar_tensor_tensor(prod[c][:, bass.ds(g * GT, GT)], pu[c % 2][:, :],
                                                       sc[:, SU + c:SU + c + 1], act_g[:, c % 2, :], ALU.mult, ALU.mult)\
                            .then_inc(prod_done, 1)
                dve.wait_ge(prod_done, count(GROUPS * CH))
                for c in range(CH):
                    ch.link(nc.vector.tensor_reduce(part[:, c:c + 1], prod[c], AX.X, ALU.max,
                                                    apply_absolute_value=True))
                nc.vector.tensor_reduce(mx[:, 1:2], part[:, :], AX.X, ALU.max).then_inc(mx_ready, 1)
                spread_max(dve, ch, 1)
                ch.done()
                nc.vector.tensor_scalar(sc[:, SY:SY + 1], wsc[:, 1, 6:7], sc[:, SH:SH + 1], None, ALU.mult)\
                    .then_inc(scales_ready, 1)
                with dve.Fori(0, GROUPS) as g:
                    dve.wait_ge(h_scaled, count(g + 1))
                    dve.wait_ge(acc_done, count(g))
                    nc.vector.tensor_scalar(rnd[:, :, :], rnd[:, :, :], MAGIC + QMAX, MAGIC - QMAX - 1.0,
                                            ALU.min, ALU.max).then_inc(h_part, 1)
                    dve.wait_ge(h_part, count(g + 1))
                    nc.vector.tensor_scalar(hq[:, :, :], rnd[:, :, :], MAGIC, None, ALU.subtract)\
                        .then_inc(hq_ready, 1)
                    dve.wait_ge(y_turned, count(g + 1))
                    residual_vector(core, nc, g, 7, misc, res_done)


def store(core, nc, out):
    stored = core.sem("stored")
    with nc.Block() as block:
        @block.sync
        def _(sp):
            sp.dma_start(out.rearrange("(n p) d -> p n d", p=P), core.x[:, :, :]).then_inc(stored, 16)
            sp.wait_ge(stored, 16)


def program(nc, d, out):
    with ExitStack() as ctx:
        core = Core(nc, ctx)
        setup(core, nc, d)
        turn_context(core, nc)
        l0_xattn(core, nc, d)
        l0_ffn(core, nc)
        late_weights(core, nc, d)
        l1_xattn(core, nc, d)
        l1_ffn(core, nc)
        narrow_attention(core, nc, d, 4, True)
        l2_ffn(core, nc, d)
        narrow_attention(core, nc, d, 6, False)
        l3_ffn(core, nc, out)
        store(core, nc, out)


def constants():
    c = np.zeros((P, CONST_W), np.float32)

    def put(name, value):
        a, b = CONST[name]
        c[0:value.shape[0], a:b] = value

    p = np.arange(P)
    pos, seq = p % SEQ, p // SEQ
    put("ident", np.eye(P))
    put("tri", (seq[:, None] == seq[None, :]) & (p[:, None] <= p[None, :]))
    k = np.arange(SEQ)
    put("caus_t", np.where(pos[:, None] <= k[None, :], -0.5 * np.log(32.0), NEG))
    put("caus_n", np.where(k[None, :] <= pos[:, None], 0.0, NEG))
    put("hm", (p[:, None] // 8) % 4 == np.arange(4)[None, :])
    freqs = np.exp(-np.arange(4, dtype=np.float32) * np.log(np.float32(10000.0)) / np.float32(4))
    ang = (pos[:, None].astype(np.float32) * freqs[None, :].astype(np.float32)).astype(np.float32)
    put("rope_c", np.tile(np.repeat(np.cos(ang), 2, axis=1), (1, 16)))
    put("rope_s", np.tile(np.stack([-np.sin(ang), np.sin(ang)], axis=-1).reshape(P, 8), (1, 16)))
    put("prio", np.tile(8.0 - np.arange(8)[None, :], (P, 1)))
    put("iota", np.tile(k[None, :], (P, 1)))
    return c


def unit_owner():
    units = np.arange(13 * P) // 176
    return np.tile(np.arange(9)[:, None] == units[None, :], (3, 1)).astype(np.float32)


def laid_out(i):
    f = {k: np.asarray(v) for k, v in i.items()}
    w = np.zeros((P, WEIGHTS_W), np.float32)

    def put(name, value):
        a, b = WEIGHTS[name]
        w[:, a:b] = value.reshape(value.shape[0], -1)

    gates = np.concatenate([f["L0_xattn_igate_kernel"], f["L0_xattn_fgate_kernel"]], axis=1)
    put("l0_gate", gates.reshape(3, P, 8).transpose(1, 0, 2))
    put("l0_q", f["L0_ffn_w_q"])
    put("l0_k", f["L0_ffn_w_k"])
    put("l0_g", f["L0_ffn_w_gate"])
    put("l0_ve", f["L0_ffn_value_experts"].transpose(2, 0, 1, 3))
    put("l0_oe", f["L0_ffn_output_experts"].reshape(8, 4, 2, 64, 128).transpose(2, 3, 0, 1, 4).reshape(P, -1))
    put("l1_q", f["L1_xattn_Wq"])
    put("l1_k", f["L1_xattn_Wk"])
    put("l1_v", f["L1_xattn_Wv"])
    put("l1_o", f["L1_xattn_Wo"].reshape(8, P, D).transpose(1, 0, 2))
    put("l1_d1", f["L1_ffn_Wd1"].transpose(1, 0, 2))
    put("l1_d2", f["L1_ffn_Wd2"].reshape(2, P, D).transpose(1, 0, 2))
    put("l1_base", f["L1_ffn_W_base"])
    put("l1_dn", f["L1_ffn_Wa_down"].transpose(1, 0, 2))
    put("l1_up", f["L1_ffn_Wa_up"].reshape(4, P, D).transpose(1, 0, 2))
    for name in "qkvo":
        put("l2_" + name, f["L2_xattn_w" + name].T)
    put("l2_gw", np.concatenate([f["L2_ffn_gate_w"], f["L2_ffn_shared_gate_w"]], axis=0).T)
    for name, key, shared in (("l2_wg", "L2_ffn_w_gate", "L2_ffn_sw_gate"), ("l2_wu", "L2_ffn_w_up", "L2_ffn_sw_up")):
        units = np.zeros((D, 13 * P), np.float32)
        units[:, 0:1584] = np.concatenate([f[key], f[shared][None]], axis=0).transpose(1, 0, 2).reshape(D, 1584)
        put(name, units)
    down = np.zeros((13 * P, D), np.float32)
    down[0:1584] = np.concatenate([f["L2_ffn_w_down"].reshape(-1, D), f["L2_ffn_sw_down"]], axis=0)
    put("l2_wd", down.reshape(13, P, D).transpose(1, 0, 2))
    put("l3_o", f["L3_xattn_Wo"].T)
    for name, key in (("l3_g", "L3_ffn_w_gate"), ("l3_u", "L3_ffn_w_up")):
        rows = np.zeros((3 * P, D), np.float32)
        rows[0:352] = f[key]
        put(name, rows.reshape(3, P, D).transpose(1, 0, 2))
    put("l3_d", f["L3_ffn_w_down"])

    inter = np.stack([f["g_xattn"], f["g_ffn"]], axis=1).reshape(8)
    rows = np.concatenate([inter, f["L0_xattn_igate_bias"], f["L0_xattn_fgate_bias"], f["L0_xattn_outnorm_scale"],
                           f["L2_xattn_bq"], f["L2_xattn_bk"], f["L2_xattn_bv"],
                           f["L3_ffn_clip_x"], f["L3_ffn_clip_down"]]).reshape(1, ROWS_W)
    cols = np.zeros((P, COLS_W), np.float32)

    def putc(name, value):
        a, b = COLS[name]
        cols[:, a:b] = value.reshape(b - a, P).T

    putc("l1_qw", np.tile(f["L1_xattn_q_norm_w"], 2))
    putc("l1_kw", np.tile(f["L1_xattn_k_norm_w"], 2))
    putc("l1_bd1", f["L1_ffn_bd1"])
    putc("l1_bd2", f["L1_ffn_bd2"])
    putc("l1_bdn", f["L1_ffn_ba_down"])
    putc("l1_bbase", f["L1_ffn_b_base"])
    putc("l1_bup", f["L1_ffn_ba_up"])
    putc("l2_bo", f["L2_xattn_bo"])
    putc("l3_bo", f["L3_xattn_bo"])
    return {"x": f["x"].reshape(TILES * P, D), "ctx": f["ctx_1024"].reshape(TILES * P, D), "weights": w,
            "rows": rows, "cols": cols, "consts": constants(), "sel": unit_owner(), "lens": f["_lenS2"].reshape(TILES, 2).T,
            "mask": f["mask_Bx1xSxS2_ik1"].reshape(NSEQ * SEQ, SEQ)}


def kernel(**inputs):
    import concourse.bacc as bacc
    from concourse.bass_utils import run_bass_kernel_spmd

    nc = bacc.Bacc("TRN2", target_bir_lowering=False, num_devices=1)
    arrays, aps = {}, {}
    for name, a in laid_out(inputs).items():
        a = np.ascontiguousarray(a)
        arrays["in_" + name] = a
        aps[name] = nc.dram_tensor("in_" + name, a.shape, mybir.dt.from_np(a.dtype), kind="ExternalInput").ap()
    out = nc.dram_tensor("out_x", (TILES * P, D), F32, kind="ExternalOutput").ap()
    program(nc, aps, out)
    r = run_bass_kernel_spmd(nc, [arrays], core_ids=[0])
    return r.results[0]["out_x"].reshape(NSEQ, SEQ, D)
```

```python
import concourse.bass as bass
from concourse import mybir
from contextlib import ExitStack
import numpy as np

F32 = mybir.dt.float32
BF16 = mybir.dt.bfloat16
I32 = mybir.dt.int32
ALU = mybir.AluOpType
ACT = mybir.ActivationFunctionType
AX = mybir.AxisListType

P = 128
SEQ = 64
NSEQ = 64
D = 128
TILES = NSEQ * SEQ // P
G = 4
GROUPS = TILES // G
GT = G * P
COUNTERS = 52
NEG = -1e30

CONST = {}
_at = 0
for _name, _w in (("ident", 128), ("tri", 128), ("caus_t", 64), ("caus_n", 64), ("hm", 4), ("rope_c", 64),
                  ("rope_s", 64), ("prio", 8), ("iota", 64)):
    CONST[_name] = (_at, _at + _w)
    _at += _w
CONST_W = _at

WEIGHTS = {}
_at = 0
for _name, _w in (("l0_gate", 24), ("l0_q", 512), ("l0_k", 512), ("l0_g", 64), ("l0_ve", 4096), ("l0_oe", 4096),
                  ("l1_q", 1024), ("l1_k", 1024), ("l1_v", 1024), ("l1_o", 1024),
                  ("l1_d1", 256), ("l1_d2", 256), ("l1_base", 128), ("l1_dn", 512), ("l1_up", 512),
                  ("l2_q", 128), ("l2_k", 128), ("l2_v", 128), ("l2_o", 128),
                  ("l2_gw", 9), ("l2_wg", 1664), ("l2_wu", 1664), ("l2_wd", 1664),
                  ("l3_o", 128), ("l3_g", 384), ("l3_u", 384), ("l3_d", 352)):
    WEIGHTS[_name] = (_at, _at + _w)
    _at += _w
WEIGHTS_W = _at
LATE = WEIGHTS["l2_q"][0]
assert WEIGHTS_W - LATE <= WEIGHTS["l1_q"][0]
LOADS = [("l0_gate", "l0_gate"), ("l0_q", "l0_oe"), ("l1_q", "l1_o"), ("l1_d1", "l1_up"), ("l2_q", "l2_o"),
         ("l2_gw", "l2_wd"), ("l3_o", "l3_o"), ("l3_g", "l3_d")]

ROWS = {}
_at = 0
for _name, _w in (("gates", 8), ("l0_bias", 8), ("l0_norm", 128), ("l2_bv", 128), ("l2_bo", 128),
                  ("l3_bo", 128), ("clips", 2)):
    ROWS[_name] = (_at, _at + _w)
    _at += _w
ROWS_W = _at

COLS = {}
_at = 0
for _name, _w in (("l1_qw", 1), ("l1_kw", 1), ("l1_bd1", 2), ("l1_bd2", 8), ("l1_bdn", 4), ("l1_bbase", 1),
                  ("l1_bup", 8), ("l2_bqk", 4)):
    COLS[_name] = (_at, _at + _w)
    _at += _w
COLS_W = _at


def count(n):
    return n + 1


def after(eng, sem, value):
    if not isinstance(value, int) or value > 0:
        eng.wait_ge(sem, count(value))


class Chain:

    def __init__(self, eng, sem, base, total):
        self.eng, self.sem, self.base, self.total, self.n = eng, sem, base, total, 0

    def link(self, ins):
        self.n += 1
        ins.then_inc(self.sem, 1)
        self.eng.wait_ge(self.sem, count(self.base + self.n))

    def done(self):
        assert self.n == self.total, (self.n, self.total)


class Core:

    def __init__(self, nc, ctx):
        self.nc, self.ctx = nc, ctx
        self.x = self.sb(ctx, "x_all", [P, TILES, D])
        self.ctx_tok = self.sb(ctx, "ctx_all", [P, TILES, D])
        self.xnT = self.sb(ctx, "xnT_all", [P, TILES * P])
        self.ctxT = self.sb(ctx, "ctxT_all", [P, TILES * P])
        self.w_all = self.sb(ctx, "w_all", [P, LATE])
        self.consts = self.sb(ctx, "consts", [P, CONST_W])
        self.rows = self.sb(ctx, "rows", [P, ROWS_W])
        self.cols = self.sb(ctx, "cols", [P, COLS_W])
        self.tanh_g = self.sb(ctx, "tanh_g", [P, 8])
        self.ident_bf = self.sb(ctx, "ident_bf", [P, P], BF16)
        self.half = self.sb(ctx, "minus_half", [P, 128])
        self.halves = [[self.sem(f"counter{h}_{i}") for i in range(COUNTERS)] for h in range(2)]
        self.x_loaded = self.sem("x_loaded")
        self.ctx_loaded = self.sem("ctx_loaded")
        self.ctx_sems = [self.sem(f"ctx_{event}") for event in ("staged", "turned", "copied")]
        self.small_loaded = self.sem("small_loaded")
        self.w_loaded = [self.sem(f"w_loaded{i}") for i in range(len(LOADS))]
        self.st = self.sb(ctx, "stats", [P, TILES, 6])
        self.mv = self.sb(ctx, "mean_rstd", [P, 6, TILES])
        self.xn = self.sb(ctx, "xn", [P, 2, G, D])

    def sb(self, ctx, name, shape, dt=F32):
        return ctx.enter_context(self.nc.sbuf_tensor(name, shape, dt))

    def ps(self, ctx, name, shape=(P, 512), dt=F32):
        return ctx.enter_context(self.nc.psum_tensor(name, list(shape), dt))

    def sem(self, name):
        return self.ctx.enter_context(self.nc.semaphore(name))

    def counters(self, k):
        half = iter(self.halves[k % 2])
        return lambda event: next(half)

    def renew(self, sp, k):
        half = self.halves[k % 2]
        first, last = half[0].num, half[-1].num
        assert last - first == COUNTERS - 1
        sp.sem_clear(range(first, last + 1))
        for sem in half:
            sp.sem_inc(sem, 1)

    def const(self, name, parts=P):
        a, b = CONST[name]
        return self.consts[0:parts, a:b]

    def w(self, name):
        a, b = WEIGHTS[name]
        if a >= LATE:
            a, b = a - LATE, b - LATE
        return self.w_all[:, a:b]

    def row(self, name):
        a, b = ROWS[name]
        return self.rows[:, a:b]

    def col(self, name):
        a, b = COLS[name]
        return self.cols[:, a:b]


def bcast(ap, axis, n):
    ap = ap.unsqueeze(axis)
    shape = list(ap.shape)
    shape[axis] = n
    return ap.broadcast_to(shape)


class NormSems:

    def __init__(self, sem):
        self.stats = sem("statistics of a tile")
        self.chain = sem("chain")
        self.var = sem("variances, means")
        self.rstd = sem("1 / deviations")
        self.xn = sem("xn of a tile")
        self.turned = sem("a tile turned")
        self.ready = sem("xnT of a group")


def norm_vector(core, nc, eng, s, eps=1e-5):
    with eng.Fori(0, GROUPS) as g:
        for j in range(G):
            nc.vector.bn_stats(core.st[:, g * G + j, :], core.x[:, g * G + j, :]).then_inc(s.stats, 1)
    eng.wait_ge(s.stats, count(TILES))
    ch = Chain(eng, s.chain, 0, 5)
    me, mo = core.st[:, :, 1], core.st[:, :, 4]
    ch.link(nc.vector.tensor_tensor(core.mv[:, 2, :], me, mo, ALU.subtract))
    ch.link(nc.vector.tensor_tensor(core.mv[:, 3, :], core.st[:, :, 2], core.st[:, :, 5], ALU.add))
    ch.link(nc.vector.scalar_tensor_tensor(core.mv[:, 4, :], core.mv[:, 2, :], 0.25, core.mv[:, 2, :],
                                           ALU.mult, ALU.mult))
    ch.link(nc.vector.tensor_scalar(core.mv[:, 5, :], core.mv[:, 3, :], 1.0 / D, eps, ALU.mult, ALU.add))
    ch.link(nc.vector.tensor_tensor(core.mv[:, 2, :], me, mo, ALU.add))
    ch.done()
    nc.vector.tensor_tensor(core.mv[:, 3, :], core.mv[:, 4, :], core.mv[:, 5, :], ALU.add).then_inc(s.var, 1)
    nc.vector.tensor_scalar(core.mv[:, 0, :], core.mv[:, 2, :], 0.5, None, ALU.mult).then_inc(s.var, 1)
    eng.wait_ge(s.var, count(2))
    eng.wait_ge(s.rstd, count(1))

    def normalise(g0):
        for half in range(2):
            after(eng, s.turned, (g0 + half - 1) * G)
            for j in range(G):
                n = g0 * G + half * G + j
                nc.vector.tensor_scalar(core.xn[:, half, j, :], core.x[:, bass.ds(n, 1), :].rearrange("p one d -> p (one d)"),
                                        core.mv[:, 0, bass.ds(n, 1)], core.mv[:, 1, bass.ds(n, 1)],
                                        ALU.subtract, ALU.mult).then_inc(s.xn, 1)

    normalise(0)
    with eng.Fori(1, GROUPS // 2) as pair:
        normalise(pair * 2)


def norm_gpsimd(core, nc, eng, s):
    eng.wait_ge(s.var, count(1))
    nc.gpsimd.tensor_tensor(core.mv[:, 1, :], core.mv[:, 3, :], core.half[:, 0:TILES], ALU.pow).then_inc(s.rstd, 1)


def norm_tensor(core, nc, eng, s, banks):
    with eng.Fori(0, GROUPS // 2) as pair:
        g0 = pair * 2
        for half in range(2):
            eng.wait_ge(s.ready, count(g0))
            for j in range(G):
                eng.wait_ge(s.xn, count(g0 * G + half * G + j + 1))
                nc.tensor.transpose(banks[half][:, j * P:(j + 1) * P], core.xn[:, half, j, :], core.const("ident"))\
                    .then_inc(s.turned, 1)


def norm_scalar(core, nc, eng, s, banks):
    with eng.Fori(0, GROUPS // 2) as pair:
        g0 = pair * 2
        for half in range(2):
            eng.wait_ge(s.turned, count(g0 * G + half * G + G))
            nc.scalar.activation(core.xnT[:, bass.ds(g0 * GT + half * GT, GT)], banks[half][:, 0:GT], ACT.Copy)\
                .then_inc(s.ready, 1)


def residual_tensor(core, nc, eng, yT, bank, turned):
    for j in range(G):
        ins = nc.tensor.transpose(bank[:, j * P:(j + 1) * P], yT[:, j * P:(j + 1) * P], core.const("ident"))
    ins.then_inc(turned, 1)


def residual_vector(core, nc, g, k, bank, done):
    xs = core.x[:, bass.ds(g * G, G), :]
    nc.vector.scalar_tensor_tensor(xs, bank[:, :].rearrange("p (j d) -> p j d", j=G), core.tanh_g[:, k:k + 1], xs,
                                   ALU.mult, ALU.add).then_inc(done, 1)


def onehot_links(core, nc, ch, out, val, m, eq, prio, op=ALU.max):
    n = list(val.shape)
    last = len(n) - 1
    ch.link(nc.vector.tensor_reduce(m, val, AX.X, op))
    ch.link(nc.vector.tensor_tensor(eq, val, bcast(m, last, 8), ALU.is_equal))
    ch.link(nc.vector.tensor_tensor(eq, eq, prio, ALU.mult))
    ch.link(nc.vector.tensor_reduce(m, eq, AX.X, ALU.max))
    ch.link(nc.vector.tensor_tensor(out, eq, bcast(m, last, 8), ALU.is_equal))


def setup(core, nc, d):
    with nc.Block() as block:
        prep, tanh_ready = core.sem("setup_prep"), core.sem("tanh_ready")

        @block.sync
        def _(sp):
            for sem in core.halves[0] + core.halves[1] + core.ctx_sems:
                sp.sem_inc(sem, 1)
            sp.dma_start(core.consts[:, :], d["consts"]).then_inc(core.small_loaded, 16)
            sp.dma_start(core.cols[:, :], d["cols"]).then_inc(core.small_loaded, 16)
            sp.dma_start(core.rows[:, :], d["rows"].broadcast_to([P, ROWS_W])).then_inc(core.small_loaded, 16)
            sp.dma_start(core.x[:, :, :], d["x"].rearrange("(n p) d -> p n d", p=P)).then_inc(core.x_loaded, 16)
            sp.dma_start(core.ctx_tok[:, :, :],
                         d["ctx"].rearrange("(n p) d -> p n d", p=P)).then_inc(core.ctx_loaded, 16)
            for i, (first, last) in enumerate(LOADS[0:4]):
                a, b = WEIGHTS[first][0], WEIGHTS[last][1]
                sp.dma_start(core.w_all[:, a:b], d["weights"][:, a:b]).then_inc(core.w_loaded[i], 16)
            sp.wait_ge(core.small_loaded, 48)
            sp.wait_ge(core.x_loaded, 16)
            sp.wait_ge(core.ctx_loaded, 16)

        @block.gpsimd
        def _(pool):
            nc.gpsimd.memset(core.half[:, :], -0.5).then_inc(prep, 1)
            pool.wait_ge(core.small_loaded, 48)
            nc.gpsimd.tensor_copy(core.ident_bf[:, :], core.const("ident")).then_inc(prep, 1)
            pool.wait_ge(prep, 2)

        @block.scalar
        def _(act):
            act.wait_ge(core.small_loaded, 48)
            nc.scalar.activation(core.tanh_g[:, :], core.row("gates"), ACT.Tanh).then_inc(tanh_ready, 1)


def late_weights(core, nc, d):
    with nc.Block() as block:
        @block.sync
        def _(sp):
            for i in range(2):
                sp.wait_ge(core.w_loaded[i], 16)
            for i, (first, last) in enumerate(LOADS[4:]):
                a, b = WEIGHTS[first][0], WEIGHTS[last][1]
                sp.dma_start(core.w_all[:, a - LATE:b - LATE], d["weights"][:, a:b]).then_inc(core.w_loaded[4 + i], 16)


def turn_context(core, nc):
    with ExitStack() as ctx:
        bank = core.ps(ctx, "turn_bank")
        stage = core.sb(ctx, "turn_stage", [P, G, D])
        staged, turned, copied = core.ctx_sems
        with nc.Block() as block:
            @block.vector
            def _(dve):
                with dve.Fori(0, GROUPS) as g:
                    dve.wait_ge(turned, count(g))
                    nc.vector.tensor_copy(stage[:, :, :], core.ctx_tok[:, bass.ds(g * G, G), :]).then_inc(staged, 1)

            @block.tensor
            def _(pe):
                with pe.Fori(0, GROUPS) as g:
                    pe.wait_ge(staged, count(g + 1))
                    pe.wait_ge(copied, count(g))
                    for j in range(G):
                        ins = nc.tensor.transpose(bank[:, j * P:(j + 1) * P], stage[:, j, :], core.const("ident"))
                    ins.then_inc(turned, 1)

            @block.scalar
            def _(act):
                with act.Fori(0, GROUPS) as g:
                    act.wait_ge(turned, count(g + 1))
                    nc.scalar.activation(core.ctxT[:, bass.ds(g * GT, GT)], bank[:, :], ACT.Copy).then_inc(copied, 1)


def l0_xattn(core, nc, d):
    NH, DH = 4, 32
    N = G * NH
    wg = core.w("l0_gate").rearrange("p (i n) -> p i n", i=3)
    scratch = nc.dram_tensor("running_max", (2, TILES * NH * SEQ), F32).ap()
    with ExitStack() as ctx:
        sb = lambda name, shape, dt=F32: core.sb(ctx, "l0x_" + name, shape, dt)
        ps = lambda name, shape=(P, 512), dt=F32: core.ps(ctx, "l0x_" + name, shape, dt)
        sem = core.counters(0)
        xs, cs = sb("xs", [P, GT]), sb("cs", [P, GT])
        gates = sb("gates", [P, TILES, 2 * NH])
        f = sb("f", [P, 3, TILES, NH])
        logf = sb("logf", [P, TILES * NH])
        csum = sb("csum", [P, TILES * NH])
        a = sb("a", [P, TILES * NH])
        aT = sb("aT", [P, P])
        mT = sb("mT", [P, P])
        top = sb("top", [P, TILES * NH])
        floor = sb("floor", [P, TILES * NH])
        m_b = sb("m_b", [P, N, SEQ])
        expo = sb("expo", [P, 2, N, SEQ])
        decay = sb("decay", [P, N, SEQ])
        cmat = sb("cmat", [P, N, SEQ])
        va = sb("va", [P, N, DH + 1])
        den = sb("den", [P, 4, N])
        hs = sb("hs", [P, N, DH])
        cen = sb("cen", [P, N, DH])
        sq = sb("sq", [P, N, DH])
        mom = sb("mom", [P, 4, N])
        hn = sb("hn", [P, 2, N, DH])
        score = [ps(f"score{h}") for h in range(NH)]
        po = [ps(f"po{i}") for i in range(2)]
        misc, gbank = ps("misc"), ps("gbank")
        ns = NormSems(sem)
        staged, gate_done, gates_ready = sem("staged"), sem("gate_done"), sem("gates_ready")
        abs_done, exp_f_done, ln_done, logf_ready = sem("abs_done"), sem("exp_f_done"), sem("ln_done"), sem("logf_ready")
        sum_done, chain, a_ready, a_turned, scan_done = (sem("sum_done"), sem("chain"), sem("a_ready"), sem("a_turned"),
                                                         sem("scan_done"))
        m_turned, floor_in, floor_ready, m_stored = sem("m_turned"), sem("floor_in"), sem("floor_ready"), core.sem("m_stored")
        m_loaded, part_done, expo_ready, decay_ready = core.sem("m_loaded"), sem("part_done"), sem("expo_ready"), sem("decay_ready")
        qk_done, cmat_ready, va_ready, pv_done = sem("qk_done"), sem("cmat_ready"), sem("va_ready"), sem("pv_done")
        ones_set, abs_sum, tail, var_ready, rstd_ready = (sem("ones_set"), sem("abs_sum"), sem("tail"), sem("var_ready"),
                                                          sem("rstd_ready"))
        sq_done, cen_done, res_done, may_pv = sem("sq_done"), sem("cen_done"), sem("res_done"), sem("may_pv")
        out_read = sem("out_read")

        with nc.Block() as block:
            @block.sync
            def _(sp):
                core.renew(sp, 1)
                sp.wait_ge(scan_done, count(2))
                sp.dma_start(scratch.rearrange("b (n s) -> n b s", s=SEQ), mT[:, :].rearrange("n (b s) -> n b s", b=2))\
                    .then_inc(m_stored, 16)
                sp.wait_ge(m_stored, 16)
                with sp.Fori(0, GROUPS) as g:
                    sp.wait_ge(part_done, count(g))
                    for b in range(2):
                        sp.dma_start(m_b[b * SEQ:(b + 1) * SEQ, :, :].rearrange("p n s -> p (n s)"),
                                     scratch[b:b + 1, bass.ds(g * N * SEQ, N * SEQ)].broadcast_to([SEQ, N * SEQ]))\
                            .then_inc(m_loaded, 16)

            @block.gpsimd
            def _(pool):
                nc.gpsimd.memset(va[:, :, :], 1.0).then_inc(ones_set, 1)
                norm_gpsimd(core, nc, pool, ns)

                def values(u):
                    after(pool, pv_done, u)
                    nc.gpsimd.tensor_copy(va[:, :, 0:DH], core.ctx_tok[:, bass.ds(u * G, G), :].rearrange(
                        "p j (h e) -> p (j h) e", h=NH)).then_inc(va_ready, 1)

                def inverse_deviation(g):
                    pool.wait_ge(var_ready, count(g + 1))
                    nc.gpsimd.tensor_tensor(mom[:, 3, :], mom[:, 2, :], core.half[:, 0:N], ALU.pow).then_inc(rstd_ready, 1)

                pool.wait_ge(ones_set, count(1))
                values(0)
                with pool.Fori(0, GROUPS - 1) as g:
                    values(g + 1)
                    inverse_deviation(g)
                inverse_deviation(GROUPS - 1)

            @block.tensor
            def _(pe):
                norm_tensor(core, nc, pe, ns, (misc, gbank))
                pe.wait_ge(core.w_loaded[0], 16)
                pe.wait_ge(ns.ready, count(GROUPS))
                with pe.Fori(0, GROUPS) as g:
                    pe.wait_ge(staged, count(g * 2 + 2))
                    pe.wait_ge(gates_ready, count(g))
                    for j in range(G):
                        for i, src in enumerate((xs, cs, cs)):
                            ins = nc.tensor.matmul(gbank[:, j * 8:j * 8 + 8], src[:, j * P:(j + 1) * P], wg[:, i, :],
                                                   start=(i == 0), stop=(i == 2))
                    ins.then_inc(gate_done, 1)
                pe.wait_ge(ns.ready, count(GROUPS))
                pe.wait_ge(gates_ready, count(GROUPS))
                pe.wait_ge(logf_ready, count(1))
                nc.tensor.matmul(gbank[:, 0:P], core.const("tri"), logf[:, :], start=True, stop=True).then_inc(sum_done, 1)
                pe.wait_ge(a_ready, count(1))
                nc.tensor.transpose(misc[:, 0:P], a[:, :], core.const("ident")).then_inc(a_turned, 1)
                pe.wait_ge(scan_done, count(2))
                nc.tensor.transpose(misc[:, 0:P], mT[:, :], core.const("ident")).then_inc(m_turned, 1)
                with pe.Fori(0, GROUPS) as g:
                    pe.wait_ge(staged, count(GROUPS * 2 + g * 2 + 2))
                    pe.wait_ge(cmat_ready, count(g * NH))
                    for h in range(NH):
                        r = slice(h * DH, (h + 1) * DH)
                        for t in range(G):
                            for b in range(2):
                                c = slice(t * P + b * SEQ, t * P + (b + 1) * SEQ)
                                ins = nc.tensor.matmul(score[h][b * SEQ:(b + 1) * SEQ, t * SEQ:(t + 1) * SEQ],
                                                       cs[r, c], xs[r, c], start=True, stop=True)
                        ins.then_inc(qk_done, 1)
                    pe.wait_ge(cmat_ready, count((g + 1) * NH))
                    pe.wait_ge(va_ready, count(g + 1))
                    pe.wait_ge(out_read, count(g * 2))
                    pe.sem_inc(may_pv, 1)
                    for t in range(G):
                        for h in range(NH):
                            n = t * NH + h
                            for b in range(2):
                                r = slice(b * SEQ, (b + 1) * SEQ)
                                ins = nc.tensor.matmul(po[t // 2][r, (n % 8) * (DH + 1):(n % 8 + 1) * (DH + 1)],
                                                       cmat[r, n, :], va[r, n, :], start=True, stop=True)
                    ins.then_inc(pv_done, 1)

            @block.scalar
            def _(act):
                def stage(u):
                    nc.scalar.activation(xs[:, :], core.xnT[:, bass.ds(u * GT, GT)], ACT.Copy).then_inc(staged, 1)
                    nc.scalar.activation(cs[:, :], core.ctxT[:, bass.ds(u * GT, GT)], ACT.Copy).then_inc(staged, 1)

                norm_scalar(core, nc, act, ns, (misc, gbank))
                act.wait_ge(ns.ready, count(GROUPS))
                with act.Fori(0, GROUPS) as g:
                    act.wait_ge(gate_done, count(g))
                    stage(g)
                act.wait_ge(gate_done, count(GROUPS))
                stage(0)
                act.wait_ge(gates_ready, count(GROUPS))
                fg = gates[:, :, NH:2 * NH]
                nc.scalar.activation(f[:, 0, :, :], fg, ACT.Abs).then_inc(abs_done, 1)
                act.wait_ge(abs_done, count(1))
                nc.scalar.activation(f[:, 1, :, :], f[:, 0, :, :], ACT.Exp, scale=-1.0).then_inc(exp_f_done, 1)
                act.wait_ge(exp_f_done, count(1))
                nc.scalar.activation(f[:, 2, :, :], f[:, 1, :, :], ACT.Ln, bias=1.0).then_inc(ln_done, 1)
                act.wait_ge(floor_in, count(1))
                nc.scalar.activation(floor[:, :], top[:, :], ACT.Exp, scale=-1.0).then_inc(floor_ready, 1)

                def decay_exp(u):
                    act.wait_ge(expo_ready, count(u + 1))
                    after(act, cmat_ready, u * NH)
                    nc.scalar.activation(decay[:, :, :], expo[:, 1, :, :], ACT.Exp).then_inc(decay_ready, 1)

                def normaliser_sums(g):
                    act.wait_ge(pv_done, count(g + 1))
                    act.wait_ge(out_read, count(g * 2))
                    for i in range(2):
                        ins = nc.scalar.activation(den[:, 0, i * 8:(i + 1) * 8],
                                                   po[i][:, 0:8 * (DH + 1)].rearrange("p (n e) -> p n e", n=8)[:, :, DH],
                                                   ACT.Abs)
                    ins.then_inc(abs_sum, 1)

                def squares(g):
                    act.wait_ge(cen_done, count(g + 1))
                    act.wait_ge(var_ready, count(g))
                    nc.scalar.activation(sq[:, :, :], cen[:, :, :], ACT.Square).then_inc(sq_done, 1)

                decay_exp(0)
                with act.Fori(0, GROUPS - 1) as g:
                    act.wait_ge(qk_done, count((g + 1) * NH))
                    stage(g + 1)
                    normaliser_sums(g)
                    decay_exp(g + 1)
                    squares(g)
                normaliser_sums(GROUPS - 1)
                squares(GROUPS - 1)

            @block.vector
            def _(dve):
                norm_vector(core, nc, dve, ns)
                with dve.Fori(0, GROUPS) as g:
                    dve.wait_ge(gate_done, count(g + 1))
                    nc.vector.tensor_tensor(gates[:, bass.ds(g * G, G), :],
                                            gbank[:, 0:G * 8].rearrange("p (j n) -> p j n", j=G),
                                            bcast(core.row("l0_bias"), 1, G), ALU.add).then_inc(gates_ready, 1)
                flat = lambda t: t.rearrange("p n h -> p (n h)")
                dve.wait_ge(ln_done, count(1))
                nc.vector.scalar_tensor_tensor(logf[:, :].rearrange("p (n h) -> p n h", h=NH), gates[:, :, NH:2 * NH], 0.0,
                                               f[:, 2, :, :], ALU.min, ALU.subtract).then_inc(logf_ready, 1)
                ch = Chain(dve, chain, 0, 2)
                dve.wait_ge(sum_done, count(1))
                ch.link(nc.vector.tensor_copy(csum[:, :], gbank[:, 0:P]))
                nc.vector.tensor_tensor(a[:, :].rearrange("p (n h) -> p n h", h=NH), gates[:, :, 0:NH],
                                        csum[:, :].rearrange("p (n h) -> p n h", h=NH), ALU.subtract).then_inc(a_ready, 1)
                dve.wait_ge(a_turned, count(1))
                ch.link(nc.vector.tensor_copy(aT[:, :], misc[:, 0:P]))
                ch.done()
                for b in range(2):
                    r = slice(b * SEQ, (b + 1) * SEQ)
                    nc.vector.tensor_tensor_scan(mT[:, r], aT[:, r], aT[:, r], -3e38, ALU.max, ALU.max)\
                        .then_inc(scan_done, 1)
                dve.wait_ge(m_turned, count(1))
                nc.vector.tensor_tensor(top[:, :], misc[:, 0:P], csum[:, :], ALU.add).then_inc(floor_in, 1)
                dve.wait_ge(a_ready, count(1))
                dve.wait_ge(floor_ready, count(1))

                def exponents(u):
                    dve.wait_ge(m_loaded, u * 32 + 32)
                    nc.vector.tensor_tensor(expo[:, 0, :, :], bcast(core.const("caus_t"), 1, N), m_b[:, :, :],
                                            ALU.subtract).then_inc(part_done, 1)
                    dve.wait_ge(part_done, count(u + 1))
                    after(dve, decay_ready, u)
                    nc.vector.tensor_tensor(expo[:, 1, :, :], expo[:, 0, :, :], bcast(a[:, bass.ds(u * N, N)], 2, SEQ),
                                            ALU.add).then_inc(expo_ready, 1)

                def decayed_scores(g):
                    dve.wait_ge(decay_ready, count(g + 1))
                    dve.wait_ge(pv_done, count(g))
                    for h in range(NH):
                        dve.wait_ge(qk_done, count(g * NH + h + 1))
                        at_h = lambda t: t[:, :, :].rearrange("p (t h) s -> p t h s", h=NH)[:, :, h, :]
                        nc.vector.tensor_tensor(at_h(cmat), score[h][:, 0:G * SEQ].rearrange("p (t s) -> p t s", t=G),
                                                at_h(decay), ALU.mult).then_inc(cmat_ready, 1)

                def outputs(g):
                    ch = Chain(dve, tail, g * 9, 9)
                    dve.wait_ge(abs_sum, count(g + 1))
                    ch.link(nc.vector.tensor_tensor(den[:, 1, :], den[:, 0, :], floor[:, bass.ds(g * N, N)], ALU.max))
                    ch.link(nc.vector.tensor_scalar(den[:, 2, :], den[:, 1, :], 1e-6, None, ALU.add))
                    ch.link(nc.vector.reciprocal(den[:, 3, :], den[:, 2, :]))
                    for i in range(2):
                        nc.vector.tensor_tensor(hs[:, i * 8:(i + 1) * 8, :],
                                                po[i][:, 0:8 * (DH + 1)].rearrange("p (n e) -> p n e", n=8)[:, :, 0:DH],
                                                bcast(den[:, 3, i * 8:(i + 1) * 8], 2, DH), ALU.mult).then_inc(out_read, 1)
                    dve.wait_ge(out_read, count(g * 2 + 2))
                    ch.link(nc.vector.tensor_reduce(mom[:, 0, :], hs[:, :, :], AX.X, ALU.add))
                    ch.link(nc.vector.tensor_scalar(mom[:, 1, :], mom[:, 0, :], 1.0 / DH, None, ALU.mult))
                    nc.vector.tensor_tensor(cen[:, :, :], hs[:, :, :], bcast(mom[:, 1, :], 2, DH), ALU.subtract)\
                        .then_inc(cen_done, 1)
                    dve.wait_ge(sq_done, count(g + 1))
                    ch.link(nc.vector.tensor_reduce(mom[:, 0, :], sq[:, :, :], AX.X, ALU.add))
                    nc.vector.tensor_scalar(mom[:, 2, :], mom[:, 0, :], 1.0 / DH, 1e-6, ALU.mult, ALU.add)\
                        .then_inc(var_ready, 1)
                    dve.wait_ge(rstd_ready, count(g + 1))
                    ch.link(nc.vector.tensor_tensor(hn[:, 0, :, :], cen[:, :, :], bcast(mom[:, 3, :], 2, DH), ALU.mult))
                    per_tile = lambda t: t.rearrange("p (j h) e -> p j (h e)", j=G)
                    ch.link(nc.vector.tensor_tensor(per_tile(hn[:, 1, :, :]), per_tile(hn[:, 0, :, :]),
                                                    bcast(core.row("l0_norm"), 1, G), ALU.mult))
                    x_g = core.x[:, bass.ds(g * G, G), :]
                    ch.link(nc.vector.scalar_tensor_tensor(x_g, per_tile(hn[:, 1, :, :]), core.tanh_g[:, 0:1], x_g,
                                                           ALU.mult, ALU.add))
                    ch.done()

                exponents(0)
                with dve.Fori(0, GROUPS - 1) as g:
                    decayed_scores(g)
                    exponents(g + 1)
                    outputs(g)
                decayed_scores(GROUPS - 1)
                outputs(GROUPS - 1)


def l0_ffn(core, nc):
    H, HD, E = 8, 64, 8
    C = H // 2
    wq, wk, wg = core.w("l0_q"), core.w("l0_k"), core.w("l0_g")
    ve = core.w("l0_ve").rearrange("p (e n) -> p e n", e=E)
    oe = core.w("l0_oe").rearrange("p (e c n) -> p e c n", e=E, c=C)
    with ExitStack() as ctx:
        sb = lambda name, shape, dt=F32: core.sb(ctx, "l0f_" + name, shape, dt)
        ps = lambda name, shape=(P, 512), dt=F32: core.ps(ctx, "l0f_" + name, shape, dt)
        sem = core.counters(1)
        causal = sb("causal", [P, SEQ], BF16)
        spread = sb("spread", [H * E, C, E, P], BF16)
        xs = sb("xs", [P, GT])
        lg = sb("logits", [P, G * H, E])
        top = sb("top", [P, 3, G * H])
        eq = sb("eq", [P, G * H, E])
        oh = sb("oh", [P, G * H, E])
        oh_bf = sb("oh_bf", [P, G, P], BF16)
        ohT = sb("ohT", [H * E, GT], BF16)
        qT = sb("qT", [P, C, GT])
        kb = sb("kb", [P, G, 2, C, 2, SEQ])
        val = sb("val", [P, 2, H, HD])
        v2 = sb("v2", [P, 2, 2, C, 2, HD])
        diff = sb("diff", [P, H, SEQ])
        prob = sb("prob", [P, 2, H, SEQ])
        mx = sb("mx", [P, 2, H])
        tot = sb("tot", [P, 2, 2, H])
        probT = sb("probT", [P, C, P])
        og = sb("og", [P, H * HD])
        oT = sb("oT", [P, C, GT])
        z = sb("z", [P, 2, GT])
        yT = core.xn[:, 0, :, :].rearrange("p j d -> p (j d)")
        work = [ps(f"work{i}") for i in range(2)]
        score = [ps(f"score{i}") for i in range(2)]
        turn, po, acc, misc = ps("turn"), ps("po"), ps("acc"), ps("misc")
        oh_turn = misc[:, 256:512].bitcast(BF16)
        ns = NormSems(sem)
        setup_done, xs_ready, lg_done, chain = sem("setup_done"), sem("xs_ready"), sem("lg_done"), sem("chain")
        top_ready, tanh_done, oh_ready, oh_turned, ohT_ready = (sem("top_ready"), sem("tanh_done"), sem("oh_ready"),
                                                                sem("oh_turned"), sem("ohT_ready"))
        qk_done, qk_copied = sem("qk_done"), sem("qk_copied")
        ve_done, pick_done, v2_ready = sem("ve_done"), sem("pick_done"), sem("v2_ready")
        score_done, sub_done, exp_done, tot_done = sem("score_done"), sem("sub_done"), sem("exp_done"), sem("tot_done")
        p_turned, pT_ready, pv_done, og_ready = sem("p_turned"), sem("pT_ready"), sem("pv_done"), sem("og_ready")
        o_turned, oT_ready, m_done, z_done = sem("o_turned"), sem("oT_ready"), sem("m_done"), sem("z_done")
        acc_done, y_ready, y_turned, res_done = sem("acc_done"), sem("y_ready"), sem("y_turned"), sem("res_done")
        gated, may_pick, max_done, sum_done = sem("gated"), sem("may_pick"), sem("max_done"), sem("sum_done")

        with nc.Block() as block:
            @block.sync
            def _(sp):
                core.renew(sp, 2)

            @block.gpsimd
            def _(pool):
                nc.gpsimd.tensor_copy(causal[:, :], core.const("caus_n")).then_inc(setup_done, 1)
                for c in range(C):
                    for a in range(2):
                        h = 2 * c + a
                        nc.gpsimd.tensor_copy(spread[:, c, :, a * HD:(a + 1) * HD],
                                              bcast(core.const("ident", H * E)[:, h * E:(h + 1) * E], 2, HD))\
                            .then_inc(setup_done, 1)
                nc.gpsimd.memset(oh_bf[:, :, :], 0.0).then_inc(setup_done, 1)
                nc.gpsimd.memset(kb[:, :, :, :, :, :], 0.0).then_inc(setup_done, 1)
                nc.gpsimd.memset(v2[:, :, :, :, :, :], 0.0).then_inc(setup_done, 1)
                norm_gpsimd(core, nc, pool, ns)

                def stage(u):
                    after(pool, ve_done, u * G * E)
                    nc.gpsimd.tensor_copy(xs[:, :], core.xnT[:, bass.ds(u * GT, GT)]).then_inc(xs_ready, 1)

                pool.wait_ge(ns.ready, count(GROUPS))
                stage(0)
                with pool.Fori(1, GROUPS) as u:
                    stage(u)

            @block.tensor
            def _(pe):
                norm_tensor(core, nc, pe, ns, (misc, acc))
                pe.wait_ge(core.w_loaded[1], 16)
                pe.wait_ge(setup_done, count(4 + H))
                pe.wait_ge(ns.ready, count(GROUPS))

                def logits(u):
                    pe.wait_ge(xs_ready, count(u + 1))
                    after(pe, ohT_ready, u)
                    for j in range(G):
                        ins = nc.tensor.matmul(misc[:, j * H * E:(j + 1) * H * E], xs[:, j * P:(j + 1) * P], wg,
                                               start=True, stop=True)
                    ins.then_inc(lg_done, 1)

                def project(u, chunks):
                    for i in chunks:
                        c = i % C
                        if i < 2:
                            after(pe, pick_done, u * G * E)
                        else:
                            pe.wait_ge(qk_copied, count(u * 2 * C + i - 1))
                        nc.tensor.matmul(work[i % 2][:, :], (wq, wk)[i // C][:, c * P:(c + 1) * P],
                                         core.xnT[:, bass.ds(u * GT, GT)], start=True, stop=True).then_inc(qk_done, 1)

                def expert_values(g, t, between=None):
                    for e in range(E):
                        n = (g * G + t) * E + e
                        after(pe, pick_done, n - 1)
                        nc.tensor.matmul(work[e % 2][:, :], xs[:, t * P:(t + 1) * P], ve[:, e, :],
                                         start=True, stop=True).then_inc(ve_done, 1)
                        if e == 2 and between:
                            between()

                def scores(g, t):
                    after(pe, sub_done, g * G + t - 1)
                    nc.tensor.matmul(score[t % 2][:, :], core.ident_bf[:, :], bcast(causal[:, :], 1, H),
                                     start=True, stop=False, skip_group_check=True)
                    for c in range(C):
                        for b in range(2):
                            ins = nc.tensor.matmul(score[t % 2][b * SEQ:(b + 1) * SEQ, c * P:(c + 1) * P],
                                                   qT[:, c, t * P + b * SEQ:t * P + (b + 1) * SEQ],
                                                   kb[:, t, b, c, :, :].rearrange("p a k -> p (a k)"),
                                                   start=False, stop=True, skip_group_check=True)
                    ins.then_inc(score_done, 1)

                def values(g, t):
                    n = g * G + t
                    pe.wait_ge(exp_done, count(n + 1))
                    pe.wait_ge(oT_ready, count(n))
                    for c in range(C):
                        ins = nc.tensor.transpose(turn[:, c * P:(c + 1) * P],
                                                  prob[:, t % 2, 2 * c:2 * c + 2, :].rearrange("p a k -> p (a k)"),
                                                  core.const("ident"))
                    ins.then_inc(p_turned, 1)
                    pe.wait_ge(pT_ready, count(n + 1))
                    pe.wait_ge(og_ready, count(n))
                    pe.wait_ge(v2_ready, count(n * 4 + 4))
                    for c in range(C):
                        for b in range(2):
                            q = slice(b * SEQ, (b + 1) * SEQ)
                            ins = nc.tensor.matmul(po[q, c * P:(c + 1) * P], probT[:, c, q],
                                                   v2[:, t % 2, b, c, :, :].rearrange("p a e -> p (a e)"),
                                                   start=True, stop=True)
                    ins.then_inc(pv_done, 1)

                def turn_out(g, t):
                    pe.wait_ge(og_ready, count(g * G + t + 1))
                    for c in range(C):
                        ins = nc.tensor.transpose(turn[:, c * P:(c + 1) * P], og[:, c * P:(c + 1) * P],
                                                  core.const("ident"))
                    ins.then_inc(o_turned, 1)

                def output_experts(g):
                    pe.wait_ge(ohT_ready, count(g + 1))
                    pe.wait_ge(oT_ready, count(g * G + G))
                    pe.wait_ge(y_ready, count(g))

                    def spread_mask(n):
                        pe.wait_ge(z_done, count(g * C * E + max(n - 1, 0)))
                        nc.tensor.matmul(work[n % 2][:, :], spread[:, n // E, n % E, :], ohT[:, :],
                                         start=True, stop=True).then_inc(m_done, 1)

                    spread_mask(0)
                    for n in range(C * E):
                        if n + 1 < C * E:
                            spread_mask(n + 1)
                        pe.wait_ge(z_done, count(g * C * E + n + 1))
                        nc.tensor.matmul(acc[:, :], oe[:, n % E, n // E, :], z[:, n % 2, :], start=(n == 0),
                                         stop=(n == C * E - 1)).then_inc(acc_done, 1)

                def turn_y(g):
                    pe.wait_ge(y_ready, count(g + 1))
                    residual_tensor(core, nc, pe, yT, misc, y_turned)

                def group(g, more):
                    pe.wait_ge(oh_ready, count(g + 1))
                    pe.wait_ge(res_done, count(g))
                    for j in range(G):
                        ins = nc.tensor.transpose(oh_turn[:, j * P:(j + 1) * P], oh_bf[:, j, :], core.ident_bf[:, :])
                    ins.then_inc(oh_turned, 1)
                    for t in range(G - 1):
                        expert_values(g, t + 1, (lambda: turn_out(g, t - 1)) if t else None)
                        scores(g, t + 1)
                        values(g, t)
                    turn_out(g, G - 2)
                    if more:
                        logits(g + 1)
                        project(g + 1, range(0, C))
                    values(g, G - 1)
                    if more:
                        project(g + 1, range(C, C + 2))
                    turn_out(g, G - 1)
                    if more:
                        project(g + 1, range(C + 2, 2 * C))
                        pe.wait_ge(qk_copied, count((g + 2) * 2 * C))
                    else:
                        pe.wait_ge(pick_done, count((g + 1) * G * E))
                    output_experts(g)
                    if more:
                        pe.wait_ge(oh_ready, count(g + 2))
                        expert_values(g + 1, 0, lambda: turn_y(g))
                        scores(g + 1, 0)
                    else:
                        turn_y(g)

                logits(0)
                project(0, range(2 * C))
                pe.wait_ge(qk_copied, count(2 * C))
                expert_values(0, 0)
                scores(0, 0)
                with pe.Fori(0, GROUPS - 1) as g:
                    group(g, True)
                group(GROUPS - 1, False)

            @block.scalar
            def _(act):
                norm_scalar(core, nc, act, ns, (misc, acc))
                act.wait_ge(setup_done, count(4 + H))

                def copy_q(u):
                    after(act, score_done, u * G)
                    for i in range(C):
                        act.wait_ge(qk_done, count(u * 2 * C + i + 1))
                        nc.scalar.activation(qT[:, i, :], work[i % 2][:, :], ACT.Copy).then_inc(qk_copied, 1)

                def copy_k(u, chunks):
                    after(act, score_done, u * G)
                    for c in chunks:
                        act.wait_ge(qk_done, count(u * 2 * C + C + c + 1))
                        for a in range(2):
                            r = slice(a * HD, (a + 1) * HD)
                            ins = nc.scalar.activation(kb[r, :, :, c, a, :],
                                                       work[c % 2][r, :].rearrange("p (t b k) -> p t b k", t=G, b=2),
                                                       ACT.Copy)
                        ins.then_inc(qk_copied, 1)

                def gate_tanh(u):
                    act.wait_ge(top_ready, count(u + 1))
                    nc.scalar.activation(top[:, 1, :], top[:, 0, :], ACT.Tanh, scale=0.5).then_inc(tanh_done, 1)

                def exp(g, t):
                    n = g * G + t
                    act.wait_ge(sub_done, count(n + 1))
                    after(act, p_turned, n - 1)
                    after(act, tot_done, n - 1)
                    nc.scalar.activation(prob[:, t % 2, :, :], diff[:, :, :], ACT.Exp, scale=HD ** -0.5)\
                        .then_inc(exp_done, 1)

                def copy_pT(g, t):
                    n = g * G + t
                    act.wait_ge(p_turned, count(n + 1))
                    act.wait_ge(pv_done, count(n))
                    nc.scalar.activation(probT[:, :, :], turn[:, :].rearrange("p (c q) -> p c q", c=C), ACT.Copy)\
                        .then_inc(pT_ready, 1)

                def copy_oT(g, t):
                    act.wait_ge(o_turned, count(g * G + t + 1))
                    act.wait_ge(z_done, count(g * C * E))
                    nc.scalar.activation(oT[:, :, t * P:(t + 1) * P], turn[:, :].rearrange("p (c q) -> p c q", c=C),
                                         ACT.Copy).then_inc(oT_ready, 1)

                def group(g, more):
                    act.wait_ge(oh_turned, count(g + 1))
                    act.wait_ge(m_done, count(g * C * E))
                    nc.scalar.activation(ohT[:, :], oh_turn[0:H * E, :], ACT.Copy).then_inc(ohT_ready, 1)
                    for t in range(G - 1):
                        if t:
                            copy_oT(g, t - 1)
                        copy_pT(g, t)
                        exp(g, t + 1)
                    copy_oT(g, G - 2)
                    if more:
                        copy_q(g + 1)
                    copy_pT(g, G - 1)
                    if more:
                        copy_k(g + 1, range(0, 2))
                    copy_oT(g, G - 1)
                    if more:
                        copy_k(g + 1, range(2, C))
                        gate_tanh(g + 1)
                    act.wait_ge(acc_done, count((g + 1) * C * E))
                    act.wait_ge(y_turned, count(g))
                    nc.scalar.activation(yT[:, :], acc[:, :], ACT.Copy).then_inc(y_ready, 1)
                    if more:
                        exp(g + 1, 0)

                copy_q(0)
                copy_k(0, range(C))
                gate_tanh(0)
                exp(0, 0)
                with act.Fori(0, GROUPS - 1) as g:
                    group(g, True)
                group(GROUPS - 1, False)

            @block.vector
            def _(dve):
                norm_vector(core, nc, dve, ns)
                dve.wait_ge(setup_done, count(4 + H))
                prio = bcast(core.const("prio"), 1, G * H)
                gate = top[:, 2, :].rearrange("p (t h) -> p t h", t=G)

                def pick_experts(u):
                    ch = Chain(dve, chain, u * 7, 7)
                    dve.wait_ge(lg_done, count(u + 1))
                    ch.link(nc.vector.tensor_scalar(lg[:, :, :], misc[:, 0:G * H * E].rearrange("p (n e) -> p n e", e=E),
                                                    17.4, -103.0, ALU.min, ALU.max))
                    nc.vector.tensor_reduce(top[:, 0, :], lg[:, :, :], AX.X, ALU.max).then_inc(top_ready, 1)
                    onehot_links(core, nc, ch, oh[:, :, :], lg[:, :, :], top[:, 2, :], eq[:, :, :], prio)
                    after(dve, oh_turned, u)
                    nc.vector.tensor_copy(oh_bf[:, :, 0:H * E], oh[:, :, :].rearrange("p (t h) e -> p t (h e)", t=G))\
                        .then_inc(oh_ready, 1)
                    dve.wait_ge(tanh_done, count(u + 1))
                    ch.link(nc.vector.tensor_scalar(top[:, 2, :], top[:, 1, :], 0.5, 0.5, ALU.mult, ALU.add))
                    ch.done()

                def pick(g, t, between=None):
                    for e in range(E):
                        n = (g * G + t) * E + e
                        dve.wait_ge(ve_done, count(n + 1))
                        w3 = work[e % 2][:, :].rearrange("p (h k) -> p h k", h=H)
                        if e == 0:
                            after(dve, v2_ready, (g * G + t - 1) * 4)
                            nc.vector.tensor_copy(val[:, t % 2, :, :], w3).then_inc(pick_done, 1)
                        else:
                            dve.wait_ge(pick_done, count(n))
                            dve.sem_inc(may_pick, 1)
                            m_e = bcast(oh[:, t * H:(t + 1) * H, e], 2, HD).bitcast(I32)
                            nc.vector.copy_predicated(val[:, t % 2, :, :], m_e, w3).then_inc(pick_done, 1)
                        if e == 1 and between:
                            between()
                    dve.wait_ge(pick_done, count((g * G + t + 1) * E))
                    after(dve, pv_done, g * G + t - 1)
                    for b in range(2):
                        for a in range(2):
                            r = slice(b * SEQ, (b + 1) * SEQ)
                            nc.vector.tensor_tensor(
                                v2[a * SEQ:(a + 1) * SEQ, t % 2, b, :, a, :],
                                val[r, t % 2, :, :].rearrange("p (c a) k -> p c a k", a=2)[:, :, a, :],
                                bcast(gate[r, t, :].rearrange("p (c a) -> p c a", a=2)[:, :, a], 2, HD),
                                ALU.mult).then_inc(v2_ready, 1)

                def softmax(g, t):
                    n = g * G + t
                    s = score[t % 2][:, :].rearrange("p (h k) -> p h k", h=H)
                    dve.wait_ge(score_done, count(n + 1))
                    nc.vector.tensor_reduce(mx[:, t % 2, :], s, AX.X, ALU.max).then_inc(max_done, 1)
                    dve.wait_ge(max_done, count(n + 1))
                    after(dve, exp_done, n)
                    nc.vector.tensor_tensor(diff[:, :, :], s, bcast(mx[:, t % 2, :], 2, SEQ), ALU.subtract)\
                        .then_inc(sub_done, 1)

                def totals(g, t):
                    n = g * G + t
                    dve.wait_ge(exp_done, count(n + 1))
                    nc.vector.tensor_reduce(tot[:, t % 2, 0, :], prob[:, t % 2, :, :], AX.X, ALU.add).then_inc(sum_done, 1)
                    dve.wait_ge(sum_done, count(n + 1))
                    nc.vector.reciprocal(tot[:, t % 2, 1, :], tot[:, t % 2, 0, :]).then_inc(tot_done, 1)
                    dve.wait_ge(tot_done, count(n + 1))
                    nc.vector.tensor_tensor(tot[:, t % 2, 0, :], tot[:, t % 2, 1, :], gate[:, t, :], ALU.mult)\
                        .then_inc(gated, 1)

                def scale_out(g, t):
                    n = g * G + t
                    dve.wait_ge(gated, count(n + 1))
                    dve.wait_ge(pv_done, count(n + 1))
                    dve.wait_ge(o_turned, count(n))
                    nc.vector.tensor_tensor(og[:, :].rearrange("p (h e) -> p h e", h=H),
                                            po[:, :].rearrange("p (h e) -> p h e", h=H),
                                            bcast(tot[:, t % 2, 0, :], 2, HD), ALU.mult).then_inc(og_ready, 1)

                def masked_outputs(g):
                    dve.wait_ge(oT_ready, count(g * G + G))
                    for n in range(C * E):
                        dve.wait_ge(m_done, count(g * C * E + n + 1))
                        dve.wait_ge(acc_done, count(g * C * E + max(n - 1, 0)))
                        nc.vector.tensor_tensor(z[:, n % 2, :], oT[:, n // E, :], work[n % 2][:, :], ALU.mult)\
                            .then_inc(z_done, 1)

                def add_to_x(g):
                    dve.wait_ge(y_turned, count(g + 1))
                    residual_vector(core, nc, g, 1, misc, res_done)

                def group(g, more):
                    for t in range(G - 1):
                        pick(g, t + 1, (lambda: scale_out(g, t - 1)) if t else None)
                        softmax(g, t + 1)
                        totals(g, t)
                    scale_out(g, G - 2)
                    totals(g, G - 1)
                    scale_out(g, G - 1)
                    if more:
                        pick_experts(g + 1)
                    masked_outputs(g)
                    if more:
                        pick(g + 1, 0)
                    add_to_x(g)
                    if more:
                        softmax(g + 1, 0)

                pick_experts(0)
                pick(0, 0)
                softmax(0, 0)
                with dve.Fori(0, GROUPS - 1) as g:
                    group(g, True)
                group(GROUPS - 1, False)


def l1_xattn(core, nc, d):
    H, HD = 16, 64
    C, W = H // 2, H * HD
    wq, wk, wv = core.w("l1_q"), core.w("l1_k"), core.w("l1_v")
    wo = core.w("l1_o").rearrange("p (c d) -> p c d", c=C)
    with ExitStack() as ctx:
        sb = lambda name, shape, dt=F32: core.sb(ctx, "l1x_" + name, shape, dt)
        ps = lambda name, shape=(P, 1024), dt=F32: core.ps(ctx, "l1x_" + name, shape, dt)
        sem = core.counters(2)
        lens_i = sb("lens_i", [P, TILES], I32)
        lens = sb("lens", [P, TILES])
        mask = sb("mask", [P, SEQ], BF16)
        xs, cs = sb("xs", [P, P]), sb("cs", [P, P])
        sq = sb("sq", [P, W])
        ms = sb("ms", [P, 4, H])
        rs = sb("rs", [P, 2, H])
        normed = sb("normed", [P, W])
        qT, kT = sb("qT", [P, C, P]), sb("kT", [P, C, P])
        v2 = sb("v2", [P, 2, C, 2, HD])
        diff = sb("diff", [P, 2, C, SEQ])
        prob = sb("prob", [P, C, 2, SEQ])
        mx = sb("mx", [P, 2, H])
        tot = sb("tot", [P, 4, H])
        probT = sb("probT", [P, C, P])
        og = sb("og", [P, W])
        oT = sb("oT", [P, C, P])
        proj, turn, score, po = ps("proj"), ps("turn"), ps("score"), ps("po")
        ns = NormSems(sem)
        lens_loaded, chain, xs_ready, mask_ready = core.sem("lens_loaded"), sem("chain"), sem("xs_ready"), sem("mask_ready")
        proj_done = [sem(f"proj_done{i}") for i in range(3)]
        sq_done = [sem(f"sq_done{i}") for i in range(2)]
        ms_ready = [sem(f"ms_ready{i}") for i in range(2)]
        rs_ready = [sem(f"rs_ready{i}") for i in range(2)]
        normed_ready = [sem(f"normed_ready{i}") for i in range(2)]
        qk_turned = [sem(f"qk_turned{i}") for i in range(2)]
        qkT_ready = [sem(f"qkT_ready{i}") for i in range(2)]
        v_ready = sem("v_ready")
        score_done, max_done, sub_done, exp_done = sem("score_done"), sem("max_done"), sem("sub_done"), sem("exp_done")
        tot_done, p_turned, pT_ready, pv_done = sem("tot_done"), sem("p_turned"), sem("pT_ready"), sem("pv_done")
        og_ready, o_turned, oT_ready, y_done, res_done = (sem("og_ready"), sem("o_turned"), sem("oT_ready"),
                                                          sem("y_done"), sem("res_done"))

        lens_ready, inv_done, v2_zero = sem("lens_ready"), sem("inv_done"), sem("v2_zero")
        sum_done = [sem(f"sum_done{i}") for i in range(2)]

        with nc.Block() as block:
            @block.sync
            def _(sp):
                core.renew(sp, 3)
                for b in range(2):
                    sp.dma_start(lens_i[b * SEQ:(b + 1) * SEQ, :],
                                 d["lens"][b:b + 1, :].broadcast_to([SEQ, TILES]))\
                        .then_inc(lens_loaded, 16)

            @block.gpsimd
            def _(pool):
                nc.gpsimd.memset(v2[:, :, :, :, :], 0.0).then_inc(v2_zero, 1)
                norm_gpsimd(core, nc, pool, ns)

                def inverse_rms(u):
                    for i in range(2):
                        pool.wait_ge(ms_ready[i], count(u + 1))
                        nc.gpsimd.tensor_tensor(rs[:, i, :], ms[:, 2 + i, :], core.half[:, 0:H], ALU.pow)\
                            .then_inc(rs_ready[i], 1)

                inverse_rms(0)
                with pool.Fori(1, TILES) as u:
                    inverse_rms(u)

            @block.tensor
            def _(pe):
                norm_tensor(core, nc, pe, ns, (po, score))
                pe.wait_ge(core.w_loaded[2], 16)
                pe.wait_ge(ns.ready, count(GROUPS))

                def project(u, i):
                    src, w = ((xs, wq), (cs, wk), (cs, wv))[i]
                    if i == 0:
                        pe.wait_ge(xs_ready, count(u * 2 + 2))
                        after(pe, v_ready, u * 4)
                    else:
                        pe.wait_ge(normed_ready[i - 1], count(u + 1))
                    for half in range(2):
                        ins = nc.tensor.matmul(proj[:, half * 512:(half + 1) * 512], src[:, :],
                                               w[:, half * 512:(half + 1) * 512], start=True, stop=True)
                    ins.then_inc(proj_done[i], 1)

                def turn_qk(u, i):
                    pe.wait_ge(normed_ready[i], count(u + 1))
                    if i == 0:
                        after(pe, pT_ready, u)
                    else:
                        pe.wait_ge(qkT_ready[0], count(u + 1))
                    for c in range(C):
                        ins = nc.tensor.transpose(turn[:, c * P:(c + 1) * P], normed[:, c * P:(c + 1) * P],
                                                  core.const("ident"))
                    ins.then_inc(qk_turned[i], 1)

                def scores(t):
                    pe.wait_ge(qkT_ready[0], count(t + 1))
                    pe.wait_ge(qkT_ready[1], count(t + 1))
                    pe.wait_ge(mask_ready, count(t + 1))
                    after(pe, sub_done, t * 2)
                    for half in range(2):
                        nc.tensor.matmul(score[:, half * 512:(half + 1) * 512], core.ident_bf[:, :],
                                         bcast(mask[:, :], 1, C), start=True, stop=False, skip_group_check=True)
                        for c in range(C):
                            r = slice(half * SEQ, (half + 1) * SEQ)
                            for b in range(2):
                                q = slice(b * SEQ, (b + 1) * SEQ)
                                ins = nc.tensor.matmul(score[q, half * 512 + c * SEQ:half * 512 + (c + 1) * SEQ],
                                                       qT[r, c, q], kT[r, c, q], start=False, stop=True,
                                                       skip_group_check=True)
                        ins.then_inc(score_done, 1)

                def turn_probs(t):
                    pe.wait_ge(exp_done, count(t * 2 + 2))
                    pe.wait_ge(qkT_ready[1], count(t + 1))
                    for c in range(C):
                        ins = nc.tensor.transpose(turn[:, c * P:(c + 1) * P],
                                                  prob[:, c, :, :].rearrange("p a k -> p (a k)"), core.const("ident"))
                    ins.then_inc(p_turned, 1)

                def values(t):
                    pe.wait_ge(pT_ready, count(t + 1))
                    pe.wait_ge(v_ready, count(t * 4 + 4))
                    pe.wait_ge(res_done, count(t))
                    for c in range(C):
                        for b in range(2):
                            q = slice(b * SEQ, (b + 1) * SEQ)
                            ins = nc.tensor.matmul(po[q, c * P:(c + 1) * P], probT[:, c, q],
                                                   v2[:, b, c, :, :].rearrange("p a e -> p (a e)"), start=True, stop=True)
                    ins.then_inc(pv_done, 1)

                def turn_out(t):
                    pe.wait_ge(og_ready, count(t + 1))
                    for c in range(C):
                        ins = nc.tensor.transpose(turn[:, c * P:(c + 1) * P], og[:, c * P:(c + 1) * P],
                                                  core.const("ident"))
                    ins.then_inc(o_turned, 1)

                def project_out(t):
                    pe.wait_ge(oT_ready, count(t + 1))
                    for c in range(C):
                        ins = nc.tensor.matmul(po[:, 0:D], oT[:, c, :], wo[:, c, :], start=(c == 0), stop=(c == C - 1))
                    ins.then_inc(y_done, 1)

                project(0, 0)
                project(0, 1)
                turn_qk(0, 0)
                turn_qk(0, 1)
                project(0, 2)
                scores(0)
                with pe.Fori(0, TILES - 1) as t:
                    project(t + 1, 0)
                    turn_probs(t)
                    values(t)
                    project(t + 1, 1)
                    turn_qk(t + 1, 0)
                    pe.wait_ge(qkT_ready[0], count(t + 2))
                    turn_out(t)
                    project_out(t)
                    turn_qk(t + 1, 1)
                    project(t + 1, 2)
                    scores(t + 1)
                turn_probs(TILES - 1)
                values(TILES - 1)
                turn_out(TILES - 1)
                project_out(TILES - 1)

            @block.scalar
            def _(act):
                norm_scalar(core, nc, act, ns, (po, score))
                act.wait_ge(lens_loaded, 32)
                act.wait_ge(v2_zero, count(1))
                nc.scalar.activation(lens[:, :], lens_i[:, :], ACT.Copy).then_inc(lens_ready, 1)

                def stage(u):
                    after(act, proj_done[2], u)
                    nc.scalar.activation(xs[:, :], core.xnT[:, bass.ds(u * P, P)], ACT.Copy).then_inc(xs_ready, 1)
                    nc.scalar.activation(cs[:, :], core.ctxT[:, bass.ds(u * P, P)], ACT.Copy).then_inc(xs_ready, 1)

                def square(u, i):
                    act.wait_ge(proj_done[i], count(u + 1))
                    after(act, ms_ready[1 - i], u + i)
                    nc.scalar.activation(sq[:, :], proj[:, :], ACT.Square).then_inc(sq_done[i], 1)

                def copy_qkT(u, i):
                    act.wait_ge(qk_turned[i], count(u + 1))
                    after(act, score_done, u * 2)
                    nc.scalar.activation((qT, kT)[i][:, :, :], turn[:, :].rearrange("p (c q) -> p c q", c=C), ACT.Copy,
                                         scale=core.col(("l1_qw", "l1_kw")[i])).then_inc(qkT_ready[i], 1)

                def copy_v(u):
                    act.wait_ge(proj_done[2], count(u + 1))
                    after(act, pv_done, u)
                    for b in range(2):
                        for half in range(2):
                            nc.scalar.activation(v2[half * SEQ:(half + 1) * SEQ, b, :, half, :],
                                                 proj[b * SEQ:(b + 1) * SEQ, :].rearrange(
                                                     "p (c two e) -> p c two e", c=C, two=2)[:, :, half, :],
                                                 ACT.Copy).then_inc(v_ready, 1)

                def exp(t):
                    for half in range(2):
                        act.wait_ge(sub_done, count(t * 2 + half + 1))
                        after(act, p_turned, t)
                        after(act, tot_done, t)
                        nc.scalar.activation(prob[:, :, half, :], diff[:, half, :, :], ACT.Exp,
                                             scale=HD ** -0.5).then_inc(exp_done, 1)

                def copy_pT(t):
                    act.wait_ge(p_turned, count(t + 1))
                    act.wait_ge(pv_done, count(t))
                    nc.scalar.activation(probT[:, :, :], turn[:, :].rearrange("p (c q) -> p c q", c=C), ACT.Copy)\
                        .then_inc(pT_ready, 1)

                def copy_oT(t):
                    act.wait_ge(o_turned, count(t + 1))
                    act.wait_ge(y_done, count(t))
                    nc.scalar.activation(oT[:, :, :], turn[:, :].rearrange("p (c q) -> p c q", c=C), ACT.Copy)\
                        .then_inc(oT_ready, 1)

                act.wait_ge(ns.ready, count(GROUPS))
                stage(0)
                square(0, 0)
                square(0, 1)
                copy_qkT(0, 0)
                copy_qkT(0, 1)
                copy_v(0)
                stage(1)
                exp(0)

                def step(t, more=True):
                    square(t + 1, 0)
                    copy_pT(t)
                    square(t + 1, 1)
                    copy_qkT(t + 1, 0)
                    copy_oT(t)
                    copy_qkT(t + 1, 1)
                    copy_v(t + 1)
                    if more:
                        stage(t + 2)
                    exp(t + 1)

                with act.Fori(0, TILES - 2) as t:
                    step(t)
                step(TILES - 2, more=False)
                copy_pT(TILES - 1)
                copy_oT(TILES - 1)

            @block.vector
            def _(dve):
                norm_vector(core, nc, dve, ns)
                dve.wait_ge(lens_ready, count(1))

                def key_mask(t):
                    after(dve, score_done, t * 2)
                    nc.vector.tensor_scalar(mask[:, :], core.const("iota"), lens[:, bass.ds(t, 1)], NEG,
                                            ALU.is_ge, ALU.mult).then_inc(mask_ready, 1)

                def mean_square(u, i):
                    dve.wait_ge(sq_done[i], count(u + 1))
                    after(dve, rs_ready[i], u)
                    nc.vector.tensor_reduce(ms[:, i, :], sq[:, :].rearrange("p (h e) -> p h e", h=H), AX.X, ALU.add)\
                        .then_inc(sum_done[i], 1)
                    dve.wait_ge(sum_done[i], count(u + 1))
                    nc.vector.tensor_scalar(ms[:, 2 + i, :], ms[:, i, :], 1.0 / HD, 1e-5, ALU.mult, ALU.add)\
                        .then_inc(ms_ready[i], 1)

                def normalise_qk(u, i):
                    dve.wait_ge(rs_ready[i], count(u + 1))
                    after(dve, qk_turned[1 - i], u + i)
                    nc.vector.tensor_tensor(normed[:, :].rearrange("p (h e) -> p h e", h=H),
                                            proj[:, :].rearrange("p (h e) -> p h e", h=H),
                                            bcast(rs[:, i, :], 2, HD), ALU.mult).then_inc(normed_ready[i], 1)

                def softmax(t):
                    for half in range(2):
                        s = score[:, half * 512:(half + 1) * 512].rearrange("p (c k) -> p c k", c=C)
                        m = mx[:, half, 0:C]
                        dve.wait_ge(score_done, count(t * 2 + half + 1))
                        after(dve, sub_done, t * 2)
                        nc.vector.tensor_reduce(m, s, AX.X, ALU.max).then_inc(max_done, 1)
                        dve.wait_ge(max_done, count(t * 2 + half + 1))
                        after(dve, exp_done, t * 2)
                        nc.vector.tensor_tensor(diff[:, half, :, :], s, bcast(m, 2, SEQ), ALU.subtract)\
                            .then_inc(sub_done, 1)

                def totals(t):
                    dve.wait_ge(exp_done, count(t * 2 + 2))
                    dve.wait_ge(og_ready, count(t))
                    nc.vector.tensor_reduce(tot[:, 0, :], prob[:, :, :, :].rearrange("p c a k -> p (c a) k"), AX.X, ALU.add)\
                        .then_inc(tot_done, 1)
                    dve.wait_ge(tot_done, count(t + 1))
                    nc.vector.reciprocal(tot[:, 1, :], tot[:, 0, :]).then_inc(inv_done, 1)

                def scale_out(t):
                    dve.wait_ge(inv_done, count(t + 1))
                    dve.wait_ge(pv_done, count(t + 1))
                    dve.wait_ge(o_turned, count(t))
                    nc.vector.tensor_tensor(og[:, :].rearrange("p (h e) -> p h e", h=H),
                                            po[:, :].rearrange("p (h e) -> p h e", h=H),
                                            bcast(tot[:, 1, :], 2, HD), ALU.mult)\
                        .then_inc(og_ready, 1)

                def add_to_x(t):
                    dve.wait_ge(y_done, count(t + 1))
                    xt = core.x[:, bass.ds(t, 1), :].rearrange("p one d -> p (one d)")
                    nc.vector.scalar_tensor_tensor(xt, po[:, 0:D], core.tanh_g[:, 2:3], xt, ALU.mult, ALU.add)\
                        .then_inc(res_done, 1)

                key_mask(0)
                mean_square(0, 0)
                normalise_qk(0, 0)
                mean_square(0, 1)
                normalise_qk(0, 1)
                softmax(0)
                with dve.Fori(0, TILES - 1) as t:
                    key_mask(t + 1)
                    mean_square(t + 1, 0)
                    normalise_qk(t + 1, 0)
                    totals(t)
                    scale_out(t)
                    mean_square(t + 1, 1)
                    normalise_qk(t + 1, 1)
                    add_to_x(t)
                    softmax(t + 1)
                totals(TILES - 1)
                scale_out(TILES - 1)
                add_to_x(TILES - 1)


def l1_ffn(core, nc):
    E, H, R = 8, 32, 64
    B = GT // SEQ
    w_d1, w_base, w_dn = core.w("l1_d1"), core.w("l1_base"), core.w("l1_dn")
    w_d2 = core.w("l1_d2").rearrange("p (c d) -> p c d", c=2)
    w_up = core.w("l1_up").rearrange("p (c d) -> p c d", c=4)
    bd1, bd2, bdn, bup = core.col("l1_bd1"), core.col("l1_bd2"), core.col("l1_bdn"), core.col("l1_bup")
    with ExitStack() as ctx:
        sb = lambda name, shape, dt=F32: core.sb(ctx, "l1f_" + name, shape, dt)
        ps = lambda name, shape=(P, 512), dt=F32: core.ps(ctx, "l1f_" + name, shape, dt)
        sem = core.counters(3)
        ones = sb("ones", [P, P])
        h1 = sb("h1", [P, 2, GT])
        diff = sb("diff", [P, 2, GT])
        sq = sb("sq", [P, 2, GT])
        sums = sb("sums", [P, E, B])
        loss = sb("loss", [P, B, E])
        m = sb("m", [P, B])
        eq = sb("eq", [P, B, E])
        oh = sb("oh", [P, B, E])
        mask = sb("mask", [P, 4, B])
        bias = sb("bias", [P, 2, B])
        a = sb("a", [P, 4, GT])
        am = sb("am", [P, 4, GT])
        yT = sb("yT", [P, GT])
        ph = [ps(f"ph{i}") for i in range(2)]
        pr = [ps(f"pr{i}") for i in range(2)]
        pa = [ps(f"pa{i}") for i in range(2)]
        acc, misc = ps("acc"), ps("misc")
        ns = NormSems(sem)
        ones_ready, h1_done, h1_ready, recon_done = sem("ones_ready"), sem("h1_done"), sem("h1_ready"), sem("recon_done")
        diff_done, sq_done, red_done, loss_done = sem("diff_done"), sem("sq_done"), sem("red_done"), sem("loss_done")
        chain, mask_ready, a_done, a_ready = sem("chain"), sem("mask_ready"), sem("a_done"), sem("a_ready")
        am_ready, acc_done, y_ready, y_turned = sem("am_ready"), sem("acc_done"), sem("y_ready"), sem("y_turned")
        res_done, bias_ready = sem("res_done"), sem("bias_ready")

        with nc.Block() as block:
            @block.sync
            def _(sp):
                core.renew(sp, 4)

            @block.gpsimd
            def _(pool):
                nc.gpsimd.memset(ones[:, :], 1.0).then_inc(ones_ready, 1)
                norm_gpsimd(core, nc, pool, ns)
                with pool.Fori(0, GROUPS) as g:
                    pool.wait_ge(mask_ready, count(g * 2 + 2))
                    pool.wait_ge(acc_done, count(g))
                    for c in range(4):
                        pool.wait_ge(a_ready, count(g * 4 + c + 1))
                        nc.gpsimd.tensor_tensor(am[:, c, :].rearrange("p (b t) -> p b t", b=B),
                                                a[:, c, :].rearrange("p (b t) -> p b t", b=B),
                                                bcast(mask[:, c, :], 2, SEQ), ALU.mult).then_inc(am_ready, 1)

            @block.tensor
            def _(pe):
                norm_tensor(core, nc, pe, ns, (misc, acc))
                pe.wait_ge(core.w_loaded[3], 16)
                pe.wait_ge(ones_ready, count(1))
                pe.wait_ge(ns.ready, count(GROUPS))
                with pe.Fori(0, GROUPS) as g:
                    x_g = core.xnT[:, bass.ds(g * GT, GT)]
                    pe.wait_ge(h1_ready, count(g * 2))
                    for c in range(2):
                        nc.tensor.matmul(ph[c][:, :], w_d1[:, c * P:(c + 1) * P], x_g, start=True, stop=True)\
                            .then_inc(h1_done, 1)
                    for e in range(E):
                        r, c = H * (e % 4), e // 4
                        pe.wait_ge(h1_ready, count(g * 2 + c + 1))
                        pe.wait_ge(diff_done, count(g * E + max(e - 1, 0)))
                        nc.tensor.matmul(pr[e % 2][:, :], w_d2[r:r + H, c, :], h1[r:r + H, c, :],
                                         start=True, stop=True).then_inc(recon_done, 1)
                    for c in range(4):
                        pe.wait_ge(a_ready, count(g * 4 + max(c - 1, 0)))
                        nc.tensor.matmul(pa[c % 2][:, :], w_dn[:, c * P:(c + 1) * P], x_g, start=True, stop=True)\
                            .then_inc(a_done, 1)
                    pe.wait_ge(red_done, count(g * E + E))
                    pe.wait_ge(res_done, count(g))
                    nc.tensor.matmul(misc[:, 0:E * B], ones[:, :], sums[:, :, :].rearrange("p e b -> p (e b)"),
                                     start=True, stop=True).then_inc(loss_done, 1)
                    pe.wait_ge(y_ready, count(g))
                    nc.tensor.matmul(acc[:, :], w_base, x_g, start=True, stop=False)
                    for c in range(4):
                        pe.wait_ge(am_ready, count(g * 4 + c + 1))
                        ins = nc.tensor.matmul(acc[:, :], w_up[:, c, :], am[:, c, :], start=False, stop=(c == 3))
                    ins.then_inc(acc_done, 1)
                    pe.wait_ge(y_ready, count(g + 1))
                    residual_tensor(core, nc, pe, yT, misc, y_turned)

            @block.scalar
            def _(act):
                norm_scalar(core, nc, act, ns, (misc, acc))
                with act.Fori(0, GROUPS) as g:
                    act.wait_ge(recon_done, count(g * E))
                    for c in range(2):
                        act.wait_ge(h1_done, count(g * 2 + c + 1))
                        nc.scalar.activation(h1[:, c, :], ph[c][:, :], ACT.Relu, bias=bd1[:, c:c + 1])\
                            .then_inc(h1_ready, 1)
                    for e in range(E):
                        act.wait_ge(diff_done, count(g * E + e + 1))
                        act.wait_ge(red_done, count(g * E + max(e - 1, 0)))
                        nc.scalar.activation(sq[:, e % 2, :], diff[:, e % 2, :], ACT.Square).then_inc(sq_done, 1)
                    act.wait_ge(am_ready, count(g * 4))
                    for c in range(4):
                        act.wait_ge(a_done, count(g * 4 + c + 1))
                        nc.scalar.activation(a[:, c, :], pa[c % 2][:, :], ACT.Relu, bias=bdn[:, c:c + 1])\
                            .then_inc(a_ready, 1)

            @block.vector
            def _(dve):
                norm_vector(core, nc, dve, ns)
                with dve.Fori(0, GROUPS) as g:
                    x_g = core.xnT[:, bass.ds(g * GT, GT)]

                    def reduce(e):
                        dve.wait_ge(sq_done, count(g * E + e + 1))
                        nc.vector.tensor_reduce(sums[:, e, :], sq[:, e % 2, :].rearrange("p (b t) -> p b t", b=B),
                                                AX.X, ALU.add).then_inc(red_done, 1)

                    dve.wait_ge(loss_done, count(g))
                    for e in range(E):
                        dve.wait_ge(recon_done, count(g * E + e + 1))
                        dve.wait_ge(sq_done, count(g * E + max(e - 1, 0)))
                        nc.vector.scalar_tensor_tensor(diff[:, e % 2, :], pr[e % 2][:, :], bd2[:, e:e + 1], x_g,
                                                       ALU.add, ALU.subtract).then_inc(diff_done, 1)
                        if e:
                            reduce(e - 1)
                    reduce(E - 1)
                    ch = Chain(dve, chain, g * 8, 8)
                    dve.wait_ge(loss_done, count(g + 1))
                    ch.link(nc.vector.tensor_copy(loss[:, :, :], misc[:, 0:E * B].rearrange("p (e b) -> p b e", e=E)))
                    onehot_links(core, nc, ch, oh[:, :, :], loss[:, :, :], m[:, :], eq[:, :, :],
                                 bcast(core.const("prio"), 1, B), ALU.min)
                    dve.wait_ge(am_ready, count(g * 4))
                    nc.vector.tensor_copy(mask[0:R, :, :], oh[0:R, :, :].rearrange("p b (c q) -> p c b q", q=2)[:, :, :, 0])\
                        .then_inc(mask_ready, 1)
                    nc.vector.tensor_copy(mask[R:P, :, :], oh[R:P, :, :].rearrange("p b (c q) -> p c b q", q=2)[:, :, :, 1])\
                        .then_inc(mask_ready, 1)
                    ch.link(nc.vector.tensor_tensor(eq[:, :, :], oh[:, :, :], bcast(bup, 1, B), ALU.mult))
                    ch.link(nc.vector.tensor_reduce(bias[:, 0, :], eq[:, :, :], AX.X, ALU.add))
                    ch.done()
                    nc.vector.tensor_scalar(bias[:, 1, :], bias[:, 0, :], core.col("l1_bbase"), None, ALU.add)\
                        .then_inc(bias_ready, 1)
                    dve.wait_ge(bias_ready, count(g + 1))
                    dve.wait_ge(acc_done, count(g + 1))
                    dve.wait_ge(y_turned, count(g))
                    nc.vector.tensor_tensor(yT[:, :].rearrange("p (b t) -> p b t", b=B),
                                            acc[:, :].rearrange("p (b t) -> p b t", b=B),
                                            bcast(bias[:, 1, :], 2, SEQ), ALU.add).then_inc(y_ready, 1)
                    dve.wait_ge(y_turned, count(g + 1))
                    residual_vector(core, nc, g, 3, misc, res_done)


def narrow_attention(core, nc, d, k, own):
    H, HD = 16, 8
    C = H // 2
    SCALE = HD ** -0.5 if own else float(D) ** -0.5
    load = 4 if own else 6
    wo, bo = (core.w("l2_o"), core.row("l2_bo")) if own else (core.w("l3_o"), core.row("l3_bo"))
    pre = f"a{k}_"
    with ExitStack() as ctx:
        sb = lambda name, shape, dt=F32: core.sb(ctx, pre + name, shape, dt)
        ps = lambda name, shape=(P, 512), dt=F32: core.ps(ctx, pre + name, shape, dt)
        sem = core.counters(k)
        qT = sb("qT", [P, 2, GT])
        km = sb("km", [P, 2, G, 2, 4, SEQ])
        v2 = sb("v2", [P, 2, G, 2, C, 2 * HD])
        diff = sb("diff", [P, H, SEQ])
        prob = sb("prob", [P, 2, H, SEQ])
        mx = sb("mx", [P, 2, H])
        tot = sb("tot", [P, 2, 2, H])
        probT = sb("probT", [P, C, P])
        og = sb("og", [P, D])
        oT = sb("oT", [P, P])
        score = [ps(f"score{i}", (P, 1024)) for i in range(2)]
        pT = ps("pT", (P, 1024))
        po, misc = ps("po"), ps("misc")
        values_at, turned_at, y_at = slice(0, D), slice(D, 2 * D), slice(2 * D, 3 * D)
        ns = NormSems(sem)
        v2_zero, max_done, sum_done = sem("v2_zero"), sem("max_done"), sem("sum_done")
        q_ready, km_ready, v_ready = sem("q_ready"), sem("km_ready"), sem("v_ready")
        score_done, sub_done, exp_done, tot_done = sem("score_done"), sem("sub_done"), sem("exp_done"), sem("tot_done")
        p_turned, pT_ready, pv_done, og_ready = sem("p_turned"), sem("pT_ready"), sem("pv_done"), sem("og_ready")
        o_turned, oT_ready, y_done, res_done = sem("o_turned"), sem("oT_ready"), sem("y_done"), sem("res_done")
        strip_done = sem("strip_done")
        if own:
            wq, wk, wv = core.w("l2_q"), core.w("l2_k"), core.w("l2_v")
            swapped = sb("swapped", [P, 2, D])
            cs = sb("cs", [P, GT])
            by_cos, by_sin = sb("by_cos", [P, 2, GT]), sb("by_sin", [P, 2, GT])
            kr = sb("kr", [P, GT])
            w_swapped, staged = sem("w_swapped"), sem("staged")
            proj_done, proj_read, rotated = sem("proj_done"), sem("proj_read"), sem("rotated")
        else:
            mask_in = sb("mask_in", [P, TILES, SEQ], I32)
            mask_bf = sb("mask_bf", [P, TILES, SEQ], BF16)
            mask_loaded, mask_ready = core.sem("mask_loaded"), sem("mask_ready")

        with nc.Block() as block:
            @block.sync
            def _(sp):
                core.renew(sp, k + 1)
                if not own:
                    sp.dma_start(mask_in[:, :, :], d["mask"].rearrange("(n p) k -> p n k", p=P)).then_inc(mask_loaded, 16)

            @block.gpsimd
            def _(pool):
                nc.gpsimd.memset(v2[:, :, :, :, :, :], 0.0).then_inc(v2_zero, 1)
                if own:
                    pool.wait_ge(core.w_loaded[load], 16)
                    for i, w in enumerate((wk, wq)):
                        pairs = lambda t: t.rearrange("p (n two) -> p n two", two=2)
                        for e in range(2):
                            nc.gpsimd.tensor_copy(pairs(swapped[:, i, :])[:, :, e], pairs(w)[:, :, 1 - e])\
                                .then_inc(w_swapped, 1)
                norm_gpsimd(core, nc, pool, ns)

                def prepare(u, half):
                    if own:
                        after(pool, proj_done, u * 5)
                        nc.gpsimd.tensor_copy(cs[:, :], core.ctxT[:, bass.ds(u * GT, GT)]).then_inc(staged, 1)
                        for i, dst in enumerate((kr[:, :], qT[:, half, :])):
                            pool.wait_ge(proj_read, count(u * 4 + 2 * i + 2))
                            if i == 0:
                                after(pool, km_ready, u * 4)
                            else:
                                after(pool, score_done, (u - 1) * G)
                            nc.gpsimd.tensor_tensor(dst, by_cos[:, i, :], by_sin[:, i, :], ALU.add).then_inc(rotated, 1)
                    else:
                        pool.wait_ge(ns.ready, count(u + 1))
                        after(pool, score_done, (u - 1) * G)
                        nc.gpsimd.tensor_copy(qT[:, half, :], core.xnT[:, bass.ds(u * GT, GT)]).then_inc(q_ready, 1)
                        after(pool, pv_done, (u - 1) * G)
                        pool.wait_ge(q_ready, count(u + 1))
                        for b in range(2):
                            rows = slice(b * SEQ, (b + 1) * SEQ)
                            for q in range(2):
                                if b or q:
                                    pool.wait_ge(v_ready, count(u * 4 + 2 * b + q))
                                nc.gpsimd.tensor_copy(v2[q * SEQ:(q + 1) * SEQ, half, :, b, :, q * HD:(q + 1) * HD],
                                                      core.ctx_tok[rows, bass.ds(u * G, G), :].rearrange(
                                                          "p j (c q e) -> p j c q e", c=C, q=2)[:, :, :, q, :])\
                                    .then_inc(v_ready, 1)
                        pool.wait_ge(v_ready, count(u * 4 + 4))

                pool.wait_ge(v2_zero, count(1))
                prepare(0, 0)
                with pool.Fori(0, GROUPS // 2 - 1) as i:
                    for half in range(2):
                        prepare(i * 2 + half + 1, 1 - half)
                prepare(GROUPS - 1, 1)

            @block.tensor
            def _(pe):
                norm_tensor(core, nc, pe, ns, (misc, po))
                pe.wait_ge(core.w_loaded[load], 16)
                pe.wait_ge(ns.ready, count(GROUPS))
                if own:
                    pe.wait_ge(w_swapped, count(4))

                def project(u, item):
                    after(pe, proj_read, u * 4 + item)
                    if item == 0:
                        after(pe, v_ready, u * 4)
                    if item == 4:
                        pe.wait_ge(staged, count(u + 1))
                        for j in range(G):
                            ins = nc.tensor.matmul(misc[:, j * P:(j + 1) * P], cs[:, j * P:(j + 1) * P], wv,
                                                   start=True, stop=True)
                    else:
                        w = (wk, swapped[:, 0, :], wq, swapped[:, 1, :])[item]
                        src = (core.ctxT, core.xnT)[item // 2]
                        ins = nc.tensor.matmul(misc[:, :], w, src[:, bass.ds(u * GT, GT)], start=True, stop=True)
                    ins.then_inc(proj_done, 1)

                def group_ready(u):
                    pe.wait_ge(rotated if own else q_ready, count(u * 2 + 2 if own else u + 1))
                    pe.wait_ge(km_ready, count(u * 4 + 4))

                def scores(n, half, t, strips):
                    s = score[t % 2]
                    if strips[0] == 0:
                        after(pe, sub_done, n - 1)
                        if not own:
                            for bank in range(2):
                                nc.tensor.matmul(s[:, bank * 512:(bank + 1) * 512], core.ident_bf[:, :],
                                                 bcast(mask_bf[:, bass.ds(n, 1), :].rearrange("p one k -> p (one k)"), 1, C),
                                                 start=True, stop=False, skip_group_check=True)
                    for strip in strips:
                        for b in range(2):
                            r = 32 * strip
                            ins = nc.tensor.matmul(
                                s[b * SEQ:(b + 1) * SEQ, strip * 256:(strip + 1) * 256],
                                qT[r:r + 32, half, t * P + b * SEQ:t * P + (b + 1) * SEQ],
                                km[r:r + 32, half, t, b, :, :].rearrange("p a k -> p (a k)"),
                                start=own, stop=True, skip_group_check=True)
                    if strips == (0, 2):
                        ins.then_inc(strip_done, 1)
                    elif strips[-1] == 3:
                        ins.then_inc(score_done, 1)

                def turn_probs(n, t):
                    pe.wait_ge(exp_done, count(n + 1))
                    pe.wait_ge(pT_ready, count(n))
                    for c in range(C):
                        ins = nc.tensor.transpose(pT[:, c * P:(c + 1) * P],
                                                  prob[:, t % 2, 2 * c:2 * c + 2, :].rearrange("p a k -> p (a k)"),
                                                  core.const("ident"))
                    ins.then_inc(p_turned, 1)

                def values(n, g, half, t):
                    pe.wait_ge(pT_ready, count(n + 1))
                    pe.wait_ge(res_done, count(n))
                    if t == 0:
                        pe.wait_ge(v_ready, count(g * 4 + 4))
                    for b in range(2):
                        for c in range(C):
                            ins = nc.tensor.matmul(po[b * SEQ:(b + 1) * SEQ, c * 2 * HD:(c + 1) * 2 * HD],
                                                   probT[:, c, b * SEQ:(b + 1) * SEQ], v2[:, half, t, b, c, :],
                                                   start=True, stop=True)
                    ins.then_inc(pv_done, 1)

                def group(g, half, prepare):
                    for t in range(G):
                        n = g * G + t
                        items = ((0, 1), (2, 3), (4,), ())[t] if own and prepare else ()
                        ahead = t + 2 < G or prepare
                        at = (n + 2, half if t + 2 < G else 1 - half, (t + 2) % G)
                        turn_probs(n, t)
                        if items:
                            project(g + 1, items[0])
                        if t == 2 and prepare:
                            group_ready(g + 1)
                        if ahead:
                            scores(*at, (0, 2))
                        values(n, g, half, t)
                        if ahead:
                            pe.wait_ge(strip_done, count(n + 3))
                            scores(*at, (1,))
                        pe.wait_ge(og_ready, count(n + 1))
                        nc.tensor.transpose(po[:, turned_at], og[:, :], core.const("ident")).then_inc(o_turned, 1)
                        if ahead:
                            scores(*at, (3,))
                        if len(items) > 1:
                            project(g + 1, items[1])
                        pe.wait_ge(oT_ready, count(n + 1))
                        nc.tensor.matmul(po[:, y_at], core.const("ident"), bo, start=True, stop=False)
                        nc.tensor.matmul(po[:, y_at], oT[:, :], wo, start=False, stop=True).then_inc(y_done, 1)

                if own:
                    for item in range(5):
                        project(0, item)
                else:
                    pe.wait_ge(mask_ready, count(1))
                group_ready(0)
                for t in range(2):
                    scores(t, 0, t, (0, 2))
                    pe.wait_ge(strip_done, count(t + 1))
                    scores(t, 0, t, (1, 3))
                with pe.Fori(0, GROUPS // 2 - 1) as i:
                    for half in range(2):
                        group(i * 2 + half, half, True)
                for half in range(2):
                    group(GROUPS - 2 + half, half, half == 0)

            @block.scalar
            def _(act):
                norm_scalar(core, nc, act, ns, (misc, po))

                def spread_keys(u, half):
                    after(act, score_done, (u - 1) * G)
                    if own:
                        act.wait_ge(rotated, count(u * 2 + 1))
                    keys = kr[:, :] if own else core.ctxT[:, bass.ds(u * GT, GT)]
                    for a in range(4):
                        nc.scalar.activation(km[:, half, :, :, a, :], keys.rearrange("p (t b k) -> p t b k", t=G, b=2),
                                             ACT.Copy, scale=core.const("hm")[:, a:a + 1]).then_inc(km_ready, 1)

                def exp(n, t):
                    act.wait_ge(sub_done, count(n + 1))
                    after(act, p_turned, n - 1)
                    after(act, tot_done, n - 1)
                    nc.scalar.activation(prob[:, t % 2, :, :], diff[:, :, :], ACT.Exp, scale=SCALE)\
                        .then_inc(exp_done, 1)

                def group(g, half, prepare):
                    for t in range(G):
                        n = g * G + t
                        act.wait_ge(p_turned, count(n + 1))
                        act.wait_ge(pv_done, count(n))
                        nc.scalar.activation(probT[:, :, :], pT[:, :].rearrange("p (c q) -> p c q", c=C), ACT.Copy)\
                            .then_inc(pT_ready, 1)
                        if t + 1 < G or prepare:
                            exp(n + 1, t + 1)
                        act.wait_ge(o_turned, count(n + 1))
                        act.wait_ge(y_done, count(n))
                        nc.scalar.activation(oT[:, :], po[:, turned_at], ACT.Copy).then_inc(oT_ready, 1)
                        if t == 1 and prepare:
                            spread_keys(g + 1, 1 - half)

                spread_keys(0, 0)
                exp(0, 0)
                with act.Fori(0, GROUPS // 2 - 1) as i:
                    for half in range(2):
                        group(i * 2 + half, half, True)
                for half in range(2):
                    group(GROUPS - 2 + half, half, half == 0)

            @block.vector
            def _(dve):
                norm_vector(core, nc, dve, ns)
                if own:
                    dve.wait_ge(v2_zero, count(1))
                else:
                    dve.wait_ge(mask_loaded, 16)
                    nc.vector.tensor_scalar(mask_bf[:, :, :], mask_in[:, :, :], 0, NEG,
                                            ALU.is_equal, ALU.mult).then_inc(mask_ready, 1)

                def read_projected(u, item, half):
                    dve.wait_ge(proj_done, count(u * 5 + item + 1))
                    if item < 4:
                        i, table = item // 2, ("rope_c", "rope_s")[item % 2]
                        dst = (by_cos, by_sin)[item % 2]
                        bias = core.col("l2_bqk")[:, item:item + 1]
                        after(dve, rotated, (u - 1) * 2 + i + 1)
                        nc.vector.scalar_tensor_tensor(dst[:, i, :].rearrange("p (b k) -> p b k", k=SEQ),
                                                       misc[:, :].rearrange("p (b k) -> p b k", k=SEQ), bias,
                                                       bcast(core.const(table), 1, 2 * G), ALU.add, ALU.mult)\
                            .then_inc(proj_read, 1)
                    else:
                        after(dve, pv_done, (u - 1) * G)
                        for b in range(2):
                            rows = slice(b * SEQ, (b + 1) * SEQ)
                            for q in range(2):
                                src = misc[rows, :].rearrange("p (j c q e) -> p j c q e", j=G, c=C, q=2)[:, :, :, q, :]
                                bias = bcast(core.row("l2_bv")[rows, :].rearrange("p (c q e) -> p c q e", c=C, q=2)
                                             [:, :, q, :], 1, G)
                                nc.vector.tensor_tensor(v2[q * SEQ:(q + 1) * SEQ, half, :, b, :, q * HD:(q + 1) * HD],
                                                        src, bias, ALU.add).then_inc(v_ready, 1)

                def softmax(n, t):
                    s = score[t % 2][:, :].rearrange("p (h k) -> p h k", h=H)
                    dve.wait_ge(score_done, count(n + 1))
                    nc.vector.tensor_reduce(mx[:, t % 2, :], s, AX.X, ALU.max).then_inc(max_done, 1)
                    dve.wait_ge(max_done, count(n + 1))
                    after(dve, exp_done, n)
                    nc.vector.tensor_tensor(diff[:, :, :], s, bcast(mx[:, t % 2, :], 2, SEQ), ALU.subtract)\
                        .then_inc(sub_done, 1)

                def totals(n, t):
                    dve.wait_ge(exp_done, count(n + 1))
                    nc.vector.tensor_reduce(tot[:, t % 2, 0, :], prob[:, t % 2, :, :], AX.X, ALU.add).then_inc(sum_done, 1)
                    dve.wait_ge(sum_done, count(n + 1))
                    nc.vector.reciprocal(tot[:, t % 2, 1, :], tot[:, t % 2, 0, :]).then_inc(tot_done, 1)

                def scale_out(n, t):
                    dve.wait_ge(tot_done, count(n + 1))
                    dve.wait_ge(pv_done, count(n + 1))
                    dve.wait_ge(o_turned, count(n))
                    nc.vector.tensor_tensor(og[:, :].rearrange("p (h e) -> p h e", h=H),
                                            po[:, values_at].rearrange("p (h e) -> p h e", h=H),
                                            bcast(tot[:, t % 2, 1, :], 2, HD), ALU.mult).then_inc(og_ready, 1)

                def add_to_x(n):
                    dve.wait_ge(y_done, count(n + 1))
                    xt = core.x[:, bass.ds(n, 1), :].rearrange("p one d -> p (one d)")
                    nc.vector.scalar_tensor_tensor(xt, po[:, y_at], core.tanh_g[:, k:k + 1], xt, ALU.mult, ALU.add)\
                        .then_inc(res_done, 1)

                def group(g, half, prepare):
                    for t in range(G):
                        n = g * G + t
                        items = ((0, 1), (2, 3), (4,), ())[t] if own and prepare else ()
                        if t + 1 < G or prepare:
                            softmax(n + 1, t + 1)
                        if items:
                            read_projected(g + 1, items[0], 1 - half)
                        totals(n, t)
                        scale_out(n, t)
                        if len(items) > 1:
                            read_projected(g + 1, items[1], 1 - half)
                        add_to_x(n)

                if own:
                    for item in range(5):
                        read_projected(0, item, 0)
                softmax(0, 0)
                with dve.Fori(0, GROUPS // 2 - 1) as i:
                    for half in range(2):
                        group(i * 2 + half, half, True)
                for half in range(2):
                    group(GROUPS - 2 + half, half, half == 0)


def l2_ffn(core, nc, d):
    E, I = 8, 176
    CH = -(-(E + 1) * I // P)
    wg, wu, wd, gw = core.w("l2_wg"), core.w("l2_wu"), core.w("l2_wd"), core.w("l2_gw")
    with ExitStack() as ctx:
        sb = lambda name, shape, dt=F32: core.sb(ctx, "l2f_" + name, shape, dt)
        ps = lambda name, shape=(P, 512), dt=F32: core.ps(ctx, "l2f_" + name, shape, dt)
        sem = core.counters(5)
        xs = sb("xs", [P, 2, GT])
        sel_bf = sb("sel_bf", [3 * (E + 1), CH * P], BF16)
        lg = sb("logits", [P, TILES, E + 1])
        oh = sb("onehots", [P, 2, TILES, E])
        eq = sb("eq", [P, TILES, E])
        l2 = sb("second", [P, TILES, E])
        m = sb("m", [P, 4, TILES])
        th = sb("th", [P, 2, TILES])
        comb = sb("comb", [P, TILES, E + 1])
        parts = sb("parts", [P, TILES, 3, E + 1], BF16)
        rest = sb("rest", [P, TILES, E + 1])
        combT = sb("combT", [3 * (E + 1), TILES * P], BF16)
        work = sb("work", [P, 6, GT])
        act_g, hu, hid = work[:, 0:2, :], work[:, 2:4, :], work[:, 4:6, :]
        sel_in = work[0:3 * (E + 1), :, :].rearrange("p a t -> p (a t)")[:, 0:CH * P]
        yT = sb("yT", [P, GT])
        pg = [ps(f"pg{i}") for i in range(2)]
        pu = [ps(f"pu{i}") for i in range(2)]
        pc = [ps(f"pc{i}") for i in range(2)]
        acc = ps("acc")
        misc = ps("misc")
        pl = pc[0][:, :].rearrange("p (n e) -> p n e", n=TILES)
        pct = [bank[0:3 * (E + 1), :].bitcast(BF16) for bank in pg + pu]
        ns = NormSems(sem)
        xs_ready, lg_done, chain, w_in, th_done = sem("xs_ready"), sem("lg_done"), sem("chain"), sem("w_in"), sem("th_done")
        comb_split, comb_turned, comb_ready = sem("comb_split"), sem("comb_turned"), sem("comb_ready")
        gu_done, silu_done, h_done, acc_done = sem("gu_done"), sem("silu_done"), sem("h_done"), sem("acc_done")
        y_ready, y_turned, res_done, sel_ready = sem("y_ready"), sem("y_turned"), sem("res_done"), sem("sel_ready")
        hchain, silu_used = sem("hchain"), sem("silu_used")

        sel_loaded = core.sem("sel_loaded")

        with nc.Block() as block:
            @block.sync
            def _(sp):
                core.renew(sp, 6)
                sp.dma_start(sel_in, d["sel"]).then_inc(sel_loaded, 16)

            @block.gpsimd
            def _(pool):
                pool.wait_ge(sel_loaded, 16)
                nc.gpsimd.tensor_copy(sel_bf[:, :], sel_in).then_inc(sel_ready, 1)
                norm_gpsimd(core, nc, pool, ns)
            @block.tensor
            def _(pe):
                norm_tensor(core, nc, pe, ns, (misc, acc))
                pe.wait_ge(core.w_loaded[5], 16)
                pe.wait_ge(sel_ready, count(1))
                pe.wait_ge(ns.ready, count(GROUPS))

                def up(g, c):
                    after(pe, h_done, g * CH + max(c - 1, 0))
                    x_g = core.xnT[:, bass.ds(g * GT, GT)]
                    nc.tensor.matmul(pg[c % 2][:, :], wg[:, c * P:(c + 1) * P], x_g, start=True, stop=True)
                    nc.tensor.matmul(pu[c % 2][:, :], wu[:, c * P:(c + 1) * P], x_g, start=True, stop=True)
                    nc.tensor.matmul(pc[c % 2][:, :], sel_bf[:, c * P:(c + 1) * P], combT[:, bass.ds(g * GT, GT)],
                                     start=True, stop=True).then_inc(gu_done, 1)

                def down(g, c):
                    pe.wait_ge(h_done, count(g * CH + c + 1))
                    ins = nc.tensor.matmul(acc[:, :], wd[:, c * P:(c + 1) * P], hid[:, c % 2, :],
                                           start=(c == 0), stop=(c == CH - 1))
                    ins.then_inc(acc_done, 1)

                for g in range(GROUPS):
                    pe.wait_ge(xs_ready, count(g + 1))
                    for j in range(G):
                        ins = nc.tensor.matmul(pl[:, g * G + j, 0:E + 1], xs[:, g % 2, j * P:(j + 1) * P], gw,
                                               start=True, stop=True)
                    ins.then_inc(lg_done, 1)
                pe.wait_ge(comb_split, count(1))
                for n in range(TILES):
                    ins = nc.tensor.transpose(pct[n // 8][:, n % 8 * P:(n % 8 + 1) * P],
                                              parts[:, n, :, :].rearrange("p a e -> p (a e)"), core.ident_bf[:, :])
                    if n % 8 == 7:
                        ins.then_inc(comb_turned, 1)
                pe.wait_ge(comb_ready, count(4))

                def turn_y(g):
                    pe.wait_ge(y_ready, count(g + 1))
                    pe.wait_ge(res_done, count(g))
                    residual_tensor(core, nc, pe, yT, misc, y_turned)

                def group(g, more):
                    pe.wait_ge(y_ready, count(g))
                    for c in range(1, CH):
                        up(g, c)
                        down(g, c - 1)
                    down(g, CH - 1)
                    if more:
                        up(g + 1, 0)
                    turn_y(g)

                up(0, 0)
                with pe.Fori(0, GROUPS - 1) as g:
                    group(g, True)
                group(GROUPS - 1, False)

            @block.scalar
            def _(act):
                norm_scalar(core, nc, act, ns, (misc, acc))
                act.wait_ge(sel_ready, count(1))
                act.wait_ge(ns.ready, count(GROUPS))
                with act.Fori(0, GROUPS // 2) as pair:
                    for half in range(2):
                        g = pair * 2 + half
                        act.wait_ge(lg_done, count(pair * 2 + max(half - 1, 0)))
                        nc.scalar.activation(xs[:, half, :], core.xnT[:, bass.ds(g * GT, GT)], ACT.Copy).then_inc(xs_ready, 1)
                act.wait_ge(w_in, count(1))
                nc.scalar.activation(th[:, :, :], m[:, 0:2, :], ACT.Tanh, scale=0.5).then_inc(th_done, 1)
                for i in range(4):
                    act.wait_ge(comb_turned, count(i + 1))
                    nc.scalar.activation(combT[:, i * 2 * GT:(i + 1) * 2 * GT], pct[i], ACT.Copy).then_inc(comb_ready, 1)

                def silu(g, c):
                    act.wait_ge(gu_done, count(g * CH + c + 1))
                    act.wait_ge(silu_used, count(g * CH + max(c - 1, 0)))
                    nc.scalar.activation(act_g[:, c % 2, :], pg[c % 2][:, :], ACT.Silu).then_inc(silu_done, 1)

                with act.Fori(0, GROUPS) as g:
                    for c in range(CH):
                        silu(g, c)
                    act.wait_ge(acc_done, count((g + 1) * CH))
                    act.wait_ge(y_turned, count(g))
                    nc.scalar.activation(yT[:, :], acc[:, :], ACT.Copy).then_inc(y_ready, 1)

            @block.vector
            def _(dve):
                norm_vector(core, nc, dve, ns)
                prio = bcast(core.const("prio"), 1, TILES)
                ch = Chain(dve, chain, 0, 21)
                dve.wait_ge(lg_done, count(GROUPS))
                ch.link(nc.vector.tensor_copy(lg[:, :, :], pl[:, :, 0:E + 1]))
                onehot_links(core, nc, ch, oh[:, 0, :, :], lg[:, :, 0:E], m[:, 2, :], eq[:, :, :], prio)
                ch.link(nc.vector.scalar_tensor_tensor(l2[:, :, :], oh[:, 0, :, :], NEG, lg[:, :, 0:E],
                                                       ALU.mult, ALU.add))
                onehot_links(core, nc, ch, oh[:, 1, :, :], l2[:, :, :], m[:, 3, :], eq[:, :, :], prio)
                ch.link(nc.vector.tensor_reduce(m[:, 2, :], lg[:, :, 0:E], AX.X, ALU.max))
                ch.link(nc.vector.tensor_reduce(m[:, 3, :], l2[:, :, :], AX.X, ALU.max))
                ch.link(nc.vector.tensor_copy(m[:, 1, :], lg[:, :, E]))
                nc.vector.tensor_tensor(m[:, 0, :], m[:, 2, :], m[:, 3, :], ALU.subtract).then_inc(w_in, 1)
                dve.wait_ge(th_done, count(1))
                ch.link(nc.vector.tensor_scalar(m[:, 2, :], th[:, 0, :], 0.5, 0.5, ALU.mult, ALU.add))
                ch.link(nc.vector.tensor_scalar(m[:, 3, :], th[:, 0, :], -0.5, 0.5, ALU.mult, ALU.add))
                ch.link(nc.vector.tensor_scalar(comb[:, :, E], th[:, 1, :], 0.5, 0.5, ALU.mult, ALU.add))
                ch.link(nc.vector.tensor_tensor(oh[:, 0, :, :], oh[:, 0, :, :], bcast(m[:, 2, :], 2, E), ALU.mult))
                ch.link(nc.vector.tensor_tensor(oh[:, 1, :, :], oh[:, 1, :, :], bcast(m[:, 3, :], 2, E), ALU.mult))
                ch.link(nc.vector.tensor_tensor(comb[:, :, 0:E], oh[:, 0, :, :], oh[:, 1, :, :], ALU.add))
                ch.done()
                ch2 = Chain(dve, hchain, 0, 4)
                ch2.link(nc.vector.tensor_copy(parts[:, :, 0, :], comb[:, :, :]))
                ch2.link(nc.vector.tensor_tensor(rest[:, :, :], comb[:, :, :], parts[:, :, 0, :], ALU.subtract))
                ch2.link(nc.vector.tensor_copy(parts[:, :, 1, :], rest[:, :, :]))
                ch2.link(nc.vector.tensor_tensor(comb[:, :, :], rest[:, :, :], parts[:, :, 1, :], ALU.subtract))
                ch2.done()
                nc.vector.tensor_copy(parts[:, :, 2, :], comb[:, :, :]).then_inc(comb_split, 1)
                with dve.Fori(0, GROUPS) as g:
                    for c in range(CH):
                        dve.wait_ge(silu_done, count(g * CH + c + 1))
                        nc.vector.tensor_tensor(hu[:, c % 2, :], act_g[:, c % 2, :], pu[c % 2][:, :], ALU.mult)\
                            .then_inc(silu_used, 1)
                        dve.wait_ge(silu_used, count(g * CH + c + 1))
                        dve.wait_ge(acc_done, count(g * CH + max(c - 1, 0)))
                        nc.vector.tensor_tensor(hid[:, c % 2, :], hu[:, c % 2, :], pc[c % 2][:, :], ALU.mult)\
                            .then_inc(h_done, 1)
                    dve.wait_ge(y_turned, count(g + 1))
                    residual_vector(core, nc, g, 5, misc, res_done)


def l3_ffn(core, nc, out):
    I, CH = 352, 3
    QMAX = 127.0
    MAGIC = 1.5 * 2.0 ** 23
    wgu = [core.w("l3_g").rearrange("p (c d) -> p c d", c=CH), core.w("l3_u").rearrange("p (c d) -> p c d", c=CH)]
    wd = core.w("l3_d")
    clips = core.row("clips")
    with ExitStack() as ctx:
        sb = lambda name, shape, dt=F32: core.sb(ctx, "l3f_" + name, shape, dt)
        ps = lambda name, shape=(P, 512), dt=F32: core.ps(ctx, "l3f_" + name, shape, dt)
        sem = core.counters(7)
        ones = sb("ones", [1, P])
        magic = sb("magic", [P, 2])
        wsc = sb("wsc", [P, 3, 8])
        wq = sb("wq", [P, 3, CH * P])
        wq_bf = sb("wq_bf", [P, 3, CH * P], BF16)
        wT = sb("wT", [P, 3, CH * P], BF16)
        sig = sb("sig", [P, 2])
        mx = sb("mx", [P, 8])
        rowmax = sb("rowmax", [1, 2])
        sc = sb("sc", [P, 24])
        part = sb("part", [P, CH])
        xq = sb("xq", [P, TILES * P], BF16)
        rnd = sb("rnd", [P, CH, GT])
        hq = sb("hq", [P, CH, GT], BF16)
        act_g = sb("act_g", [P, 2, GT])
        yT = sb("yT", [P, GT])
        prod = [core.ctx_tok[:, :, :].rearrange("p n d -> p (n d)"), core.ctxT[:, :], core.xnT[:, :]]
        pg = [ps(f"pg{i}") for i in range(2)]
        pu = [ps(f"pu{i}") for i in range(2)]
        acc, misc, small = ps("acc"), ps("misc"), ps("small")
        wbank = ps("wbank", (P, 1024), BF16)
        ns = NormSems(sem)
        chain, ready, wq_ready, wt_done, wT_ready = sem("chain"), sem("ready"), sem("wq_ready"), sem("wt_done"), sem("wT_ready")
        sig_ready, mx_ready, mx_turned, row_ready, mx_spread = (sem("sig_ready"), sem("mx_ready"), sem("mx_turned"),
                                                               sem("row_ready"), sem("mx_spread"))
        scales_ready = sem("scales_ready")
        x_scaled, x_clipped, xq_ready = sem("x_scaled"), sem("x_clipped"), sem("xq_ready")
        gu_done, silu_done, prod_done, part_done = sem("gu_done"), sem("silu_done"), sem("prod_done"), sem("part_done")
        h_scaled, h_part, hq_ready, acc_done = sem("h_scaled"), sem("h_part"), sem("hq_ready"), sem("acc_done")
        y_ready, y_turned, res_done, stored = sem("y_ready"), sem("y_turned"), sem("res_done"), sem("stored")
        consts_ready = sem("consts_ready")
        SX, RX, SH, RH, SG, SU, SY = 0, 1, 2, 3, 4, 8, 12

        def spread_max(dve, ch, k):
            dve.wait_ge(mx_turned, count(k + 1))
            nc.vector.tensor_reduce(rowmax[0:1, k:k + 1], misc[0:1, 0:P], AX.X, ALU.max).then_inc(row_ready, 1)
            dve.wait_ge(mx_spread, count(k + 1))
            ch.link(nc.vector.tensor_tensor(mx[:, 4 + k:5 + k], small[:, 0:1], sig[:, k:k + 1], ALU.mult))
            ch.link(nc.vector.tensor_scalar(sc[:, 2 * k:2 * k + 1], mx[:, 4 + k:5 + k], 1.0 / QMAX, None, ALU.mult))
            ch.link(nc.vector.reciprocal(sc[:, 2 * k + 1:2 * k + 2], sc[:, 2 * k:2 * k + 1]))

        def spread_max_tensor(pe, k):
            pe.wait_ge(mx_ready, count(k + 1))
            nc.tensor.transpose(misc[0:1, 0:P], mx[:, k:k + 1], core.const("ident")).then_inc(mx_turned, 1)
            pe.wait_ge(row_ready, count(k + 1))
            nc.tensor.matmul(small[:, 0:1], ones[:, :], rowmax[0:1, k:k + 1], start=True, stop=True)\
                .then_inc(mx_spread, 1)

        with nc.Block() as block:
            @block.gpsimd
            def _(pool):
                nc.gpsimd.memset(ones[:, :], 1.0).then_inc(consts_ready, 1)
                nc.gpsimd.memset(magic[:, 0:1], MAGIC).then_inc(consts_ready, 1)
                nc.gpsimd.memset(magic[:, 1:2], -MAGIC).then_inc(consts_ready, 1)
                nc.gpsimd.memset(wq_bf[:, 2, I:CH * P], 0.0).then_inc(consts_ready, 1)
                norm_gpsimd(core, nc, pool, ns)

            @block.tensor
            def _(pe):
                norm_tensor(core, nc, pe, ns, (misc, acc))
                pe.wait_ge(consts_ready, count(4))
                pe.wait_ge(wq_ready, count(3))
                for k in range(3):
                    for c in range(CH):
                        ins = nc.tensor.transpose(wbank[:, c * P:(c + 1) * P], wq_bf[:, k, c * P:(c + 1) * P],
                                                  core.ident_bf[:, :])
                    ins.then_inc(wt_done, 1)
                    pe.wait_ge(wT_ready, count(k + 1))
                pe.wait_ge(ns.ready, count(GROUPS))
                spread_max_tensor(pe, 0)
                with pe.Fori(0, GROUPS) as g:
                    x_g = xq[:, bass.ds(g * GT, GT)]
                    pe.wait_ge(xq_ready, count(g + 1))
                    for c in range(CH):
                        b = c % 2
                        pe.wait_ge(prod_done, count(g * CH + max(c - 1, 0)))
                        nc.tensor.matmul(pg[b][:, :], wT[:, 0, c * P:(c + 1) * P], x_g, start=True, stop=True)
                        nc.tensor.matmul(pu[b][:, :], wT[:, 1, c * P:(c + 1) * P], x_g, start=True, stop=True)\
                            .then_inc(gu_done, 1)
                spread_max_tensor(pe, 1)
                with pe.Fori(0, GROUPS) as g:
                    pe.wait_ge(hq_ready, count(g + 1))
                    pe.wait_ge(y_ready, count(g))
                    for c in range(CH):
                        ins = nc.tensor.matmul(acc[:, :], wT[:, 2, c * P:(c + 1) * P], hq[:, c, :],
                                               start=(c == 0), stop=(c == CH - 1))
                    ins.then_inc(acc_done, 1)
                    pe.wait_ge(y_ready, count(g + 1))
                    pe.wait_ge(res_done, count(g))
                    residual_tensor(core, nc, pe, yT, misc, y_turned)

            @block.scalar
            def _(act):
                norm_scalar(core, nc, act, ns, (misc, acc))
                act.wait_ge(consts_ready, count(4))
                nc.scalar.activation(sig[:, :], clips, ACT.Tanh, scale=0.5).then_inc(sig_ready, 1)
                for k in range(3):
                    act.wait_ge(wt_done, count(k + 1))
                    nc.scalar.activation(wT[:, k, :], wbank[:, 0:CH * P], ACT.Copy).then_inc(wT_ready, 1)
                act.wait_ge(scales_ready, count(1))
                with act.Fori(0, GROUPS) as g:
                    act.wait_ge(xq_ready, count(g))
                    nc.scalar.activation(rnd[:, 0, :], core.xnT[:, bass.ds(g * GT, GT)], ACT.Identity,
                                         bias=magic[:, 0:1], scale=sc[:, RX:RX + 1]).then_inc(x_scaled, 1)
                    act.wait_ge(x_clipped, count(g + 1))
                    nc.scalar.activation(xq[:, bass.ds(g * GT, GT)], rnd[:, 1, :], ACT.Identity,
                                         bias=magic[:, 1:2]).then_inc(xq_ready, 1)
                with act.Fori(0, GROUPS) as g:
                    for c in range(CH):
                        act.wait_ge(gu_done, count(g * CH + c + 1))
                        act.wait_ge(prod_done, count(g * CH + max(c - 1, 0)))
                        nc.scalar.activation(act_g[:, c % 2, :], pg[c % 2][:, :], ACT.Silu,
                                             scale=sc[:, SG + c:SG + c + 1]).then_inc(silu_done, 1)
                act.wait_ge(scales_ready, count(2))
                with act.Fori(0, GROUPS) as g:
                    act.wait_ge(hq_ready, count(g))
                    for c in range(CH):
                        ins = nc.scalar.activation(rnd[:, c, :], prod[c][:, bass.ds(g * GT, GT)], ACT.Identity,
                                                   bias=magic[:, 0:1], scale=sc[:, RH:RH + 1])
                    ins.then_inc(h_scaled, 1)
                    act.wait_ge(acc_done, count(g + 1))
                    act.wait_ge(y_turned, count(g))
                    nc.scalar.activation(yT[:, :], acc[:, :], ACT.Copy, scale=sc[:, SY:SY + 1]).then_inc(y_ready, 1)

            @block.vector
            def _(dve):
                dve.wait_ge(core.w_loaded[7], 16)
                ch = Chain(dve, chain, 0, 26)
                ch.link(nc.vector.tensor_reduce(wsc[:, 0, 0:3], wgu[0], AX.X, ALU.max, apply_absolute_value=True))
                ch.link(nc.vector.tensor_reduce(wsc[:, 0, 3:6], wgu[1], AX.X, ALU.max, apply_absolute_value=True))
                ch.link(nc.vector.tensor_reduce(wsc[:, 0, 6:7], wd, AX.X, ALU.max, apply_absolute_value=True))
                ch.link(nc.vector.tensor_scalar(wsc[:, 1, 0:7], wsc[:, 0, 0:7], 1.0 / QMAX, 1e-30, ALU.mult, ALU.max))
                ch.link(nc.vector.reciprocal(wsc[:, 2, 0:7], wsc[:, 1, 0:7]))
                for k in range(2):
                    for c in range(CH):
                        ins = nc.vector.tensor_scalar(wq[:, k, c * P:(c + 1) * P], wgu[k][:, c, :],
                                                      wsc[:, 2, 3 * k + c:3 * k + c + 1], MAGIC, ALU.mult, ALU.add)
                        ch.link(ins)
                ch.link(nc.vector.tensor_scalar(wq[:, 2, 0:I], wd, wsc[:, 2, 6:7], MAGIC, ALU.mult, ALU.add))
                dve.wait_ge(consts_ready, count(4))
                for k, n in ((0, CH * P), (1, CH * P), (2, I)):
                    ch.link(nc.vector.tensor_scalar(wq[:, k, 0:n], wq[:, k, 0:n], MAGIC, QMAX, ALU.subtract, ALU.min))
                    nc.vector.tensor_scalar(wq_bf[:, k, 0:n], wq[:, k, 0:n], -QMAX - 1.0, None, ALU.max)\
                        .then_inc(wq_ready, 1)
                norm_vector(core, nc, dve, ns)
                dve.wait_ge(sig_ready, count(1))
                ch.link(nc.vector.tensor_scalar(sig[:, :], sig[:, :], 0.5, 0.5, ALU.mult, ALU.add))
                dve.wait_ge(ns.ready, count(GROUPS))
                nc.vector.tensor_reduce(mx[:, 0:1], core.xnT[:, :], AX.X, ALU.max, apply_absolute_value=True)\
                    .then_inc(mx_ready, 1)
                spread_max(dve, ch, 0)
                ch.link(nc.vector.tensor_scalar(sc[:, SG:SG + 3], wsc[:, 1, 0:3], sc[:, SX:SX + 1], None, ALU.mult))
                nc.vector.tensor_scalar(sc[:, SU:SU + 3], wsc[:, 1, 3:6], sc[:, SX:SX + 1], None, ALU.mult)\
                    .then_inc(scales_ready, 1)
                with dve.Fori(0, GROUPS) as g:
                    dve.wait_ge(x_scaled, count(g + 1))
                    nc.vector.tensor_scalar(rnd[:, 1, :], rnd[:, 0, :], MAGIC + QMAX, MAGIC - QMAX - 1.0,
                                            ALU.min, ALU.max).then_inc(x_clipped, 1)
                dve.wait_ge(xq_ready, count(GROUPS))
                with dve.Fori(0, GROUPS) as g:
                    for c in range(CH):
                        dve.wait_ge(silu_done, count(g * CH + c + 1))
                        nc.vector.scalar_tensor_tensor(prod[c][:, bass.ds(g * GT, GT)], pu[c % 2][:, :],
                                                       sc[:, SU + c:SU + c + 1], act_g[:, c % 2, :], ALU.mult, ALU.mult)\
                            .then_inc(prod_done, 1)
                dve.wait_ge(prod_done, count(GROUPS * CH))
                for c in range(CH):
                    ch.link(nc.vector.tensor_reduce(part[:, c:c + 1], prod[c], AX.X, ALU.max,
                                                    apply_absolute_value=True))
                nc.vector.tensor_reduce(mx[:, 1:2], part[:, :], AX.X, ALU.max).then_inc(mx_ready, 1)
                spread_max(dve, ch, 1)
                ch.done()
                nc.vector.tensor_scalar(sc[:, SY:SY + 1], wsc[:, 1, 6:7], sc[:, SH:SH + 1], None, ALU.mult)\
                    .then_inc(scales_ready, 1)
                with dve.Fori(0, GROUPS) as g:
                    dve.wait_ge(h_scaled, count(g + 1))
                    dve.wait_ge(acc_done, count(g))
                    nc.vector.tensor_scalar(rnd[:, :, :], rnd[:, :, :], MAGIC + QMAX, MAGIC - QMAX - 1.0,
                                            ALU.min, ALU.max).then_inc(h_part, 1)
                    dve.wait_ge(h_part, count(g + 1))
                    nc.vector.tensor_scalar(hq[:, :, :], rnd[:, :, :], MAGIC, None, ALU.subtract)\
                        .then_inc(hq_ready, 1)
                    dve.wait_ge(y_turned, count(g + 1))
                    residual_vector(core, nc, g, 7, misc, res_done)


def store(core, nc, out):
    stored = core.sem("stored")
    with nc.Block() as block:
        @block.sync
        def _(sp):
            sp.dma_start(out.rearrange("(n p) d -> p n d", p=P), core.x[:, :, :]).then_inc(stored, 16)
            sp.wait_ge(stored, 16)


def program(nc, d, out):
    with ExitStack() as ctx:
        core = Core(nc, ctx)
        setup(core, nc, d)
        turn_context(core, nc)
        l0_xattn(core, nc, d)
        l0_ffn(core, nc)
        late_weights(core, nc, d)
        l1_xattn(core, nc, d)
        l1_ffn(core, nc)
        narrow_attention(core, nc, d, 4, True)
        l2_ffn(core, nc, d)
        narrow_attention(core, nc, d, 6, False)
        l3_ffn(core, nc, out)
        store(core, nc, out)


def constants():
    c = np.zeros((P, CONST_W), np.float32)

    def put(name, value):
        a, b = CONST[name]
        c[0:value.shape[0], a:b] = value

    p = np.arange(P)
    pos, seq = p % SEQ, p // SEQ
    put("ident", np.eye(P))
    put("tri", (seq[:, None] == seq[None, :]) & (p[:, None] <= p[None, :]))
    k = np.arange(SEQ)
    put("caus_t", np.where(pos[:, None] <= k[None, :], -0.5 * np.log(32.0), NEG))
    put("caus_n", np.where(k[None, :] <= pos[:, None], 0.0, NEG))
    put("hm", (p[:, None] // 8) % 4 == np.arange(4)[None, :])
    freqs = np.exp(-np.arange(4, dtype=np.float32) * np.log(np.float32(10000.0)) / np.float32(4))
    ang = freqs[(p % 8) // 2][:, None] * k[None, :].astype(np.float32)
    put("rope_c", np.cos(ang))
    put("rope_s", np.where(p[:, None] % 2 == 0, -np.sin(ang), np.sin(ang)))
    put("prio", np.tile(8.0 - np.arange(8)[None, :], (P, 1)))
    put("iota", np.tile(k[None, :], (P, 1)))
    return c


def unit_owner():
    units = np.arange(13 * P) // 176
    return np.tile(np.arange(9)[:, None] == units[None, :], (3, 1)).astype(np.float32)


def laid_out(i):
    f = {k: np.asarray(v) for k, v in i.items()}
    w = np.zeros((P, WEIGHTS_W), np.float32)

    def put(name, value):
        a, b = WEIGHTS[name]
        w[:, a:b] = value.reshape(value.shape[0], -1)

    gates = np.concatenate([f["L0_xattn_igate_kernel"], f["L0_xattn_fgate_kernel"]], axis=1)
    put("l0_gate", gates.reshape(3, P, 8).transpose(1, 0, 2))
    put("l0_q", f["L0_ffn_w_q"])
    put("l0_k", f["L0_ffn_w_k"])
    put("l0_g", f["L0_ffn_w_gate"])
    put("l0_ve", f["L0_ffn_value_experts"].transpose(2, 0, 1, 3))
    put("l0_oe", f["L0_ffn_output_experts"].reshape(8, 4, 2, 64, 128).transpose(2, 3, 0, 1, 4).reshape(P, -1))
    put("l1_q", f["L1_xattn_Wq"])
    put("l1_k", f["L1_xattn_Wk"])
    put("l1_v", f["L1_xattn_Wv"])
    put("l1_o", f["L1_xattn_Wo"].reshape(8, P, D).transpose(1, 0, 2))
    put("l1_d1", f["L1_ffn_Wd1"].transpose(1, 0, 2))
    put("l1_d2", f["L1_ffn_Wd2"].reshape(2, P, D).transpose(1, 0, 2))
    put("l1_base", f["L1_ffn_W_base"])
    put("l1_dn", f["L1_ffn_Wa_down"].transpose(1, 0, 2))
    put("l1_up", f["L1_ffn_Wa_up"].reshape(4, P, D).transpose(1, 0, 2))
    for name in "qkvo":
        put("l2_" + name, f["L2_xattn_w" + name].T)
    put("l2_gw", np.concatenate([f["L2_ffn_gate_w"], f["L2_ffn_shared_gate_w"]], axis=0).T)
    for name, key, shared in (("l2_wg", "L2_ffn_w_gate", "L2_ffn_sw_gate"), ("l2_wu", "L2_ffn_w_up", "L2_ffn_sw_up")):
        units = np.zeros((D, 13 * P), np.float32)
        units[:, 0:1584] = np.concatenate([f[key], f[shared][None]], axis=0).transpose(1, 0, 2).reshape(D, 1584)
        put(name, units)
    down = np.zeros((13 * P, D), np.float32)
    down[0:1584] = np.concatenate([f["L2_ffn_w_down"].reshape(-1, D), f["L2_ffn_sw_down"]], axis=0)
    put("l2_wd", down.reshape(13, P, D).transpose(1, 0, 2))
    put("l3_o", f["L3_xattn_Wo"].T)
    for name, key in (("l3_g", "L3_ffn_w_gate"), ("l3_u", "L3_ffn_w_up")):
        rows = np.zeros((3 * P, D), np.float32)
        rows[0:352] = f[key]
        put(name, rows.reshape(3, P, D).transpose(1, 0, 2))
    put("l3_d", f["L3_ffn_w_down"])

    inter = np.stack([f["g_xattn"], f["g_ffn"]], axis=1).reshape(8)
    rows = np.concatenate([inter, f["L0_xattn_igate_bias"], f["L0_xattn_fgate_bias"], f["L0_xattn_outnorm_scale"],
                           f["L2_xattn_bv"], f["L2_xattn_bo"], f["L3_xattn_bo"],
                           f["L3_ffn_clip_x"], f["L3_ffn_clip_down"]]).reshape(1, ROWS_W)
    cols = np.zeros((P, COLS_W), np.float32)

    def putc(name, value):
        a, b = COLS[name]
        cols[:, a:b] = value.reshape(b - a, P).T

    putc("l1_qw", np.tile(f["L1_xattn_q_norm_w"], 2))
    putc("l1_kw", np.tile(f["L1_xattn_k_norm_w"], 2))
    putc("l1_bd1", f["L1_ffn_bd1"])
    putc("l1_bd2", f["L1_ffn_bd2"])
    putc("l1_bdn", f["L1_ffn_ba_down"])
    putc("l1_bbase", f["L1_ffn_b_base"])
    putc("l1_bup", f["L1_ffn_ba_up"])
    pairs_swapped = np.arange(P) ^ 1
    putc("l2_bqk", np.concatenate([b[o] for b in (f["L2_xattn_bk"], f["L2_xattn_bq"])
                                   for o in (np.arange(P), pairs_swapped)]))
    return {"x": f["x"].reshape(TILES * P, D), "ctx": f["ctx_1024"].reshape(TILES * P, D), "weights": w,
            "rows": rows, "cols": cols, "consts": constants(), "sel": unit_owner(), "lens": f["_lenS2"].reshape(TILES, 2).T,
            "mask": f["mask_Bx1xSxS2_ik1"].reshape(NSEQ * SEQ, SEQ)}


def kernel(**inputs):
    import concourse.bacc as bacc
    from concourse.bass_utils import run_bass_kernel_spmd

    nc = bacc.Bacc("TRN2", target_bir_lowering=False, num_devices=1)
    arrays, aps = {}, {}
    for name, a in laid_out(inputs).items():
        a = np.ascontiguousarray(a)
        arrays["in_" + name] = a
        aps[name] = nc.dram_tensor("in_" + name, a.shape, mybir.dt.from_np(a.dtype), kind="ExternalInput").ap()
    out = nc.dram_tensor("out_x", (TILES * P, D), F32, kind="ExternalOutput").ap()
    program(nc, aps, out)
    r = run_bass_kernel_spmd(nc, [arrays], core_ids=[0])
    return r.results[0]["out_x"].reshape(NSEQ, SEQ, D)
```
